# Optimizing a Trainium2 kernel written in Bass

```python
import numpy as np
import jax
import jax.numpy as jnp

def _softmax(x, axis=-1):
    return jax.nn.softmax(x, axis=axis)

def _gelu(x):
    return jax.nn.gelu(x, approximate=True)

def _silu(x):
    return jax.nn.silu(x)

def _sigmoid(x):
    return jax.nn.sigmoid(x)

def _layernorm(x, axis=-1, eps=1e-05):
    m = jnp.mean(x, axis=axis, keepdims=True)
    v = jnp.var(x, axis=axis, keepdims=True)
    return (x - m) / jnp.sqrt(v + eps)

def _scatter_add(tgt, idx, src, axis=0):
    return tgt.at[idx].add(src)

def _segment_sum(src, seg, n):
    return jax.ops.segment_sum(src, seg, n)
kernel_name = 'mk_pixart_resid_d2_seqx_r8_be5fb5'

def setup_inputs(seed: int=0):
    np.random.seed(seed)
    _w = jnp.asarray

    def _rec_inputs():
        import jax
        import jax.numpy as jnp
        _rk = jax.random.key(seed)
        x = -0.0005146 + 1 * jax.random.normal(jax.random.fold_in(_rk, 1), (4, 256, 128), jnp.float32)
        _lenS = 256 - jax.random.randint(jax.random.fold_in(_rk, 7), (4,), 0, max(1, 256 // 4) + 1, jnp.int32)
        _lenS2 = 1601 - jax.random.randint(jax.random.fold_in(_rk, 8), (4,), 0, max(1, 1601 // 4) + 1, jnp.int32)
        _ctx_1024P = jax.random.normal(jax.random.fold_in(_rk, 11), (4, 16, 128), jnp.float32)
        _ctx_1024c = jax.random.dirichlet(jax.random.fold_in(_rk, 511), 0.3 * jnp.ones((16,), jnp.float32), (4, 1601))
        _ctx_1024t = jnp.einsum('bsk,bkd->bsd', _ctx_1024c, _ctx_1024P)
        _ctx_1024t = _ctx_1024t * jax.lax.rsqrt(jnp.mean(jnp.square(_ctx_1024t)) + 1e-12) * 0.953939
        ctx_1024 = -0.000125008 + 0.999885 * (_ctx_1024t + 0.3 * jax.random.normal(jax.random.fold_in(_rk, 611), (4, 1601, 128), jnp.float32))
        cond_1024 = -0.00920427 + 1.00102 * jax.random.normal(jax.random.fold_in(_rk, 12), (4, 128), jnp.float32)
        _validS = jnp.arange(256)[None, :] < _lenS[:, None]
        _validS2 = jnp.arange(1601)[None, :] < _lenS2[:, None]
        _causal = jnp.tril(jnp.ones((256, 256), dtype=bool))
        mask_BxS_bf0 = jnp.logical_not(jnp.ones((4, 256), dtype=bool))
        mask_BxS2_bf0 = jnp.logical_not(jnp.ones((4, 1601), dtype=bool))
        return (x, ctx_1024, cond_1024, mask_BxS_bf0, mask_BxS2_bf0)
    x, ctx_1024, cond_1024, mask_BxS_bf0, mask_BxS2_bf0 = _rec_inputs()

    def _L0_xcond_setup():
        import jax, jax.numpy as jnp
        import numpy as np
        DIM = 128
        DIM_HEAD = 64
        HEADS = 16
        INNER = DIM_HEAD * HEADS
        B, N1, N2 = (8, 512, 32)
        EPS = 1e-05

        def layer_norm(x, w, b):
            mu = jnp.mean(x, axis=-1, keepdims=True)
            var = jnp.var(x, axis=-1, keepdims=True)
            return (x - mu) * jax.lax.rsqrt(var + EPS) * w + b
        key = jax.random.key(seed)
        ks = jax.random.split(key, 10)
        return {'x': jax.random.normal(ks[0], (B, N1, DIM), jnp.float32), 'latents': jax.random.normal(ks[1], (B, N2, DIM), jnp.float32), 'shift': jax.random.normal(ks[2], (B, DIM), jnp.float32), 'scale': jax.random.normal(ks[3], (B, DIM), jnp.float32), 'ln1_w': jnp.ones((DIM,), jnp.float32), 'ln1_b': jnp.zeros((DIM,), jnp.float32), 'ln2_w': jnp.ones((DIM,), jnp.float32), 'ln2_b': jnp.zeros((DIM,), jnp.float32), 'Wq': jax.random.normal(ks[4], (INNER, DIM), jnp.float32) * 0.02, 'Wkv': jax.random.normal(ks[5], (2 * INNER, DIM), jnp.float32) * 0.02, 'Wo': jax.random.normal(ks[6], (DIM, INNER), jnp.float32) * 0.02}
    _L0_xcond_all = _L0_xcond_setup()
    _L0_xcond_in = {k: v for k, v in _L0_xcond_all.items() if k in ('ln1_w', 'ln1_b', 'ln2_w', 'ln2_b', 'Wq', 'Wkv', 'Wo')}
    del _L0_xcond_all

    def _L0_ffn_setup():
        import jax, jax.numpy as jnp
        import numpy as np
        from jax import lax
        N_HEADS = 16
        TOP_K = 2
        N_EXPERTS = 8

        def layer_norm(x, w, b, eps=1e-05):
            mu = jnp.mean(x, axis=-1, keepdims=True)
            var = jnp.mean(jnp.square(x - mu), axis=-1, keepdims=True)
            return (x - mu) * lax.rsqrt(var + eps) * w + b

        def attention(x, w_qkv, b_qkv, w_o, b_o):
            B, T, D = x.shape
            dh = D // N_HEADS
            qkv = x @ w_qkv + b_qkv
            q, k, v = jnp.split(qkv, 3, axis=-1)
            q = q.reshape(B, T, N_HEADS, dh)
            k = k.reshape(B, T, N_HEADS, dh)
            v = v.reshape(B, T, N_HEADS, dh)
            scores = jnp.einsum('bqhd,bkhd->bhqk', q, k) / jnp.sqrt(jnp.float32(dh)).astype(x.dtype)
            probs = jax.nn.softmax(scores, axis=-1)
            ctx = jnp.einsum('bhqk,bkhd->bqhd', probs, v).reshape(B, T, D)
            return ctx @ w_o + b_o

        def moe_ff(x, w_gate, w1, b1, w2, b2):
            B, T, D = x.shape
            t = x.reshape(B * T, D)
            probs = jax.nn.softmax(t @ w_gate, axis=-1)
            tw, ti = lax.top_k(probs, TOP_K)
            tw = tw / jnp.sum(tw, axis=-1, keepdims=True)
            out = jnp.zeros_like(t)
            for e in range(N_EXPERTS):
                we = jnp.sum(jnp.where(ti == e, tw, 0.0), axis=-1)
                h = jax.nn.gelu(t @ w1[e] + b1[e]) @ w2[e] + b2[e]
                out = out + we[:, None] * h
            return out.reshape(B, T, D)
        key = jax.random.key(seed)
        ks = jax.random.split(key, 8)
        B, T, D, H, E = (4, 64, 128, 512, 8)
        s = lambda d: 1.0 / np.sqrt(d)
        return {'x': jax.random.normal(ks[0], (B, T, D), jnp.float32), 'ln1_w': jnp.ones((D,), jnp.float32), 'ln1_b': jnp.zeros((D,), jnp.float32), 'ln2_w': jnp.ones((D,), jnp.float32), 'ln2_b': jnp.zeros((D,), jnp.float32), 'w_qkv': jax.random.normal(ks[1], (D, 3 * D), jnp.float32) * s(D), 'b_qkv': jnp.zeros((3 * D,), jnp.float32), 'w_o': jax.random.normal(ks[2], (D, D), jnp.float32) * s(D), 'b_o': jnp.zeros((D,), jnp.float32), 'w_gate': jax.random.normal(ks[3], (D, E), jnp.float32) * s(D), 'w1': jax.random.normal(ks[4], (E, D, H), jnp.float32) * s(D), 'b1': jnp.zeros((E, H), jnp.float32), 'w2': jax.random.normal(ks[5], (E, H, D), jnp.float32) * s(H), 'b2': jnp.zeros((E, D), jnp.float32)}
    _L0_ffn_all = _L0_ffn_setup()
    _L0_ffn_in = {k: v for k, v in _L0_ffn_all.items() if k in ('ln1_w', 'ln1_b', 'ln2_w', 'ln2_b', 'w_qkv', 'b_qkv', 'w_o', 'b_o', 'w_gate', 'w1', 'b1', 'w2', 'b2')}
    del _L0_ffn_all

    def _L1_xcond_setup():
        import jax, jax.numpy as jnp
        import numpy as np
        NL, D, H, DFF = (6, 128, 16, 512)
        HD = D // H

        def _rope(x):
            L = x.shape[1]
            half = HD // 2
            inv = 1.0 / 10000.0 ** (jnp.arange(half, dtype=jnp.float32) / half)
            ang = jnp.arange(L, dtype=jnp.float32)[:, None] * inv
            cos = jnp.cos(ang)[None, :, None, :]
            sin = jnp.sin(ang)[None, :, None, :]
            x1, x2 = (x[..., :half], x[..., half:])
            return jnp.concatenate([x1 * cos - x2 * sin, x1 * sin + x2 * cos], axis=-1)

        def _ln(x, eps=1e-05):
            m = jnp.mean(x, axis=-1, keepdims=True)
            v = jnp.var(x, axis=-1, keepdims=True)
            return (x - m) * jax.lax.rsqrt(v + eps)

        def _adaln(x, emb, w, b):
            gb = emb[:, 0, :] @ w.T + b
            g, be = jnp.split(gb, 2, axis=-1)
            return _ln(x) * (1.0 + g[:, None, :]) + be[:, None, :]

        def _attn(q, k, v, mask):
            scores = jnp.einsum('bqhd,bkhd->bhqk', q, k) / np.float32(np.sqrt(HD))
            scores = jnp.where(mask[:, None, None, :], jnp.float32(-jnp.inf), scores)
            w = jax.nn.softmax(scores, axis=-1)
            return jnp.einsum('bhqk,bkhd->bqhd', w, v)
        key = jax.random.key(seed)
        ks = jax.random.split(key, 20)
        B, L, LC = (4, 128, 64)
        s = 0.02
        inp = {'x': jax.random.normal(ks[0], (B, L, D), jnp.float32), 'noise_emb': jax.random.normal(ks[1], (B, 1, D), jnp.float32), 'context': jax.random.normal(ks[2], (B, LC, D), jnp.float32), 'src_mask': jnp.zeros((B, L), bool), 'ctx_mask': jnp.zeros((B, LC), bool), 'n1_w': jax.random.normal(ks[3], (NL, 2 * D, D), jnp.float32) * s, 'n1_b': jnp.zeros((NL, 2 * D), jnp.float32), 'n2_w': jax.random.normal(ks[4], (NL, 2 * D, D), jnp.float32) * s, 'n2_b': jnp.zeros((NL, 2 * D), jnp.float32), 'n3_w': jax.random.normal(ks[5], (NL, 2 * D, D), jnp.float32) * s, 'n3_b': jnp.zeros((NL, 2 * D), jnp.float32), 'qkv_w': jax.random.normal(ks[6], (NL, 3 * D, D), jnp.float32) * s, 'so_w': jax.random.normal(ks[7], (NL, D, D), jnp.float32) * s, 'cq_w': jax.random.normal(ks[8], (NL, D, D), jnp.float32) * s, 'ck_w': jax.random.normal(ks[9], (NL, D, D), jnp.float32) * s, 'cv_w': jax.random.normal(ks[10], (NL, D, D), jnp.float32) * s, 'co_w': jax.random.normal(ks[11], (NL, D, D), jnp.float32) * s, 'f1_w': jax.random.normal(ks[12], (NL, DFF, D), jnp.float32) * s, 'f1_b': jnp.zeros((NL, DFF), jnp.float32), 'f2_w': jax.random.normal(ks[13], (NL, D, DFF), jnp.float32) * s, 'f2_b': jnp.zeros((NL, D), jnp.float32)}
        return inp
    _L1_xcond_all = _L1_xcond_setup()
    _L1_xcond_in = {k: v for k, v in _L1_xcond_all.items() if k in ('n1_w', 'n1_b', 'n2_w', 'n2_b', 'n3_w', 'n3_b', 'qkv_w', 'so_w', 'cq_w', 'ck_w', 'cv_w', 'co_w', 'f1_w', 'f1_b', 'f2_w', 'f2_b')}
    del _L1_xcond_all

    def _L1_ffn_setup():
        import jax, jax.numpy as jnp
        import numpy as np
        B, S, D, H, E = (4, 256, 128, 512, 8)
        key = jax.random.key(seed)
        ks = jax.random.split(key, 8)
        s_d = 1.0 / np.sqrt(D)
        s_h = 1.0 / np.sqrt(H)
        return {'x': jax.random.normal(ks[0], (B, S, D), dtype=jnp.float32), 'gate_w': jax.random.uniform(ks[1], (E, D), jnp.float32, -s_d, s_d), 'gate_b': jax.random.uniform(ks[2], (E,), jnp.float32, -s_d, s_d), 'w1': jax.random.uniform(ks[3], (E, H, D), jnp.float32, -s_d, s_d), 'b1': jax.random.uniform(ks[4], (E, H), jnp.float32, -s_d, s_d), 'w2': jax.random.uniform(ks[5], (E, D, H), jnp.float32, -s_h, s_h), 'b2': jax.random.uniform(ks[6], (E, D), jnp.float32, -s_h, s_h)}
    _L1_ffn_all = _L1_ffn_setup()
    _L1_ffn_in = {k: v for k, v in _L1_ffn_all.items() if k in ('gate_w', 'gate_b', 'w1', 'b1', 'w2', 'b2')}
    del _L1_ffn_all
    return {'x': x, 'ctx_1024': ctx_1024, 'cond_1024': cond_1024, 'mask_BxS_bf0': mask_BxS_bf0, 'mask_BxS2_bf0': mask_BxS2_bf0, 'L0_xcond_ln1_w': _L0_xcond_in['ln1_w'], 'L0_xcond_ln1_b': _L0_xcond_in['ln1_b'], 'L0_xcond_ln2_w': _L0_xcond_in['ln2_w'], 'L0_xcond_ln2_b': _L0_xcond_in['ln2_b'], 'L0_xcond_Wq': _L0_xcond_in['Wq'], 'L0_xcond_Wkv': _L0_xcond_in['Wkv'], 'L0_xcond_Wo': _L0_xcond_in['Wo'], 'L0_ffn_ln1_w': _L0_ffn_in['ln1_w'], 'L0_ffn_ln1_b': _L0_ffn_in['ln1_b'], 'L0_ffn_ln2_w': _L0_ffn_in['ln2_w'], 'L0_ffn_ln2_b': _L0_ffn_in['ln2_b'], 'L0_ffn_w_qkv': _L0_ffn_in['w_qkv'], 'L0_ffn_b_qkv': _L0_ffn_in['b_qkv'], 'L0_ffn_w_o': _L0_ffn_in['w_o'], 'L0_ffn_b_o': _L0_ffn_in['b_o'], 'L0_ffn_w_gate': _L0_ffn_in['w_gate'], 'L0_ffn_w1': _L0_ffn_in['w1'], 'L0_ffn_b1': _L0_ffn_in['b1'], 'L0_ffn_w2': _L0_ffn_in['w2'], 'L0_ffn_b2': _L0_ffn_in['b2'], 'L1_xcond_n1_w': _L1_xcond_in['n1_w'], 'L1_xcond_n1_b': _L1_xcond_in['n1_b'], 'L1_xcond_n2_w': _L1_xcond_in['n2_w'], 'L1_xcond_n2_b': _L1_xcond_in['n2_b'], 'L1_xcond_n3_w': _L1_xcond_in['n3_w'], 'L1_xcond_n3_b': _L1_xcond_in['n3_b'], 'L1_xcond_qkv_w': _L1_xcond_in['qkv_w'], 'L1_xcond_so_w': _L1_xcond_in['so_w'], 'L1_xcond_cq_w': _L1_xcond_in['cq_w'], 'L1_xcond_ck_w': _L1_xcond_in['ck_w'], 'L1_xcond_cv_w': _L1_xcond_in['cv_w'], 'L1_xcond_co_w': _L1_xcond_in['co_w'], 'L1_xcond_f1_w': _L1_xcond_in['f1_w'], 'L1_xcond_f1_b': _L1_xcond_in['f1_b'], 'L1_xcond_f2_w': _L1_xcond_in['f2_w'], 'L1_xcond_f2_b': _L1_xcond_in['f2_b'], 'L1_ffn_gate_w': _L1_ffn_in['gate_w'], 'L1_ffn_gate_b': _L1_ffn_in['gate_b'], 'L1_ffn_w1': _L1_ffn_in['w1'], 'L1_ffn_b1': _L1_ffn_in['b1'], 'L1_ffn_w2': _L1_ffn_in['w2'], 'L1_ffn_b2': _L1_ffn_in['b2']}

def reference(x, ctx_1024, cond_1024, mask_BxS_bf0, mask_BxS2_bf0, L0_xcond_ln1_w, L0_xcond_ln1_b, L0_xcond_ln2_w, L0_xcond_ln2_b, L0_xcond_Wq, L0_xcond_Wkv, L0_xcond_Wo, L0_ffn_ln1_w, L0_ffn_ln1_b, L0_ffn_ln2_w, L0_ffn_ln2_b, L0_ffn_w_qkv, L0_ffn_b_qkv, L0_ffn_w_o, L0_ffn_b_o, L0_ffn_w_gate, L0_ffn_w1, L0_ffn_b1, L0_ffn_w2, L0_ffn_b2, L1_xcond_n1_w, L1_xcond_n1_b, L1_xcond_n2_w, L1_xcond_n2_b, L1_xcond_n3_w, L1_xcond_n3_b, L1_xcond_qkv_w, L1_xcond_so_w, L1_xcond_cq_w, L1_xcond_ck_w, L1_xcond_cv_w, L1_xcond_co_w, L1_xcond_f1_w, L1_xcond_f1_b, L1_xcond_f2_w, L1_xcond_f2_b, L1_ffn_gate_w, L1_ffn_gate_b, L1_ffn_w1, L1_ffn_b1, L1_ffn_w2, L1_ffn_b2):
    import jax
    import jax.numpy as jnp

    def _L0_xcond_ref(x, latents, shift, scale, ln1_w, ln1_b, ln2_w, ln2_b, Wq, Wkv, Wo):
        import jax, jax.numpy as jnp
        import numpy as np
        DIM = 128
        DIM_HEAD = 64
        HEADS = 16
        INNER = DIM_HEAD * HEADS
        B, N1, N2 = (8, 512, 32)
        EPS = 1e-05

        def layer_norm(x, w, b):
            mu = jnp.mean(x, axis=-1, keepdims=True)
            var = jnp.var(x, axis=-1, keepdims=True)
            return (x - mu) * jax.lax.rsqrt(var + EPS) * w + b
        x = layer_norm(x, ln1_w, ln1_b)
        lat = layer_norm(latents, ln2_w, ln2_b)
        lat = lat * (1.0 + scale[:, None, :]) + shift[:, None, :]
        b, n2, _ = lat.shape
        q = jnp.einsum('bld,ed->ble', lat, Wq)
        kv_in = jnp.concatenate((x, lat), axis=-2)
        kv = jnp.einsum('bld,ed->ble', kv_in, Wkv)
        k, v = jnp.split(kv, 2, axis=-1)

        def to_heads(t):
            bsz, L, _ = t.shape
            return t.reshape(bsz, L, HEADS, DIM_HEAD).transpose(0, 2, 1, 3)
        q, k, v = (to_heads(q), to_heads(k), to_heads(v))
        attn_scale = 1.0 / np.sqrt(np.sqrt(DIM_HEAD)).astype(np.float32)
        logits = jnp.einsum('bhqd,bhkd->bhqk', q * attn_scale, k * attn_scale)
        w = jax.nn.softmax(logits.astype(jnp.float32), axis=-1).astype(logits.dtype)
        out = jnp.einsum('bhqk,bhkd->bhqd', w, v)
        out = out.transpose(0, 2, 1, 3).reshape(b, n2, INNER)
        return jnp.einsum('ble,de->bld', out, Wo)

    def _L0_ffn_ref(x, ln1_w, ln1_b, ln2_w, ln2_b, w_qkv, b_qkv, w_o, b_o, w_gate, w1, b1, w2, b2):
        import jax, jax.numpy as jnp
        import numpy as np
        from jax import lax
        N_HEADS = 16
        TOP_K = 2
        N_EXPERTS = 8

        def layer_norm(x, w, b, eps=1e-05):
            mu = jnp.mean(x, axis=-1, keepdims=True)
            var = jnp.mean(jnp.square(x - mu), axis=-1, keepdims=True)
            return (x - mu) * lax.rsqrt(var + eps) * w + b

        def attention(x, w_qkv, b_qkv, w_o, b_o):
            B, T, D = x.shape
            dh = D // N_HEADS
            qkv = x @ w_qkv + b_qkv
            q, k, v = jnp.split(qkv, 3, axis=-1)
            q = q.reshape(B, T, N_HEADS, dh)
            k = k.reshape(B, T, N_HEADS, dh)
            v = v.reshape(B, T, N_HEADS, dh)
            scores = jnp.einsum('bqhd,bkhd->bhqk', q, k) / jnp.sqrt(jnp.float32(dh)).astype(x.dtype)
            probs = jax.nn.softmax(scores, axis=-1)
            ctx = jnp.einsum('bhqk,bkhd->bqhd', probs, v).reshape(B, T, D)
            return ctx @ w_o + b_o

        def moe_ff(x, w_gate, w1, b1, w2, b2):
            B, T, D = x.shape
            t = x.reshape(B * T, D)
            probs = jax.nn.softmax(t @ w_gate, axis=-1)
            tw, ti = lax.top_k(probs, TOP_K)
            tw = tw / jnp.sum(tw, axis=-1, keepdims=True)
            out = jnp.zeros_like(t)
            for e in range(N_EXPERTS):
                we = jnp.sum(jnp.where(ti == e, tw, 0.0), axis=-1)
                h = jax.nn.gelu(t @ w1[e] + b1[e]) @ w2[e] + b2[e]
                out = out + we[:, None] * h
            return out.reshape(B, T, D)
        h = x + attention(layer_norm(x, ln1_w, ln1_b), w_qkv, b_qkv, w_o, b_o)
        return h + moe_ff(layer_norm(h, ln2_w, ln2_b), w_gate, w1, b1, w2, b2)

    def _L1_xcond_ref(x, noise_emb, context, src_mask, ctx_mask, n1_w, n1_b, n2_w, n2_b, n3_w, n3_b, qkv_w, so_w, cq_w, ck_w, cv_w, co_w, f1_w, f1_b, f2_w, f2_b):
        import jax, jax.numpy as jnp
        import numpy as np
        NL, D, H, DFF = (6, 128, 16, 512)
        HD = D // H

        def _rope(x):
            L = x.shape[1]
            half = HD // 2
            inv = 1.0 / 10000.0 ** (jnp.arange(half, dtype=jnp.float32) / half)
            ang = jnp.arange(L, dtype=jnp.float32)[:, None] * inv
            cos = jnp.cos(ang)[None, :, None, :]
            sin = jnp.sin(ang)[None, :, None, :]
            x1, x2 = (x[..., :half], x[..., half:])
            return jnp.concatenate([x1 * cos - x2 * sin, x1 * sin + x2 * cos], axis=-1)

        def _ln(x, eps=1e-05):
            m = jnp.mean(x, axis=-1, keepdims=True)
            v = jnp.var(x, axis=-1, keepdims=True)
            return (x - m) * jax.lax.rsqrt(v + eps)

        def _adaln(x, emb, w, b):
            gb = emb[:, 0, :] @ w.T + b
            g, be = jnp.split(gb, 2, axis=-1)
            return _ln(x) * (1.0 + g[:, None, :]) + be[:, None, :]

        def _attn(q, k, v, mask):
            scores = jnp.einsum('bqhd,bkhd->bhqk', q, k) / np.float32(np.sqrt(HD))
            scores = jnp.where(mask[:, None, None, :], jnp.float32(-jnp.inf), scores)
            w = jax.nn.softmax(scores, axis=-1)
            return jnp.einsum('bhqk,bkhd->bqhd', w, v)
        B, L, _ = x.shape
        LC = context.shape[1]
        for i in range(NL):
            xn = _adaln(x, noise_emb, n1_w[i], n1_b[i])
            qkv = xn @ qkv_w[i].T
            q, k, v = jnp.split(qkv, 3, axis=-1)
            q = _rope(q.reshape(B, L, H, HD))
            k = _rope(k.reshape(B, L, H, HD))
            v = v.reshape(B, L, H, HD)
            a = _attn(q, k, v, src_mask).reshape(B, L, D) @ so_w[i].T
            x = x + a
            xn = _adaln(x, noise_emb, n2_w[i], n2_b[i])
            q = _rope((xn @ cq_w[i].T).reshape(B, L, H, HD))
            k = _rope((context @ ck_w[i].T).reshape(B, LC, H, HD))
            v = (context @ cv_w[i].T).reshape(B, LC, H, HD)
            a = _attn(q, k, v, ctx_mask).reshape(B, L, D) @ co_w[i].T
            x = x + a
            xn = _adaln(x, noise_emb, n3_w[i], n3_b[i])
            h = jax.nn.gelu(xn @ f1_w[i].T + f1_b[i], approximate=False)
            x = x + (h @ f2_w[i].T + f2_b[i])
        return x

    def _L1_ffn_ref(x, gate_w, gate_b, w1, b1, w2, b2):
        import jax, jax.numpy as jnp
        import numpy as np
        B, S, D, H, E = (4, 256, 128, 512, 8)
        b, s, d = x.shape
        xf = x.reshape(-1, d)
        logits = xf @ gate_w.T + gate_b
        top1 = jnp.argmax(logits, axis=-1)
        out = jnp.zeros_like(xf)
        n_experts = w1.shape[0]
        for e in range(n_experts):
            h = jax.nn.relu(xf @ w1[e].T + b1[e])
            y = h @ w2[e].T + b2[e]
            out = out + jnp.where((top1 == e)[:, None], y, jnp.zeros((), y.dtype))
        return out.reshape(b, s, d)
    x = x + _L0_xcond_ref(ctx_1024, _layernorm(x, axis=-1), cond_1024, cond_1024, L0_xcond_ln1_w, L0_xcond_ln1_b, L0_xcond_ln2_w, L0_xcond_ln2_b, L0_xcond_Wq, L0_xcond_Wkv, L0_xcond_Wo)
    x = x + _L0_ffn_ref(_layernorm(x, axis=-1), L0_ffn_ln1_w, L0_ffn_ln1_b, L0_ffn_ln2_w, L0_ffn_ln2_b, L0_ffn_w_qkv, L0_ffn_b_qkv, L0_ffn_w_o, L0_ffn_b_o, L0_ffn_w_gate, L0_ffn_w1, L0_ffn_b1, L0_ffn_w2, L0_ffn_b2)
    x = x + _L1_xcond_ref(_layernorm(x, axis=-1), cond_1024[:, None, :], ctx_1024, mask_BxS_bf0, mask_BxS2_bf0, L1_xcond_n1_w, L1_xcond_n1_b, L1_xcond_n2_w, L1_xcond_n2_b, L1_xcond_n3_w, L1_xcond_n3_b, L1_xcond_qkv_w, L1_xcond_so_w, L1_xcond_cq_w, L1_xcond_ck_w, L1_xcond_cv_w, L1_xcond_co_w, L1_xcond_f1_w, L1_xcond_f1_b, L1_xcond_f2_w, L1_xcond_f2_b)
    x = x + _L1_ffn_ref(_layernorm(x, axis=-1), L1_ffn_gate_w, L1_ffn_gate_b, L1_ffn_w1, L1_ffn_b1, L1_ffn_w2, L1_ffn_b2)
    return x

_drawn_inputs = setup_inputs


def setup_inputs(seed=0):
    import zlib

    import numpy as np

    out = dict(_drawn_inputs(seed))
    spreads = {'L0_xcond_ln1_w': (1.0, 0.6),
     'L0_xcond_ln1_b': (0.0, 0.294),
     'L0_xcond_ln2_w': (1.0, 0.6),
     'L0_xcond_ln2_b': (0.0, 0.448),
     'L0_ffn_ln1_w': (1.0, 0.2),
     'L0_ffn_ln1_b': (0.0, 0.1),
     'L0_ffn_ln2_w': (1.0, 0.2),
     'L0_ffn_ln2_b': (0.0, 0.1),
     'L0_ffn_b_qkv': (0.0, 0.1),
     'L0_ffn_b_o': (0.0, 0.1),
     'L0_ffn_b1': (0.0, 0.29),
     'L0_ffn_b2': (0.0, 0.1),
     'L1_xcond_n1_b': (0.0, 0.8),
     'L1_xcond_n2_b': (0.0, 2.0),
     'L1_xcond_n3_b': (0.0, 0.8),
     'L1_xcond_f1_b': (0.0, 0.316),
     'L1_xcond_f2_b': (0.0, 0.1)}
    factors = {'L0_xcond_Wq': 3.998,
     'L1_xcond_n1_w': 4.435,
     'L1_xcond_n2_w': 8.0,
     'L1_xcond_n3_w': 3.389,
     'L1_xcond_qkv_w': 3.714,
     'L1_xcond_so_w': 3.509,
     'L1_xcond_cq_w': 8.0,
     'L1_xcond_ck_w': 8.0,
     'L1_ffn_b1': 8.0,
     'L1_ffn_b2': 6.715}
    for name, (base, spread) in spreads.items():
        noise = np.random.default_rng([zlib.crc32(name.encode()), seed]).standard_normal(out[name].shape)
        drawn = base * np.exp(spread * noise) if base else spread * noise
        out[name] = jnp.asarray(drawn.astype(out[name].dtype))
    for name, factor in factors.items():
        out[name] = (out[name] * factor).astype(out[name].dtype)
    return out
```

```python
from contextlib import ExitStack

import numpy as np

import concourse.bass as bass
from concourse import mybir

F32 = mybir.dt.float32
BF16 = mybir.dt.bfloat16
U8 = mybir.dt.uint8
U32 = mybir.dt.uint32
ALU = mybir.AluOpType
ACT = mybir.ActivationFunctionType
AX = mybir.AxisListType

P = 128
B, S, D = 4, 256, 128
NTOK = B * S
TILES = NTOK // P
QT = S // P
SC = 1601
H, HD = 16, 8
PAIRS = H // 2
UNITS = B * PAIRS
NL, DFF, E = 6, 512, 8
FC = DFF // P
EA = 64
EPS = 1e-5
MASKED = -1.0e30

PARTS_Q = (0, 0, 1, 0, 2, 1)
PARTS_K = (0, 1, 0, 2, 0, 1)
SLOTS = len(PARTS_Q)
ROWS = HD * SLOTS
R0 = 2
VW = 32
RING = 4

_NAMES = [("n1", 256), ("n2", 256), ("n3", 256), ("q", 128), ("qs", 128), ("k", 128), ("ks", 128), ("v", 128),
          ("so", 128), ("cq", 128), ("cqs", 128), ("ck", 128), ("cks", 128), ("cv", 128), ("co", 128),
          ("f1", DFF), ("f2", DFF), ("n1b", 2), ("n2b", 2), ("n3b", 2), ("f1b", FC)]
COL, _at = {}, 0
for _n, _w in _NAMES:
    COL[_n] = (_at, _w)
    _at += _w
WCOLS = _at


def key_tiles(n):
    return [(k, min(P, n - k)) for k in range(0, n, P)]


class Unit:

    def __init__(self, step, i, r):
        self.step, self.i, self.r = step, i, r

    def at(self, k=0):
        return self.step * self.i + (self.r + k)

    def turn(self, k=0):
        return self.i + (self.r + k) // self.step + 1

    def buf(self, n, k=0):
        return (self.r + k) % n


def wait(eng, sem, value):
    if isinstance(value, int) and value <= 0:
        return
    eng.wait_ge(sem, value)


def build_program(nc, T, out, stop=None, dump=None):
    top = ExitStack()
    sems = []

    def sem(name):
        s = top.enter_context(nc.semaphore(name))
        sems.append(s)
        return s

    def clear():
        if sems:
            nc.all_engine_barrier(sems_to_clear=range(sems[0].num, sems[-1].num + 1))

    def sb(st, name, shape, dt=F32):
        return st.enter_context(nc.sbuf_tensor(name, shape, dt))

    psum = top.enter_context(nc.psum_tensor("psum", [P, 8, 512], F32))

    k_ctx_d = nc.dram_tensor("k_ctx_parts", [B, P, SLOTS, SC], BF16, kind="Internal").ap()
    k_self_d = nc.dram_tensor("k_self_parts", [B, P, SLOTS, S], BF16, kind="Internal").ap()
    q_d = nc.dram_tensor("q_parts", [B, P, SLOTS, S], BF16, kind="Internal").ap()
    m_ctx_d = nc.dram_tensor("m_ctx", [B * H, SC], BF16, kind="Internal").ap()
    m_self_d = nc.dram_tensor("m_self", [B * H, S], BF16, kind="Internal").ap()
    m_none_d = nc.dram_tensor("m_none", [B * H, S], BF16, kind="Internal").ap()

    x_sb = sb(top, "x_sb", [P, TILES, D])
    z_sb = sb(top, "z_sb", [P, TILES, D])
    xhat = sb(top, "xhat", [P, TILES, D])
    xnT = sb(top, "xnT", [P, NTOK])
    ident = sb(top, "ident", [P, P])
    condT = sb(top, "condT", [P, B])
    vecs = sb(top, "vecs", [P, 12])
    stats = sb(top, "stats", [P, TILES + 6, 6])
    mv = sb(top, "mv", [P, TILES + 6, 2])
    rstd = sb(top, "rstd", [P, TILES + 6])
    nhalf = sb(top, "nhalf", [P, TILES + 6])
    scl = sb(top, "scl", [P, B])
    bia = sb(top, "bia", [P, B])
    ones_row = sb(top, "ones_row", [1, P])
    brow = sb(top, "brow", [1, 2 * D])

    loaded = sem("loaded")
    loaded2 = sem("loaded2")
    stat_done = sem("stat_done")
    aggr_done = sem("aggr_done")
    eps_added = sem("eps_added")
    rstd_done = sem("rstd_done")
    norm_done = sem("norm_done")
    transposed = sem("transposed")
    affine_done = sem("affine_done")
    mod_made = sem("mod_made")
    mod_ready = sem("mod_ready")
    chain = sem("chain")
    ring_loaded = [sem(f"ring_loaded{i}") for i in range(RING)]
    row_cleared = sem("row_cleared")
    v_staged = sem("v_staged")
    max_scores = sem("max_scores")
    max_read = sem("max_read")
    max_done = sem("max_done")
    max_row = sem("max_row")
    shift_ready = sem("shift_ready")
    scored = sem("scored")
    exp_done = sem("exp_done")
    pv_done = sem("pv_done")
    o_copied = sem("o_copied")
    o_turned = sem("o_turned")
    o_scaled = sem("o_scaled")
    rec_done = sem("rec_done")
    proj_made = sem("proj_made")
    proj_read = sem("proj_read")
    mixed = sem("mixed")
    summed = sem("summed")
    hi_done = sem("hi_done")
    rest_done = sem("rest_done")
    mid_done = sem("mid_done")
    lo_done = sem("lo_done")
    parts_out = [sem("parts_out0"), sem("parts_out1")]
    v_made = sem("v_made")
    v_read = sem("v_read")
    turned = sem("turned")
    turned_out = sem("turned_out")
    up_made = sem("up_made")
    act_done = sem("act_done")
    down_made = sem("down_made")
    down_read = sem("down_read")
    weights_in = [sem("weights_in0"), sem("weights_in1")]
    gate_made = sem("gate_made")
    gate_step = sem("gate_step")
    gate_exp = sem("gate_exp")
    stored = sem("stored")
    swept = sem("swept")
    sum_bc = sem("sum_bc")
    zeroed = sem("zeroed")

    with ExitStack() as st:
        mk = sb(st, "mk", [B * H, SC], U8)
        mb = sb(st, "mb", [B * H, SC], BF16)
        ms = sb(st, "ms", [B * H, S], U8)
        mbs = sb(st, "mbs", [B * H, 2, S], BF16)
        with nc.Block() as block:
            @block.sync
            def _(sp):
                sp.dma_start(mk[:, :], T["mask_ctx"]).then_inc(loaded, 16)
                sp.dma_start(ms[:, :], T["mask_x"]).then_inc(loaded, 16)
                sp.dma_start(x_sb[:, :, :], T["x"].rearrange("b (t p) d -> p (b t) d", p=P)).then_inc(loaded2, 16)
                sp.dma_start(ident[:, :], T["ident"]).then_inc(loaded2, 16)
                sp.dma_start(condT[:, :], T["condT"]).then_inc(loaded2, 16)
                sp.dma_start(vecs[:, :], T["vecs"]).then_inc(loaded2, 16)
                sp.wait_ge(chain, 3)
                sp.dma_start(m_ctx_d, mb[:, :]).then_inc(stored, 16)
                sp.dma_start(m_self_d, mbs[:, 0, :]).then_inc(stored, 16)
                sp.dma_start(m_none_d, mbs[:, 1, :]).then_inc(stored, 16)
                sp.wait_ge(stored, 48)
                sp.wait_ge(loaded2, 64)

            @block.vector
            def _(dve):
                dve.memset(nhalf[:, :], -0.5)
                dve.memset(ones_row[:, :], 1.0)
                dve.wait_ge(loaded, 32)
                dve.tensor_scalar(mb[:, :], mk[:, :], MASKED, None, ALU.mult).then_inc(chain, 1)
                dve.tensor_scalar(mbs[:, 0, :], ms[:, :], MASKED, None, ALU.mult).then_inc(chain, 1)
                dve.memset(mbs[:, 1, :], 0.0).then_inc(chain, 1)
        clear()

    def layer_norm(src, dst, passes=1, turn=None, modulate=None, affine=None):
        with nc.Block() as block:
            @block.vector
            def _(dve):
                for n in range(passes):
                    a = src if n == 0 else dst
                    wait(dve, norm_done, TILES * n)
                    for t in range(TILES):
                        dve.bn_stats(stats[:, t, :], a[:, t, :]).then_inc(stat_done, 1)
                    dve.wait_ge(stat_done, TILES * (n + 1))
                    for t in range(TILES):
                        dve.bn_aggr(mv[:, t, :], stats[:, t, :]).then_inc(aggr_done, 1)
                    dve.wait_ge(rstd_done, n + 1)
                    for t in range(TILES):
                        dve.tensor_scalar(dst[:, t, :], a[:, t, :], mv[:, t, 0:1], rstd[:, t:t + 1],
                                          ALU.subtract, ALU.mult).then_inc(norm_done, 1)
                if turn is None:
                    return
                if modulate is not None:
                    wb = modulate[1]
                    dve.wait_ge(mod_made, 1)
                    dve.tensor_scalar(scl[:, :], psum[:, 2, 0:B], wb[:, 0:1], 1.0, ALU.add, ALU.add).then_inc(mod_ready, 1)
                    dve.tensor_scalar(bia[:, :], psum[:, 2, B:2 * B], wb[:, 1:2], None, ALU.add).then_inc(mod_ready, 1)
                    dve.wait_ge(mod_ready, 2)
                for b in range(B):
                    s = scl[:, b:b + 1] if modulate is not None else affine[0](b)
                    o = bia[:, b:b + 1] if modulate is not None else affine[1](b)
                    dve.wait_ge(transposed, QT * (b + 1))
                    dve.tensor_scalar(turn[:, b * S:(b + 1) * S], psum[:, b % 2, 0:S], s, o,
                                      ALU.mult, ALU.add).then_inc(affine_done, 1)

            @block.gpsimd
            def _(pool):
                for n in range(passes):
                    pool.wait_ge(aggr_done, TILES * (n + 1))
                    pool.tensor_scalar(rstd[:, 0:TILES], mv[:, 0:TILES, 1], EPS, None, ALU.add).then_inc(eps_added, 1)
                    pool.wait_ge(eps_added, n + 1)
                    pool.tensor_tensor(rstd[:, 0:TILES], rstd[:, 0:TILES], nhalf[:, 0:TILES], ALU.pow).then_inc(rstd_done, 1)

            @block.tensor
            def _(pe):
                if turn is None:
                    return
                if modulate is not None:
                    w = modulate[0]
                    pe.matmul(psum[:, 2, 0:B], w[:, 0:P], condT[:, :], start=True, stop=True)
                    pe.matmul(psum[:, 2, B:2 * B], w[:, P:2 * P], condT[:, :], start=True, stop=True).then_inc(mod_made, 1)
                for t in range(TILES):
                    b, h = divmod(t, QT)
                    pe.wait_ge(norm_done, TILES * (passes - 1) + t + 1)
                    wait(pe, affine_done, b - 1)
                    pe.transpose(psum[:, b % 2, h * P:(h + 1) * P], dst[:, t, :], ident[:, :]).then_inc(transposed, 1)
        clear()

    def resampler():
        KTS = key_tiles(SC) + [(SC, P), (SC + P, P)]
        NK = SC + S
        KT = len(KTS)
        CT = len(key_tiles(SC))
        st = ExitStack()
        a_sb = sb(st, "a_sb", [P, H, P])
        b_sb = sb(st, "b_sb", [P, H, D])
        qp = sb(st, "qp", [P, UNITS, 2 * S])
        qhi = sb(st, "qhi", [P, UNITS, 2 * S], BF16)
        ones_f = sb(st, "ones_f", [P, P])
        ones_b = sb(st, "ones_b", [1, P], BF16)
        lnw = sb(st, "lnw", [P, 2, D])

        layer_norm(x_sb, xhat, passes=2, turn=None)

        with ExitStack() as s2:
            wq = sb(s2, "wq", [EA, H, D])
            wk = sb(s2, "wk", [EA, H, D])
            wv = sb(s2, "wv", [EA, H, D])
            wo = sb(s2, "wo", [EA, H, D])
            with nc.Block() as block:
                @block.sync
                def _(sp):
                    sp.dma_start(wq[:, :, :], T["Wq"]).then_inc(loaded, 16)
                    sp.dma_start(wk[:, :, :], T["Wk"]).then_inc(loaded, 16)
                    sp.dma_start(wv[:, :, :], T["Wv"]).then_inc(loaded, 16)
                    sp.dma_start(wo[:, :, :], T["Wo"]).then_inc(loaded, 16)
                    sp.dma_start(lnw[:, 0, :], T["ln1_w"].partition_broadcast(P)).then_inc(loaded2, 16)
                    sp.dma_start(lnw[:, 1, :], T["ln1_b"].partition_broadcast(P)).then_inc(loaded2, 16)
                    sp.wait_ge(loaded2, 32)

                @block.vector
                def _(dve):
                    dve.memset(ones_f[:, :], 1.0)
                    dve.memset(ones_b[:, :], 1.0)
                    dve.tensor_scalar(scl[:, :], condT[:, :], 1.0, vecs[:, 0:1], ALU.add, ALU.mult).then_inc(chain, 1)
                    dve.tensor_scalar(bia[:, :], condT[:, :], 1.0, vecs[:, 1:2], ALU.add, ALU.mult).then_inc(chain, 1)
                    dve.wait_ge(chain, 2)
                    dve.tensor_tensor(bia[:, :], bia[:, :], condT[:, :], ALU.add).then_inc(chain, 1)
                    dve.wait_ge(chain, 3)
                    for b in range(B):
                        dve.wait_ge(transposed, QT * (b + 1))
                        dve.tensor_scalar(xnT[:, b * S:(b + 1) * S], psum[:, b % 2, 0:S], scl[:, b:b + 1], bia[:, b:b + 1],
                                          ALU.mult, ALU.add).then_inc(affine_done, 1)
                    for h in range(H):
                        dve.wait_ge(proj_made, h + 1)
                        dve.tensor_copy(a_sb[:, h, :], psum[:, 2 + h % 2, 0:P]).then_inc(proj_read, 1)
                        dve.tensor_copy(b_sb[:, h, :], psum[:, 2 + h % 2, P:2 * P]).then_inc(proj_read, 1)
                    for h in range(H):
                        for c in range(2):
                            n = 2 * h + c
                            dve.wait_ge(up_made, n + 1)
                            dve.tensor_copy(qp[:, :, :].rearrange("p (b u) (h q) -> p b u h q", u=PAIRS, h=2)[:, 2 * c:2 * c + 2, h // 2, h % 2, :],
                                            psum[:, 4 + n % 2, :].rearrange("p (b q) -> p b q", b=2)).then_inc(down_made, 1)

                @block.scalar
                def _(act):
                    for h in range(H):
                        for c in range(2):
                            n = 2 * h + c
                            act.wait_ge(down_made, n + 1)
                            act.activation(qhi[:, :, :].rearrange("p (b u) (h q) -> p b u h q", u=PAIRS, h=2)[:, 2 * c:2 * c + 2, h // 2, h % 2, :],
                                           qp[:, :, :].rearrange("p (b u) (h q) -> p b u h q", u=PAIRS, h=2)[:, 2 * c:2 * c + 2, h // 2, h % 2, :], ACT.Copy)

                @block.tensor
                def _(pe):
                    for t in range(TILES):
                        b, h = divmod(t, QT)
                        wait(pe, affine_done, b - 1)
                        pe.transpose(psum[:, b % 2, h * P:(h + 1) * P], xhat[:, t, :], ident[:, :]).then_inc(transposed, 1)
                    pe.wait_ge(loaded, 64)
                    for h in range(H):
                        wait(pe, proj_read, 2 * (h - 1))
                        pe.matmul(psum[:, 2 + h % 2, 0:P], wq[:, h, :], wk[:, h, :], start=True, stop=True)
                        pe.matmul(psum[:, 2 + h % 2, P:2 * P], wv[:, h, :], wo[:, h, :], start=True, stop=True).then_inc(proj_made, 1)
                    pe.wait_ge(affine_done, B)
                    pe.wait_ge(proj_read, 2 * H)
                    for h in range(H):
                        for c in range(2):
                            n = 2 * h + c
                            wait(pe, down_made, n - 1)
                            pe.matmul(psum[:, 4 + n % 2, :], a_sb[:, h, :], xnT[:, c * 512:(c + 1) * 512], start=True, stop=True).then_inc(up_made, 1)
            clear()

        craw = sb(st, "craw", [P, CT, D])
        ck = sb(st, "ck", [P, KT, D])
        cT = sb(st, "cT", [P, NK])
        cTh = sb(st, "cTh", [P, NK], BF16)
        NP = 3
        probs = sb(st, "probs", [P, NP, 512])
        psumm = sb(st, "psumm", [P, 2, 512])
        mp = sb(st, "mp", [P, 2, 4, 2])
        nm = sb(st, "nm", [P, 2, 4])
        nrow = sb(st, "nrow", [1, 2, 512], BF16)
        yraw = sb(st, "yraw", [P, 512])
        rec = sb(st, "rec", [P, 512])
        yn = sb(st, "yn", [P, 512])
        acc = sb(st, "acc", [P, QT, D])
        tail = KTS[CT - 1][1]

        with nc.Fori(0, B) as b:
            with nc.Block() as block:
                @block.sync
                def _(sp):
                    sp.dma_start(craw[:, 0:CT - 1, :], T["ctx"][b, 0:(CT - 1) * P, :].rearrange("(t p) d -> p t d", p=P)).then_inc(loaded, 16)
                    sp.dma_start(craw[0:tail, CT - 1, :], T["ctx"][b, (CT - 1) * P:SC, :]).then_inc(loaded, 16)

                @block.vector
                def _(dve):
                    dve.tensor_copy(cT[:, SC:NK], xnT[:, bass.ds(b * S, S)]).then_inc(mixed, 1)
                    dve.memset(acc[:, :, :], 0.0)
                    dve.wait_ge(loaded, 32)
                    for t in range(CT):
                        n = KTS[t][1]
                        dve.bn_stats(stats[0:n, t, :], craw[0:n, t, :]).then_inc(stat_done, 1)
                    dve.wait_ge(stat_done, CT)
                    for t in range(CT):
                        n = KTS[t][1]
                        dve.bn_aggr(mv[0:n, t, :], stats[0:n, t, :]).then_inc(aggr_done, 1)
                    dve.wait_ge(rstd_done, 2)
                    for t in range(CT):
                        n = KTS[t][1]
                        dve.tensor_scalar(craw[0:n, t, :], craw[0:n, t, :], mv[0:n, t, 0:1], rstd[0:n, t:t + 1],
                                          ALU.subtract, ALU.mult).then_inc(norm_done, 1)
                    for t in range(CT):
                        n = KTS[t][1]
                        dve.wait_ge(norm_done, t + 1)
                        dve.tensor_tensor(ck[0:n, t, :], craw[0:n, t, :], lnw[0:n, 0, :], ALU.mult).then_inc(chain, 1)
                    for t in range(CT):
                        n = KTS[t][1]
                        dve.wait_ge(chain, t + 1)
                        dve.tensor_tensor(ck[0:n, t, :], ck[0:n, t, :], lnw[0:n, 1, :], ALU.add).then_inc(affine_done, 1)
                    for t in range(CT, KT):
                        dve.wait_ge(transposed, t - CT + 1)
                        dve.tensor_copy(ck[:, t, :], psum[:, t - CT, 0:P]).then_inc(mixed, 1)
                    for t in range(CT):
                        k, n = KTS[t]
                        dve.wait_ge(turned, t + 1)
                        dve.tensor_copy(cT[:, k:k + n], psum[:, 2 + t % 2, 0:n]).then_inc(turned_out, 1)

                @block.gpsimd
                def _(pool):
                    pool.wait_ge(aggr_done, CT)
                    for lo, hi, n in ((0, CT - 1, P), (CT - 1, CT, tail)):
                        pool.tensor_scalar(rstd[0:n, lo:hi], mv[0:n, lo:hi, 1], EPS, None, ALU.add).then_inc(eps_added, 1)
                    pool.wait_ge(eps_added, 2)
                    for lo, hi, n in ((0, CT - 1, P), (CT - 1, CT, tail)):
                        pool.tensor_tensor(rstd[0:n, lo:hi], rstd[0:n, lo:hi], nhalf[0:n, lo:hi], ALU.pow).then_inc(rstd_done, 1)

                @block.scalar
                def _(act):
                    act.wait_ge(mixed, 1)
                    act.activation(cTh[:, SC:NK], cT[:, SC:NK], ACT.Copy)
                    for t in range(CT):
                        k, n = KTS[t]
                        act.wait_ge(turned_out, t + 1)
                        act.activation(cTh[:, k:k + n], cT[:, k:k + n], ACT.Copy)

                @block.tensor
                def _(pe):
                    pe.wait_ge(mixed, 1)
                    for t in range(CT, KT):
                        k, n = KTS[t]
                        pe.transpose(psum[:, t - CT, 0:P], cT[:, k:k + n], ident[:, :]).then_inc(transposed, 1)
                    for t in range(CT):
                        n = KTS[t][1]
                        pe.wait_ge(affine_done, t + 1)
                        wait(pe, turned_out, t - 1)
                        pe.transpose(psum[:, 2 + t % 2, 0:n], ck[0:n, t, :], ident[0:n, 0:n]).then_inc(turned, 1)
            clear()

            NG = 8
            WIDE = 1024
            STEP = 2
            SUM_AT, PROJ_AT, MAX_AT = 2, 6, KT - 2
            group_at = [1 + g for g in range(NG)]

            def loop(eng, body, prologue, epilogue):
                prologue()
                for r in range(STEP):
                    body(Unit(STEP, 0, r), r == 0, False)
                with eng.Fori(1, PAIRS // STEP - 1) as i:
                    for r in range(STEP):
                        body(Unit(STEP, i, r), False, False)
                for r in range(STEP):
                    body(Unit(STEP, PAIRS // STEP - 1, r), False, r == STEP - 1)
                epilogue(Unit(STEP, PAIRS // STEP - 1, STEP - 1))

            with nc.Block() as block:
                @block.tensor
                def _(pe):
                    def group(u, k, g):
                        hq, c = divmod(g, 2)
                        lo, hi = c * WIDE, min(NK, (c + 1) * WIDE)
                        wait(pe, max_read, NG * u.at(k) + g - 1)
                        for o in range(lo, hi, 512):
                            m = min(512, hi - o)
                            mm = pe.matmul(psum[:, 2 * (g % 2) + (o - lo) // 512, 0:m],
                                           qhi[:, PAIRS * b + u.at(k), hq * P:(hq + 1) * P],
                                           cTh[:, o:o + m], start=True, stop=True)
                        mm.then_inc(max_scores, 1)

                    def turn_max(u, k):
                        pe.wait_ge(max_done, u.at(k) + 1)
                        wait(pe, proj_read, u.at(k) - 1)
                        for hq in range(4):
                            mm = pe.matmul(psum[0:1, 7, hq * P:(hq + 1) * P], nm[:, u.buf(2, k), hq:hq + 1], ident[:, :],
                                           start=True, stop=True)
                        mm.then_inc(max_row, 1)

                    def broadcast_sum(u, k):
                        pe.wait_ge(summed, KT * (u.at(k) + 1))
                        wait(pe, proj_read, u.at(k))
                        pe.matmul(psum[:, 7, :], ones_f[:, :], psumm[:, u.buf(2, k), :], start=True, stop=True).then_inc(sum_bc, 1)

                    def project(u, k):
                        pe.wait_ge(o_scaled, u.at(k) + 1)
                        for q in range(QT):
                            for h in range(2):
                                mm = pe.matmul(psum[:, 7, q * D:(q + 1) * D], yn[:, h * S + q * P:h * S + (q + 1) * P],
                                               b_sb[:, 2 * u.at(k) + h, :], start=(h == 0), stop=(h == 1))
                        mm.then_inc(proj_made, 1)

                    def prologue():
                        u = Unit(STEP, 0, 0)
                        for g in range(NG):
                            group(u, 0, g)
                        turn_max(u, 0)

                    def body(u, first, last):
                        pe.wait_ge(shift_ready, u.at() + 1)
                        for s in range(KT + 1):
                            m = KT * u.r + s
                            if s < KT:
                                k, n = KTS[s]
                                wait(pe, exp_done, KT * u.at() + s - 1)
                                pe.matmul(psum[0:n, 4 + m % 2, :], cT[:, k:k + n], qp[:, PAIRS * b + u.at(), :], start=True, stop=False)
                                pe.matmul(psum[0:n, 4 + m % 2, :], ones_b[0:1, 0:n], nrow[0:1, u.buf(2), :],
                                          start=False, stop=True).then_inc(scored, 1)
                            if not last:
                                for g in range(NG):
                                    if group_at[g] == s:
                                        group(u, 1, g)
                            if s >= 1:
                                k, n = KTS[s - 1]
                                pe.wait_ge(exp_done, KT * u.at() + s)
                                if s == 1:
                                    wait(pe, o_copied, u.at())
                                pe.matmul(psum[:, 6, :], ck[0:n, s - 1, :], probs[0:n, (m - 1) % NP, :],
                                          start=(s == 1), stop=(s == KT)).then_inc(pv_done, 1)
                            if s == SUM_AT and not first:
                                broadcast_sum(u, -1)
                            if s == PROJ_AT and not first:
                                project(u, -1)
                            if s == MAX_AT and not last:
                                turn_max(u, 1)

                    def epilogue(u):
                        broadcast_sum(u, 0)
                        project(u, 0)

                    loop(pe, body, prologue, epilogue)

                @block.scalar
                def _(act):
                    def row(u, k):
                        act.wait_ge(max_row, u.at(k) + 1)
                        wait(act, scored, KT * u.at(k - 1))
                        act.activation(nrow[0:1, u.buf(2, k), :], psum[0:1, 7, :], ACT.Copy).then_inc(shift_ready, 1)

                    def copy_o(u, k):
                        act.wait_ge(pv_done, KT * (u.at(k) + 1))
                        wait(act, o_scaled, u.at(k))
                        act.activation(yraw[:, :], psum[:, 6, :], ACT.Copy).then_inc(o_copied, 1)

                    def body(u, first, last):
                        if not first:
                            copy_o(u, -1)
                        for s in range(KT):
                            m = KT * u.r + s
                            if s == MAX_AT + 1 and not last:
                                row(u, 1)
                            n = KTS[s][1]
                            act.wait_ge(scored, KT * u.at() + s + 1)
                            wait(act, pv_done, KT * u.at() + s - NP + 1)
                            wait(act, summed, KT * u.at() + s - NP + 1)
                            act.activation(probs[0:n, m % NP, :], psum[0:n, 4 + m % 2, :], ACT.Exp, scale=EA ** -0.5).then_inc(exp_done, 1)

                    loop(act, body, lambda: row(Unit(STEP, 0, 0), 0), lambda u: copy_o(u, 0))

                @block.vector
                def _(dve):
                    def group(u, k, g):
                        hq, c = divmod(g, 2)
                        m = min(NK, (c + 1) * WIDE) - c * WIDE
                        dve.wait_ge(max_scores, NG * u.at(k) + g + 1)
                        src = psum[:, 2 * (g % 2):2 * (g % 2) + 2, :].rearrange("p a n -> p (a n)")[:, 0:m]
                        dve.tensor_reduce(mp[:, u.buf(2, k), hq, c:c + 1], src, op=ALU.max, axis=AX.X).then_inc(max_read, 1)

                    def merge(u, k):
                        dve.wait_ge(max_read, NG * (u.at(k) + 1))
                        wait(dve, max_row, u.at(k) - 1)
                        dve.tensor_reduce(nm[:, u.buf(2, k), :], mp[:, u.buf(2, k), :, :], op=ALU.max, axis=AX.X,
                                          negate=True).then_inc(max_done, 1)

                    def scale(u, k):
                        dve.wait_ge(sum_bc, u.at(k) + 1)
                        dve.reciprocal(rec[:, :], psum[:, 7, :]).then_inc(rec_done, 1)
                        dve.wait_ge(rec_done, u.at(k) + 1)
                        dve.wait_ge(o_copied, u.at(k) + 1)
                        wait(dve, proj_made, u.at(k))
                        dve.tensor_tensor(yn[:, :], yraw[:, :], rec[:, :], ALU.mult).then_inc(o_scaled, 1)

                    def add(u, k):
                        dve.wait_ge(proj_made, u.at(k) + 1)
                        dve.tensor_tensor(acc[:, :, :], acc[:, :, :], psum[:, 7, 0:QT * D].rearrange("p (t d) -> p t d", t=QT),
                                          ALU.add).then_inc(proj_read, 1)

                    def prologue():
                        u = Unit(STEP, 0, 0)
                        for g in range(NG):
                            group(u, 0, g)
                        merge(u, 0)

                    def body(u, first, last):
                        for g in range(NG):
                            if not last:
                                group(u, 1, g)
                            if g == 1 and not first:
                                scale(u, -1)
                            if g == 5 and not first:
                                add(u, -1)
                        if not last:
                            merge(u, 1)

                    def epilogue(u):
                        scale(u, 0)
                        add(u, 0)
                        dve.wait_ge(proj_read, PAIRS)
                        dve.tensor_tensor(x_sb[:, bass.ds(QT * b, QT), :], x_sb[:, bass.ds(QT * b, QT), :], acc[:, :, :], ALU.add)

                    loop(dve, body, prologue, epilogue)

                @block.gpsimd
                def _(pool):
                    def body(u, first, last):
                        for s in range(KT):
                            m = KT * u.r + s
                            if s == 0:
                                continue
                            n = KTS[s][1]
                            pool.wait_ge(exp_done, KT * u.at() + s + 1)
                            if s == 1:
                                wait(pool, sum_bc, u.at() - 1)
                                pool.tensor_tensor(psumm[:, u.buf(2), :], probs[:, (m - 1) % NP, :], probs[:, m % NP, :],
                                                   ALU.add).then_inc(summed, 2)
                            else:
                                pool.wait_ge(summed, KT * u.at() + s)
                                pool.tensor_tensor(psumm[0:n, u.buf(2), :], psumm[0:n, u.buf(2), :], probs[0:n, m % NP, :],
                                                   ALU.add).then_inc(summed, 1)

                    loop(pool, body, lambda: None, lambda u: None)
            clear()
        st.close()

    def make_operands(st, jobs, vjobs, par):
        NJ, NV = len(jobs), len(vjobs)
        mixA, mixB, tot, rest, hi, mid, lo = par
        parts = (hi, mid, lo)
        with nc.Block() as block:
            @block.tensor
            def _(pe):
                vi = 0
                for j, job in enumerate(jobs):
                    n = job["n"]
                    wait(pe, mixed, 2 * (j - 1))
                    mm = pe.matmul(psum[:, 2 * (j % 2), 0:n], job["w"], job["rhs"], start=True, stop=True)
                    if job["ws"] is not None:
                        mm = pe.matmul(psum[:, 2 * (j % 2) + 1, 0:n], job["ws"], job["rhs"], start=True, stop=True)
                    mm.then_inc(up_made, 1)
                    while vi < NV and vi * NJ < (j + 1) * NV:
                        lhsT, rhs, n, dst, bias = vjobs[vi]
                        wait(pe, v_read, vi - 1)
                        mm = pe.matmul(psum[0:n, 4 + vi % 2, 0:D], lhsT, rhs, start=True, stop=bias is None)
                        if bias is not None:
                            mm = pe.matmul(psum[0:n, 4 + vi % 2, 0:D], ones_row[0:1, 0:n], bias, start=False, stop=True)
                        mm.then_inc(v_made, 1)
                        vi += 1

            @block.vector
            def _(dve):
                def remainder(j):
                    n = jobs[j]["n"]
                    dve.wait_ge(hi_done, j + 1)
                    wait(dve, lo_done, j - 1)
                    dve.tensor_tensor(rest[:, j % 2, 0:n], tot[:, j % 2, 0:n], hi[:, j % 2, 0:n], ALU.subtract).then_inc(rest_done, 1)

                for j, job in enumerate(jobs):
                    n = job["n"]
                    dve.wait_ge(up_made, j + 1)
                    wait(dve, summed, j - 1)
                    if job["ws"] is None:
                        dve.tensor_scalar(mixA[:, j % 2, 0:n], psum[:, 2 * (j % 2), 0:n], job["bias"], None, ALU.add).then_inc(mixed, 2)
                    else:
                        dve.tensor_tensor(mixA[:, j % 2, 0:n], psum[:, 2 * (j % 2), 0:n], job["cos"], ALU.mult).then_inc(mixed, 1)
                        dve.tensor_tensor(mixB[:, j % 2, 0:n], psum[:, 2 * (j % 2) + 1, 0:n], job["sin"], ALU.mult).then_inc(mixed, 1)
                    if j >= 1:
                        remainder(j - 1)
                remainder(NJ - 1)

            @block.gpsimd
            def _(pool):
                def last_part(j):
                    n = jobs[j]["n"]
                    pool.wait_ge(mid_done, j + 1)
                    wait(pool, parts_out[j % 2], 16 * SLOTS * (j // 2))
                    pool.tensor_tensor(lo[:, j % 2, 0:n], rest[:, j % 2, 0:n], mid[:, j % 2, 0:n], ALU.subtract).then_inc(lo_done, 1)

                for j, job in enumerate(jobs):
                    n = job["n"]
                    pool.wait_ge(mixed, 2 * (j + 1))
                    wait(pool, rest_done, j - 1)
                    if job["ws"] is None:
                        pool.tensor_copy(tot[:, j % 2, 0:n], mixA[:, j % 2, 0:n]).then_inc(summed, 1)
                    else:
                        pool.tensor_tensor(tot[:, j % 2, 0:n], mixA[:, j % 2, 0:n], mixB[:, j % 2, 0:n], ALU.add).then_inc(summed, 1)
                    if j >= 1:
                        last_part(j - 1)
                last_part(NJ - 1)

            @block.scalar
            def _(act):
                def middle(j):
                    n = jobs[j]["n"]
                    act.wait_ge(rest_done, j + 1)
                    wait(act, lo_done, j - 1)
                    act.activation(mid[:, j % 2, 0:n], rest[:, j % 2, 0:n], ACT.Copy).then_inc(mid_done, 1)

                vi = 0
                for j, job in enumerate(jobs):
                    n = job["n"]
                    act.wait_ge(summed, j + 1)
                    wait(act, rest_done, j - 1)
                    wait(act, parts_out[j % 2], 16 * SLOTS * (j // 2))
                    act.activation(hi[:, j % 2, 0:n], tot[:, j % 2, 0:n], ACT.Copy).then_inc(hi_done, 1)
                    if j >= 1:
                        middle(j - 1)
                    while vi < NV and vi * NJ < (j + 1) * NV:
                        _, _, n, dst, _ = vjobs[vi]
                        act.wait_ge(v_made, vi + 1)
                        act.activation(dst, psum[0:n, 4 + vi % 2, 0:D].rearrange("k (u h d) -> k u h d", u=PAIRS, h=2), ACT.Copy).then_inc(v_read, 1)
                        vi += 1
                middle(NJ - 1)

            @block.sync
            def _(sp):
                for j, job in enumerate(jobs):
                    n = job["n"]
                    for part, done in enumerate((hi_done, mid_done, lo_done)):
                        sp.wait_ge(done, j + 1)
                        for slot in range(SLOTS):
                            if job["parts"][slot] == part:
                                sp.dma_start(job["dst"](slot), parts[part][:, j % 2, 0:n]).then_inc(parts_out[j % 2], 16)
                sp.wait_ge(parts_out[0], 16 * SLOTS * ((NJ + 1) // 2))
                sp.wait_ge(parts_out[1], 16 * SLOTS * (NJ // 2))
        clear()

    def attention(bufs, NK, k_dram, m_dram, values, o_tok):
        kst, qst, vst, probs, mp, nm, oT, rec, sel = bufs
        KTS = key_tiles(NK)
        KT = len(KTS)
        WIDE = 1024
        if NK > WIDE // 4:
            groups = [(hq, c * WIDE, min(NK, (c + 1) * WIDE)) for hq in range(4) for c in range(2)]
            group_at = [1 + g for g in range(8)]
            TURN_AT, MAX_AT, NORM_BEHIND = 2, KT - 2, 2
        else:
            groups = [None]
            group_at = [0]
            TURN_AT, MAX_AT, NORM_BEHIND = 1, KT, 0
        NG = len(groups)
        k_units = k_dram.rearrange("b (h d) s n -> (b h) (d s) n", h=H)
        q_units = q_d.rearrange("b (h d) s n -> (b h) (d s) n", h=H)

        def loop(eng, body, prologue, epilogue):
            last = UNITS // RING - 1
            prologue()
            for r in range(RING):
                body(Unit(RING, 0, r), 0 * RING + r)
            with eng.Fori(1, last) as i:
                for r in range(RING):
                    body(Unit(RING, i, r), None)
            for r in range(RING):
                body(Unit(RING, last, r), last * RING + r)
            epilogue(Unit(RING, last, RING - 1))

        with nc.Block() as block:
            @block.sync
            def _(sp):
                def load(u, k):
                    wait(sp, scored, KT * u.at(k - RING + 1))
                    r = u.buf(RING, k)
                    for h in range(2):
                        lo = 64 * h + R0
                        sp.dma_start(kst[lo:lo + ROWS, r, 0:NK], k_units[2 * u.at(k) + h]).then_inc(ring_loaded[r], 16)
                        sp.dma_start(qst[lo:lo + ROWS, r, h * S:(h + 1) * S], q_units[2 * u.at(k) + h]).then_inc(ring_loaded[r], 16)
                    sp.dma_start(kst[1:66:64, r, 0:NK], m_dram[bass.ds(2 * u.at(k), 2), :]).then_inc(ring_loaded[r], 16)

                def prologue():
                    for k in range(RING - 1):
                        load(Unit(RING, 0, 0), k)

                def body(u, static):
                    if static is None or static + RING - 1 < UNITS:
                        load(u, RING - 1)

                loop(sp, body, prologue, lambda u: None)

            @block.tensor
            def _(pe):
                def group(u, k, g):
                    r = u.buf(RING, k)
                    if g == 0:
                        pe.wait_ge(ring_loaded[r], 16 * 5 * u.turn(k))
                        pe.wait_ge(row_cleared, 2 * u.at(k) + 2)
                    wait(pe, max_read, NG * u.at(k) + g - 1)
                    if groups[g] is None:
                        bank = 2 * u.buf(2, k)
                        for hq in range(4):
                            mm = pe.matmul(psum[:, bank + hq // 2, (hq % 2) * S:(hq % 2 + 1) * S], qst[:, r, hq * P:(hq + 1) * P],
                                           kst[:, r, 0:NK], start=True, stop=True)
                    else:
                        hq, lo, hi_ = groups[g]
                        for o in range(lo, hi_, 512):
                            m = min(512, hi_ - o)
                            mm = pe.matmul(psum[:, 2 * (g % 2) + (o - lo) // 512, 0:m], qst[:, r, hq * P:(hq + 1) * P],
                                           kst[:, r, o:o + m], start=True, stop=True)
                    mm.then_inc(max_scores, 1)

                def turn_max(u, k):
                    pe.wait_ge(max_done, u.at(k) + 1)
                    wait(pe, o_scaled, u.at(k - 1))
                    for h in range(2):
                        for q in range(QT):
                            mm = pe.matmul(psum[64 * h:64 * h + 1, 7, q * P:(q + 1) * P], nm[:, u.buf(2, k), 2 * h + q:2 * h + q + 1],
                                           ident[:, :], start=True, stop=True)
                    mm.then_inc(max_row, 1)

                def turn_o(u, k):
                    pe.wait_ge(o_copied, u.at(k) + 1)
                    wait(pe, o_scaled, u.at(k))
                    for q in range(QT):
                        mm = pe.matmul(psum[:, 7, S + 18 * q:S + 18 * (q + 1)], oT[:, u.buf(2, k), q * P:(q + 1) * P], sel[:, :],
                                       start=True, stop=True)
                    mm.then_inc(o_turned, 1)

                def prologue():
                    u = Unit(RING, 0, 0)
                    for g in range(NG):
                        group(u, 0, g)
                    turn_max(u, 0)

                def body(u, static):
                    first, last = static == 0, static == UNITS - 1
                    pe.wait_ge(shift_ready, 2 * u.at() + 2)
                    r = u.buf(RING)
                    for s in range(KT + 1):
                        m = KT * u.r + s
                        if s < KT:
                            k, n = KTS[s]
                            wait(pe, exp_done, KT * u.at() + s - 1)
                            pe.matmul(psum[0:n, 4 + m % 2, :], kst[:, r, k:k + n], qst[:, r, :], start=True, stop=True).then_inc(scored, 1)
                        if not last:
                            for g in range(NG):
                                if group_at[g] == s:
                                    group(u, 1, g)
                        if s >= 1:
                            n = KTS[s - 1][1]
                            if s == 1:
                                pe.wait_ge(v_staged, u.at() + 1)
                                wait(pe, o_copied, u.at())
                            pe.wait_ge(exp_done, KT * u.at() + s)
                            for h in range(2):
                                c = 2 * ((s - 1) % 2) + h
                                mm = pe.matmul(psum[VW * c:VW * (c + 1), 6, 0:S], vst[0:n, u.buf(2), s - 1, h, :],
                                               probs[0:n, (m - 1) % 2, h * S:(h + 1) * S], start=(s <= 2), stop=(s > KT - 2))
                            mm.then_inc(pv_done, 1)
                        if s == TURN_AT and not first:
                            turn_o(u, -1)
                        if s == MAX_AT and not last:
                            turn_max(u, 1)

                loop(pe, body, prologue, lambda u: turn_o(u, 0))

            @block.scalar
            def _(act):
                def rows(u, k):
                    act.wait_ge(max_row, u.at(k) + 1)
                    r = u.buf(RING, k)
                    act.activation(qst[0:1, r, 0:S], psum[0:1, 7, 0:S], ACT.Copy).then_inc(shift_ready, 1)
                    act.activation(qst[64:65, r, S:2 * S], psum[64:65, 7, 0:S], ACT.Copy).then_inc(shift_ready, 1)

                def copy_o(u, k):
                    act.wait_ge(pv_done, KT * (u.at(k) + 1))
                    wait(act, o_turned, u.at(k) - 1)
                    act.activation(oT[:, u.buf(2, k), :], psum[:, 6, 0:S], ACT.Copy).then_inc(o_copied, 1)

                def body(u, static):
                    first, last = static == 0, static == UNITS - 1
                    if not first:
                        copy_o(u, -1)
                    for s in range(KT):
                        m = KT * u.r + s
                        if s == MAX_AT + 1 and not last:
                            rows(u, 1)
                        n = KTS[s][1]
                        act.wait_ge(scored, KT * u.at() + s + 1)
                        wait(act, pv_done, KT * u.at() + s - 1)
                        act.activation(probs[0:n, m % 2, :], psum[0:n, 4 + m % 2, :], ACT.Exp, scale=HD ** -0.5).then_inc(exp_done, 1)
                    if MAX_AT + 1 >= KT and not last:
                        rows(u, 1)

                loop(act, body, lambda: rows(Unit(RING, 0, 0), 0), lambda u: copy_o(u, 0))

            @block.vector
            def _(dve):
                def group(u, k, g):
                    dve.wait_ge(max_scores, NG * u.at(k) + g + 1)
                    if groups[g] is None:
                        wait(dve, max_row, u.at(k) - 1)
                        src = psum[:, 2 * u.buf(2, k):2 * u.buf(2, k) + 2, :].rearrange("p a (h n) -> p (a h) n", h=2)
                        dve.tensor_reduce(nm[:, u.buf(2, k), :], src, op=ALU.max, axis=AX.X, negate=True).then_inc(max_read, 1)
                        return
                    hq, lo, hi_ = groups[g]
                    src = psum[:, 2 * (g % 2):2 * (g % 2) + 2, :].rearrange("p a n -> p (a n)")[:, 0:hi_ - lo]
                    dve.tensor_reduce(mp[:, u.buf(2, k), hq, g % 2:g % 2 + 1], src, op=ALU.max, axis=AX.X).then_inc(max_read, 1)

                def merge(u, k):
                    dve.wait_ge(max_read, NG * (u.at(k) + 1))
                    if groups[0] is None:
                        dve.sem_inc(max_done, 1)
                        return
                    wait(dve, max_row, u.at(k) - 1)
                    dve.tensor_reduce(nm[:, u.buf(2, k), :], mp[:, u.buf(2, k), :, :], op=ALU.max, axis=AX.X,
                                      negate=True).then_inc(max_done, 1)

                def normalise(u, k):
                    dve.wait_ge(o_turned, u.at(k) + 1)
                    o = psum[:, 7, S:S + 36].rearrange("p (g e) -> p g e", g=4)
                    dve.reciprocal(rec[:, u.buf(2, k), :], o[:, :, HD]).then_inc(rec_done, 1)
                    dve.wait_ge(rec_done, u.at(k) + 1)
                    dve.tensor_tensor(o_tok[:, u.at(k), :, :], o[:, :, 0:HD],
                                      rec[:, u.buf(2, k), :].unsqueeze(2).to_broadcast([P, 4, HD]), ALU.mult).then_inc(o_scaled, 1)

                def clear_row(u, k):
                    wait(dve, scored, KT * u.at(k - RING + 1))
                    r = u.buf(RING, k)
                    dve.memset(qst[0:1, r, 0:S].bitcast(U32), 0).then_inc(row_cleared, 1)
                    dve.memset(qst[64:65, r, S:2 * S].bitcast(U32), 0).then_inc(row_cleared, 1)

                def stage(u, k):
                    wait(dve, pv_done, KT * u.at(k - 1))
                    dve.tensor_copy(vst[:, u.buf(2, k), 0:KT, :, 0:HD + 1], values[:, u.at(k), :, :, :]).then_inc(v_staged, 1)

                def prologue():
                    u = Unit(RING, 0, 0)
                    clear_row(u, 0)
                    clear_row(u, 1)
                    stage(u, 0)
                    for g in range(NG):
                        group(u, 0, g)
                    merge(u, 0)

                def body(u, static):
                    first, last = static == 0, static == UNITS - 1
                    for g in range(NG):
                        if not last:
                            group(u, 1, g)
                            if g == NG - 1:
                                merge(u, 1)
                        if g == NORM_BEHIND:
                            if not first:
                                normalise(u, -1)
                            if static is None or static + 2 < UNITS:
                                clear_row(u, 2)
                            if not last:
                                stage(u, 1)

                loop(dve, body, prologue, lambda u: normalise(u, 0))
        clear()

    def project_out(o_tok, oTT, w, bias, z):
        with nc.Block() as block:
            @block.tensor
            def _(pe):
                for t in range(TILES):
                    pe.wait_ge(swept, t + 1)
                    pe.transpose(psum[:, t // 4, (t % 4) * P:(t % 4 + 1) * P], xhat[:, t, :], ident[:, :]).then_inc(turned, 1)
                for t in range(TILES):
                    k = t // 4
                    pe.wait_ge(turned_out, k + 1)
                    o = psum[:, 2 + k, (t % 4) * D:(t % 4 + 1) * D]
                    mm = pe.matmul(o, oTT[:, t * P:(t + 1) * P], w, start=True, stop=bias is None)
                    if bias is not None:
                        mm = pe.matmul(o, ones_row[0:1, :], bias, start=False, stop=True)
                    mm.then_inc(proj_made, 1)

            @block.gpsimd
            def _(pool):
                for t in range(TILES):
                    b, q = divmod(t, QT)
                    pool.tensor_copy(xhat[:, t, :].rearrange("p (u h d) -> p u h d", u=PAIRS, h=2),
                                     o_tok[:, b * PAIRS:(b + 1) * PAIRS, 2 * q:2 * q + 2, :]).then_inc(swept, 1)

            @block.scalar
            def _(act):
                for k in range(2):
                    act.wait_ge(turned, 4 * (k + 1))
                    act.activation(oTT[:, k * 512:(k + 1) * 512], psum[:, k, :], ACT.Copy).then_inc(turned_out, 1)

            @block.vector
            def _(dve):
                for k in range(2):
                    dve.wait_ge(proj_made, 4 * (k + 1))
                    dve.tensor_tensor(z[:, 4 * k:4 * k + 4, :], z[:, 4 * k:4 * k + 4, :],
                                      psum[:, 2 + k, :].rearrange("p (t d) -> p t d", t=4), ALU.add)
        clear()

    def feed_forward(w1, b1, w2, b2, hT, z):
        with nc.Block() as block:
            @block.tensor
            def _(pe):
                for k in range(2):
                    for c in range(FC):
                        n = FC * k + c
                        wait(pe, act_done, n - 1)
                        pe.matmul(psum[:, n % 2, :], w1[:, c * P:(c + 1) * P], xnT[:, k * 512:(k + 1) * 512],
                                  start=True, stop=True).then_inc(up_made, 1)
                for t in range(TILES):
                    k = t // 4
                    pe.wait_ge(act_done, FC * (k + 1))
                    o = psum[:, 2 + k, (t % 4) * D:(t % 4 + 1) * D]
                    for c in range(FC):
                        pe.matmul(o, hT[:, c, t * P:(t + 1) * P], w2[:, c * D:(c + 1) * D], start=(c == 0), stop=False)
                    pe.matmul(o, ones_row[0:1, :], b2, start=False, stop=True).then_inc(down_made, 1)

            @block.scalar
            def _(act):
                for k in range(2):
                    for c in range(FC):
                        act.wait_ge(up_made, FC * k + c + 1)
                        act.activation(hT[:, c, k * 512:(k + 1) * 512], psum[:, (FC * k + c) % 2, :], ACT.Gelu,
                                       bias=b1[:, c:c + 1]).then_inc(act_done, 1)

            @block.vector
            def _(dve):
                for k in range(2):
                    dve.wait_ge(down_made, 4 * (k + 1))
                    dve.tensor_tensor(z[:, 4 * k:4 * k + 4, :], z[:, 4 * k:4 * k + 4, :],
                                      psum[:, 2 + k, :].rearrange("p (t d) -> p t d", t=4), ALU.add)
        clear()

    def experts(gate_w, gate_b, w1_d, b1_d, w2_d, b2_d, func, top, z, tag):
        with ExitStack() as st:
            hT = sb(st, tag + "_moe_h", [P, FC, NTOK])
            w1 = sb(st, tag + "_moe_w1", [P, 2, DFF])
            w2 = sb(st, tag + "_moe_w2", [P, 2, DFF])
            b1 = sb(st, tag + "_moe_b1", [P, 2, FC])
            b2 = sb(st, tag + "_moe_b2", [1, 2, D])
            gw = sb(st, tag + "_gate_w", [P, E])
            gb = sb(st, tag + "_gate_b", [1, E])
            iota = sb(st, tag + "_iota", [P, E])
            logit = sb(st, tag + "_logit", [P, TILES, E])
            best = sb(st, tag + "_best", [P, TILES, 8])
            besti = sb(st, tag + "_besti", [P, TILES, 8], U32)
            bestf = sb(st, tag + "_bestf", [P, TILES, 8])
            g1 = sb(st, tag + "_g1", [P, TILES, 2])
            we = sb(st, tag + "_we", [P, TILES, E])
            tmp = sb(st, tag + "_moe_tmp", [P, TILES, E])
            wcol = sb(st, tag + "_wcol", [P, 2, TILES])
            with nc.Block() as block:
                @block.sync
                def _(sp):
                    sp.dma_start(gw[:, :], gate_w).then_inc(loaded, 16)
                    sp.dma_start(iota[:, :], T["iota"]).then_inc(loaded, 16)
                    if gate_b is not None:
                        sp.dma_start(gb[:, :], gate_b).then_inc(loaded, 16)

                @block.tensor
                def _(pe):
                    pe.wait_ge(loaded, 48 if gate_b is not None else 32)
                    for t in range(TILES):
                        mm = pe.matmul(psum[:, 0, t * E:(t + 1) * E], xnT[:, t * P:(t + 1) * P], gw[:, :], start=True, stop=gate_b is None)
                        if gate_b is not None:
                            mm = pe.matmul(psum[:, 0, t * E:(t + 1) * E], ones_row[0:1, :], gb[:, :], start=False, stop=True)
                    mm.then_inc(gate_made, 1)

                @block.scalar
                def _(act):
                    if top == 2:
                        act.wait_ge(gate_step, 4)
                        act.activation(g1[:, :, 1:2], g1[:, :, 0:1], ACT.Exp).then_inc(gate_exp, 1)

                @block.vector
                def _(dve):
                    n = [0]

                    def link(ins):
                        n[0] += 1
                        ins.then_inc(gate_step, 1)
                        dve.wait_ge(gate_step, n[0])

                    dve.wait_ge(gate_made, 1)
                    dve.wait_ge(loaded, 48 if gate_b is not None else 32)
                    link(dve.tensor_copy(logit[:, :, :], psum[:, 0, 0:TILES * E].rearrange("p (t e) -> p t e", e=E)))
                    for t in range(TILES):
                        ins = dve.max(best[:, t, :], logit[:, t, :])
                        ins.then_inc(chain, 1)
                    dve.wait_ge(chain, TILES)
                    for t in range(TILES):
                        ins = dve.max_index(besti[:, t, :], best[:, t, :], logit[:, t, :])
                        ins.then_inc(swept, 1)
                    dve.wait_ge(swept, TILES)
                    link(dve.tensor_copy(bestf[:, :, :], besti[:, :, :]))
                    ids = iota[:, :].unsqueeze(1).to_broadcast([P, TILES, E])
                    link(dve.tensor_tensor(we[:, :, :], ids, bestf[:, :, 0:1].to_broadcast([P, TILES, E]), ALU.is_equal))
                    if top == 2:
                        link(dve.tensor_tensor(g1[:, :, 0:1], best[:, :, 1:2], best[:, :, 0:1], ALU.subtract))
                        link(dve.tensor_tensor(tmp[:, :, :], ids, bestf[:, :, 1:2].to_broadcast([P, TILES, E]), ALU.is_equal))
                        dve.wait_ge(gate_exp, 1)
                        link(dve.tensor_tensor(tmp[:, :, :], tmp[:, :, :], g1[:, :, 1:2].to_broadcast([P, TILES, E]), ALU.mult))
                        link(dve.tensor_tensor(we[:, :, :], we[:, :, :], tmp[:, :, :], ALU.add))
                        link(dve.tensor_scalar(g1[:, :, 0:1], g1[:, :, 1:2], 1.0, None, ALU.add))
                        link(dve.reciprocal(g1[:, :, 1:2], g1[:, :, 0:1]))
                        link(dve.tensor_tensor(we[:, :, :], we[:, :, :], g1[:, :, 1:2].to_broadcast([P, TILES, E]), ALU.mult))
            clear()

            NU = 2 * FC
            with nc.Block() as block:
                @block.sync
                def _(sp):
                    with sp.Fori(0, E // 2) as i:
                        for r in range(2):
                            sp.wait_ge(swept, 2 * i + r + 1)
                            e = 2 * i + r
                            sp.dma_start(w1[:, r, :], w1_d[e]).then_inc(weights_in[r], 16)
                            sp.dma_start(w2[:, r, :], w2_d[e]).then_inc(weights_in[r], 16)
                            sp.dma_start(b1[:, r, :], b1_d[e]).then_inc(weights_in[r], 16)
                            sp.dma_start(b2[:, r, :], b2_d[e]).then_inc(weights_in[r], 16)

                @block.tensor
                def _(pe):
                    pe.sem_inc(swept, 2)
                    with pe.Fori(0, E // 2) as i:
                        for r in range(2):
                            pe.wait_ge(weights_in[r], 64 * i + 64)
                            for k in range(2):
                                for c in range(FC):
                                    n = FC * k + c
                                    pe.wait_ge(act_done, NU * (2 * i + r) + n + 1)
                                    pe.matmul(psum[:, n % 2, :], w1[:, r, c * P:(c + 1) * P], xnT[:, k * 512:(k + 1) * 512],
                                              start=True, stop=True).then_inc(up_made, 1)
                            for t in range(TILES):
                                k = t // 4
                                if t % 4 == 0:
                                    pe.wait_ge(act_done, NU * (2 * i + r) + FC * (k + 1) + 2)
                                    pe.wait_ge(down_read, TILES * (2 * i + r) + 4 * k + 4)
                                o = psum[:, 2 + k, (t % 4) * D:(t % 4 + 1) * D]
                                for c in range(FC):
                                    pe.matmul(o, hT[:, c, t * P:(t + 1) * P], w2[:, r, c * D:(c + 1) * D], start=(c == 0), stop=False)
                                mm = pe.matmul(o, ones_row[0:1, :], b2[0:1, r, :], start=False, stop=True)
                                if t % 4 == 3:
                                    mm.then_inc(down_made, 1)
                            pe.wait_ge(down_made, 2 * (2 * i + r) + 2)
                            pe.sem_inc(swept, 1)

                @block.scalar
                def _(act):
                    act.sem_inc(act_done, 2)
                    with act.Fori(0, E // 2) as i:
                        for r in range(2):
                            for k in range(2):
                                for c in range(FC):
                                    n = FC * k + c
                                    act.wait_ge(up_made, NU * (2 * i + r) + n + 1)
                                    if c == 0:
                                        act.wait_ge(swept, 2 * i + r + 2 - 0)
                                    act.activation(hT[:, c, k * 512:(k + 1) * 512], psum[:, n % 2, :], func,
                                                   bias=b1[:, r, c:c + 1]).then_inc(act_done, 1)

                @block.vector
                def _(dve):
                    dve.sem_inc(down_read, TILES)
                    with dve.Fori(0, E // 2) as i:
                        for r in range(2):
                            dve.tensor_copy(wcol[:, r, :], we[:, :, 2 * i + r]).then_inc(chain, 1)
                            dve.wait_ge(chain, 2 * i + r + 1)
                            for t in range(TILES):
                                k = t // 4
                                if t % 4 == 0:
                                    dve.wait_ge(down_made, 2 * (2 * i + r) + k + 1)
                                dve.scalar_tensor_tensor(z[:, t, :], psum[:, 2 + k, (t % 4) * D:(t % 4 + 1) * D], wcol[:, r, t:t + 1],
                                                         z[:, t, :], ALU.mult, ALU.add).then_inc(down_read, 1)
            clear()

    def add_into(a, b):
        with nc.Block() as block:
            @block.vector
            def _(dve):
                dve.tensor_tensor(a[:, :, :], a[:, :, :], b[:, :, :], ALU.add)
        clear()

    def finish(src, inner=None):
        with nc.Block() as block:
            @block.sync
            def _(sp):
                sp.dma_start(out.rearrange("b (t p) d -> p (b t) d", p=P), src[:, :, :]).then_inc(stored, 16)
                sp.wait_ge(stored, 16)
        if inner is not None:
            inner.close()
        top.close()

    resampler()
    if stop == "A":
        return finish(x_sb)

    KTC = len(key_tiles(SC))
    st = ExitStack()
    KTS_SELF = S // P
    v_self = sb(st, "v_self", [P, UNITS, KTS_SELF, 2, HD + 1])
    kst = sb(st, "kst", [P, RING, SC], BF16)
    qst = sb(st, "qst", [P, RING, 2 * S], BF16)
    vst = sb(st, "vst", [P, 2, KTC, 2, VW])
    probs = sb(st, "probs8", [P, 2, 2 * S])
    mp = sb(st, "mp8", [P, 2, 4, 2])
    nm = sb(st, "nm8", [P, 2, 4])
    oT = sb(st, "oT", [P, 2, S])
    rec = sb(st, "rec8", [P, 2, 4])
    sel = sb(st, "sel", [P, 18])
    o_tok = sb(st, "o_tok", [P, UNITS, 4, HD])
    oTT = sb(st, "oTT", [P, NTOK])
    bufs = (kst, qst, vst, probs, mp, nm, oT, rec, sel)
    par = (sb(st, "mixA", [P, 2, 512]), sb(st, "mixB", [P, 2, 512]), sb(st, "tot", [P, 2, 512]), sb(st, "rest", [P, 2, 512]),
           sb(st, "hi", [P, 2, 512], BF16), sb(st, "mid", [P, 2, 512], BF16), sb(st, "lo", [P, 2, 512], BF16))

    with nc.Block() as block:
        @block.vector
        def _(dve):
            dve.memset(qst[:, :, :], 0.0)
            dve.memset(v_self[:, :, :, :, :], 1.0)
            dve.memset(kst[:, :, :], 0.0).then_inc(zeroed, 1)
            dve.wait_ge(zeroed, 1)
            dve.memset(kst[0:1, :, :], 1.0)
            dve.memset(kst[64:65, :, :], 1.0)

        @block.gpsimd
        def _(pool):
            pool.memset(vst[:, :, :, :, :], 0.0)

        @block.sync
        def _(sp):
            sp.dma_start(sel[:, :], T["sel"]).then_inc(loaded, 16)
            sp.wait_ge(loaded, 16)
    clear()
    with nc.Block() as block:
        @block.sync
        def _(sp):
            for r in range(RING):
                sp.dma_start(qst[1:2, r, 0:S], T["ones"]).then_inc(loaded2, 16)
                sp.dma_start(qst[65:66, r, S:2 * S], T["ones"]).then_inc(loaded2, 16)
            sp.wait_ge(loaded2, 32 * RING)
    clear()

    with ExitStack() as s2:
        wqkv = sb(s2, "wqkv", [P, 3 * D])
        wo2 = sb(s2, "wo2", [P, D])
        bq = sb(s2, "bq", [P, 2])
        bvr = sb(s2, "bvr", [1, D])
        bor = sb(s2, "bor", [1, D])
        with nc.Block() as block:
            @block.sync
            def _(sp):
                sp.dma_start(wqkv[:, :], T["w_qkv"]).then_inc(loaded, 16)
                sp.dma_start(wo2[:, :], T["w_o"]).then_inc(loaded, 16)
                sp.dma_start(bq[:, :], T["b_qk"]).then_inc(loaded, 16)
                sp.dma_start(bvr[:, :], T["b_v"]).then_inc(loaded, 16)
                sp.dma_start(bor[:, :], T["b_o"]).then_inc(loaded, 16)
                sp.wait_ge(loaded, 80)
        clear()
        layer_norm(x_sb, z_sb)
        layer_norm(z_sb, xhat, turn=xnT, affine=(lambda b: vecs[:, 2:3], lambda b: vecs[:, 3:4]))
        jobs, vjobs = [], []
        for b in range(B):
            for w, parts, dram in ((0, PARTS_Q, q_d), (1, PARTS_K, k_self_d)):
                jobs.append(dict(n=S, w=wqkv[:, w * D:(w + 1) * D], ws=None, bias=bq[:, w:w + 1], rhs=xnT[:, b * S:(b + 1) * S],
                                 parts=parts, dst=lambda slot, b=b, dram=dram: dram[b, :, slot, :]))
            for t in range(KTS_SELF):
                at = b * S + t * P
                vjobs.append((xnT[:, at:at + P], wqkv[:, 2 * D:3 * D], P,
                              v_self[:, b * PAIRS:(b + 1) * PAIRS, t, :, 0:HD], bvr[0:1, :]))
        make_operands(st, jobs, vjobs, par)
        attention(bufs, S, k_self_d, m_none_d, v_self, o_tok)
        project_out(o_tok, oTT, wo2[:, :], bor[0:1, :], z_sb)
    if stop == "B1":
        return finish(z_sb, st)
    layer_norm(z_sb, xhat, turn=xnT, affine=(lambda b: vecs[:, 4:5], lambda b: vecs[:, 5:6]))
    experts(T["w_gate"], None, T["L0_w1"], T["L0_b1"], T["L0_w2"], T["L0_b2"], ACT.Gelu_apprx_tanh, 2, z_sb, "l0")
    add_into(x_sb, z_sb)
    if stop == "B":
        return finish(x_sb, st)

    with ExitStack() as s2:
        v_ctx = sb(s2, "v_ctx", [P, UNITS, KTC, 2, HD + 1])
        ctxT = sb(s2, "ctxT", [P, B * SC])
        cos = sb(s2, "cos", [P, SC])
        sin = sb(s2, "sin", [P, SC])
        W = sb(s2, "W", [P, WCOLS])
        hT = oTT

        layer_norm(x_sb, z_sb)
        with nc.Block() as block:
            @block.sync
            def _(sp):
                sp.dma_start(ctxT[:, :], T["ctxT"]).then_inc(loaded, 16)
                sp.dma_start(cos[:, :], T["cos"]).then_inc(loaded, 16)
                sp.dma_start(sin[:, :], T["sin"]).then_inc(loaded, 16)
                sp.wait_ge(loaded, 48)

            @block.vector
            def _(dve):
                dve.memset(v_ctx[:, :, :, :, :], 1.0)
        clear()

        def w(name):
            at, n = COL[name]
            return W[:, at:at + n]

        def rope_jobs(wn, ws, rhs, n, pos, parts, dst):
            return dict(n=n, w=w(wn), ws=w(ws), rhs=rhs, cos=cos[:, pos:pos + n], sin=sin[:, pos:pos + n], parts=parts, dst=dst)

        with nc.Fori(0, NL if stop != "C1" else 1) as l:
            with nc.Block() as block:
                @block.sync
                def _(sp):
                    sp.dma_start(W[:, :], T["layers"][l]).then_inc(loaded, 16)
                    sp.dma_start(brow[0:1, 0:D], T["f2_b"][l]).then_inc(loaded, 16)
                    sp.wait_ge(loaded, 32)
            clear()
            layer_norm(z_sb, xhat, turn=xnT, modulate=(w("n1"), w("n1b")))
            jobs, vjobs = [], []
            for b in range(B):
                for wn, parts, dram in (("q", PARTS_Q, q_d), ("k", PARTS_K, k_self_d)):
                    jobs.append(rope_jobs(wn, wn + "s", xnT[:, b * S:(b + 1) * S], S, 0, parts,
                                          lambda slot, b=b, dram=dram: dram[b, :, slot, :]))
                for t in range(KTS_SELF):
                    at = b * S + t * P
                    vjobs.append((xnT[:, at:at + P], w("v"), P, v_self[:, b * PAIRS:(b + 1) * PAIRS, t, :, 0:HD], None))
            make_operands(st, jobs, vjobs, par)
            attention(bufs, S, k_self_d, m_self_d, v_self, o_tok)
            project_out(o_tok, oTT, w("so"), None, z_sb)
            layer_norm(z_sb, xhat, turn=xnT, modulate=(w("n2"), w("n2b")))
            jobs, vjobs = [], []
            cuts = [0, 401, 801, 1201, SC]
            for b in range(B):
                jobs.append(rope_jobs("cq", "cqs", xnT[:, b * S:(b + 1) * S], S, 0, PARTS_Q, lambda slot, b=b: q_d[b, :, slot, :]))
                for lo_, hi_ in zip(cuts, cuts[1:]):
                    jobs.append(rope_jobs("ck", "cks", ctxT[:, b * SC + lo_:b * SC + hi_], hi_ - lo_, lo_, PARTS_K,
                                          lambda slot, b=b, lo_=lo_, hi_=hi_: k_ctx_d[b, :, slot, lo_:hi_]))
                for t, (k, n) in enumerate(key_tiles(SC)):
                    vjobs.append((ctxT[:, b * SC + k:b * SC + k + n], w("cv"), n,
                                  v_ctx[0:n, b * PAIRS:(b + 1) * PAIRS, t, :, 0:HD], None))
            make_operands(st, jobs, vjobs, par)
            attention(bufs, SC, k_ctx_d, m_ctx_d, v_ctx, o_tok)
            project_out(o_tok, oTT, w("co"), None, z_sb)
            layer_norm(z_sb, xhat, turn=xnT, modulate=(w("n3"), w("n3b")))
            with ExitStack() as s3:
                hid = sb(s3, "hid", [P, FC, NTOK])
                feed_forward(w("f1"), w("f1b"), w("f2"), brow[0:1, 0:D], hid, z_sb)
    if stop in ("C", "C1"):
        return finish(z_sb, st)
    add_into(x_sb, z_sb)

    layer_norm(x_sb, xhat, turn=xnT, affine=(lambda b: 1.0, lambda b: 0.0))
    experts(T["gate_w"], T["gate_b"], T["L1_w1"], T["L1_b1"], T["L1_w2"], T["L1_b2"], ACT.Relu, 1, x_sb, "l1")
    st.close()
    finish(x_sb)


def _layout(I):
    f = np.ascontiguousarray
    A = {k: np.asarray(v) for k, v in I.items()}
    T = {}
    T["x"] = A["x"]
    T["ctx"] = A["ctx_1024"]
    T["ctxT"] = f(A["ctx_1024"].transpose(2, 0, 1).reshape(D, B * SC))
    T["condT"] = f(A["cond_1024"].T)
    T["mask_ctx"] = f(np.repeat(A["mask_BxS2_bf0"], H, axis=0))
    T["mask_x"] = f(np.repeat(A["mask_BxS_bf0"], H, axis=0))
    T["ident"] = np.eye(P, dtype=np.float32)
    names = ["L0_xcond_ln2_w", "L0_xcond_ln2_b", "L0_ffn_ln1_w", "L0_ffn_ln1_b", "L0_ffn_ln2_w", "L0_ffn_ln2_b"]
    T["vecs"] = f(np.stack([A[n] for n in names] * 2, axis=1))
    T["ln1_w"], T["ln1_b"] = A["L0_xcond_ln1_w"].reshape(1, D), A["L0_xcond_ln1_b"].reshape(1, D)
    heads = lambda a: f(a.reshape(H, EA, D).transpose(1, 0, 2))
    T["Wq"] = heads(A["L0_xcond_Wq"])
    T["Wk"] = heads(A["L0_xcond_Wkv"][:H * EA])
    T["Wv"] = heads(A["L0_xcond_Wkv"][H * EA:])
    T["Wo"] = heads(A["L0_xcond_Wo"].T)
    sel = np.zeros((P, 18), np.float32)
    for c in range(4):
        for e in range(HD + 1):
            sel[VW * c + e, (HD + 1) * (c % 2) + e] = 1
    T["sel"] = sel
    T["ones"] = np.ones((1, S), T_BF16())
    T["iota"] = f(np.tile(np.arange(E, dtype=np.float32), (P, 1)))
    half = HD // 2
    inv = (np.float32(1.0) / np.float32(10000.0) ** (np.arange(half, dtype=np.float32) / np.float32(half))).astype(np.float32)
    ang = (np.arange(SC, dtype=np.float32)[:, None] * inv).astype(np.float32)
    c, s = np.cos(ang).T, np.sin(ang).T
    T["cos"] = f(np.tile(np.concatenate([c, c]), (H, 1)).astype(np.float32))
    T["sin"] = f(np.tile(np.concatenate([-s, s]), (H, 1)).astype(np.float32))
    T["w_qkv"], T["w_o"] = A["L0_ffn_w_qkv"], A["L0_ffn_w_o"]
    bqkv = A["L0_ffn_b_qkv"].reshape(3, D)
    T["b_qk"] = f(bqkv[0:2].T)
    T["b_v"] = f(bqkv[2:3])
    T["b_o"] = A["L0_ffn_b_o"].reshape(1, D)
    T["w_gate"] = A["L0_ffn_w_gate"]
    T["L0_w1"] = A["L0_ffn_w1"]
    T["L0_b1"] = f(A["L0_ffn_b1"].reshape(E, FC, P).transpose(0, 2, 1))
    T["L0_w2"] = f(A["L0_ffn_w2"].reshape(E, FC, P, D).transpose(0, 2, 1, 3).reshape(E, P, FC * D))
    T["L0_b2"] = A["L0_ffn_b2"].reshape(E, 1, D)
    T["gate_w"] = f(A["L1_ffn_gate_w"].T)
    T["gate_b"] = A["L1_ffn_gate_b"].reshape(1, E)
    T["L1_w1"] = f(A["L1_ffn_w1"].transpose(0, 2, 1))
    T["L1_b1"] = f(A["L1_ffn_b1"].reshape(E, FC, P).transpose(0, 2, 1))
    T["L1_w2"] = f(A["L1_ffn_w2"].reshape(E, D, FC, P).transpose(0, 3, 2, 1).reshape(E, P, FC * D))
    T["L1_b2"] = A["L1_ffn_b2"].reshape(E, 1, D)
    g = lambda n: A["L1_xcond_" + n]
    swap = np.arange(D).reshape(H, 2, half)[:, ::-1].reshape(D)
    t = lambda a: a.transpose(0, 2, 1)
    qkv = g("qkv_w")
    q, k, v = qkv[:, 0:D], qkv[:, D:2 * D], qkv[:, 2 * D:]
    col = lambda a, n: a.reshape(NL, n, P).transpose(0, 2, 1)
    parts = [t(g("n1_w")), t(g("n2_w")), t(g("n3_w")), t(q), t(q[:, swap]), t(k), t(k[:, swap]), t(v), t(g("so_w")),
             t(g("cq_w")), t(g("cq_w")[:, swap]), t(g("ck_w")), t(g("ck_w")[:, swap]), t(g("cv_w")), t(g("co_w")), t(g("f1_w")),
             g("f2_w").reshape(NL, D, FC, P).transpose(0, 3, 2, 1).reshape(NL, P, FC * D),
             col(g("n1_b"), 2), col(g("n2_b"), 2), col(g("n3_b"), 2), col(g("f1_b"), FC)]
    T["layers"] = f(np.concatenate(parts, axis=2))
    T["f2_b"] = g("f2_b").reshape(NL, 1, D)
    return {n: f(a) for n, a in T.items()}


def T_BF16():
    return mybir.dt.np(BF16)


def kernel(**inputs):
    import concourse.bacc as _bacc
    from concourse.bass_utils import run_bass_kernel_spmd as _run

    T = _layout(inputs)
    nc = _bacc.Bacc("TRN2", target_bir_lowering=False, num_devices=1)
    arrays, aps = {}, {}
    for name, a in T.items():
        arrays[f"in_{name}"] = a
        aps[name] = nc.dram_tensor(f"in_{name}", a.shape, mybir.dt.from_np(a.dtype), kind="ExternalInput").ap()
    out = nc.dram_tensor("out", (B, S, D), F32, kind="ExternalOutput").ap()
    build_program(nc, aps, out)
    r = _run(nc, [arrays], core_ids=[0])
    return r.results[0]["out"]
```

```python
from contextlib import ExitStack

import numpy as np

import concourse.bass as bass
from concourse import mybir

F32 = mybir.dt.float32
BF16 = mybir.dt.bfloat16
U8 = mybir.dt.uint8
U32 = mybir.dt.uint32
ALU = mybir.AluOpType
ACT = mybir.ActivationFunctionType
AX = mybir.AxisListType

P = 128
B, S, D = 4, 256, 128
NTOK = B * S
TILES = NTOK // P
QT = S // P
SC = 1601
H, HD = 16, 8
PAIRS = H // 2
UNITS = B * PAIRS
NL, DFF, E = 6, 512, 8
FC = DFF // P
EA = 64
EPS = 1e-5
MASKED = -1.0e30

PARTS_Q = (0, 0, 1, 0, 2, 1)
PARTS_K = (0, 1, 0, 2, 0, 1)
SLOTS = len(PARTS_Q)
ROWS = HD * SLOTS
R0 = 2
VW = 32
RING = 4

_NAMES = [("n1", 256), ("n2", 256), ("n3", 256), ("q", 128), ("qs", 128), ("k", 128), ("ks", 128), ("v", 128),
          ("so", 128), ("cq", 128), ("cqs", 128), ("ck", 128), ("cks", 128), ("cv", 128), ("co", 128),
          ("f1", DFF), ("f2", DFF), ("n1b", 2), ("n2b", 2), ("n3b", 2), ("f1b", FC)]
COL, _at = {}, 0
for _n, _w in _NAMES:
    COL[_n] = (_at, _w)
    _at += _w
WCOLS = _at


def key_tiles(n):
    return [(k, min(P, n - k)) for k in range(0, n, P)]


class Unit:

    def __init__(self, step, i, r):
        self.step, self.i, self.r = step, i, r

    def at(self, k=0):
        return self.step * self.i + (self.r + k)

    def turn(self, k=0):
        return self.i + (self.r + k) // self.step + 1

    def buf(self, n, k=0):
        return (self.r + k) % n


def wait(eng, sem, value):
    if isinstance(value, int) and value <= 0:
        return
    eng.wait_ge(sem, value)


def build_program(nc, T, out, stop=None, dump=None):
    top = ExitStack()
    sems = []

    def sem(name):
        s = top.enter_context(nc.semaphore(name))
        sems.append(s)
        return s

    def clear():
        if sems:
            nc.all_engine_barrier(sems_to_clear=range(sems[0].num, sems[-1].num + 1))

    def sb(st, name, shape, dt=F32):
        return st.enter_context(nc.sbuf_tensor(name, shape, dt))

    psum = top.enter_context(nc.psum_tensor("psum", [P, 8, 512], F32))

    k_ctx_d = nc.dram_tensor("k_ctx_parts", [B * H, 1 + ROWS, SC], BF16, kind="Internal").ap()
    k_self_d = nc.dram_tensor("k_self_parts", [B * H, 1 + ROWS, S], BF16, kind="Internal").ap()
    k_first_d = nc.dram_tensor("k_first_parts", [B * H, 1 + ROWS, S], BF16, kind="Internal").ap()
    q_d = nc.dram_tensor("q_parts", [B, P, SLOTS, S], BF16, kind="Internal").ap()

    x_sb = sb(top, "x_sb", [P, TILES, D])
    z_sb = sb(top, "z_sb", [P, TILES, D])
    xhat = sb(top, "xhat", [P, TILES, D])
    xnT = sb(top, "xnT", [P, NTOK])
    ident = sb(top, "ident", [P, P])
    ident_b = sb(top, "ident_b", [P, P], BF16)
    condT = sb(top, "condT", [P, B])
    vecs = sb(top, "vecs", [P, 12])
    stats = sb(top, "stats", [P, TILES + 6, 6])
    mv = sb(top, "mv", [P, TILES + 6, 2])
    rstd = sb(top, "rstd", [P, TILES + 6])
    nhalf = sb(top, "nhalf", [P, TILES + 6])
    scl = sb(top, "scl", [P, B])
    bia = sb(top, "bia", [P, B])
    ones_col = sb(top, "ones_col", [P, 1])
    ones_row = sb(top, "ones_row", [1, P])
    brow = sb(top, "brow", [1, 2 * D])

    loaded = sem("loaded")
    loaded2 = sem("loaded2")
    stat_done = sem("stat_done")
    aggr_done = sem("aggr_done")
    eps_added = sem("eps_added")
    rstd_done = sem("rstd_done")
    norm_done = sem("norm_done")
    transposed = sem("transposed")
    affine_done = sem("affine_done")
    mod_made = sem("mod_made")
    mod_ready = sem("mod_ready")
    chain = sem("chain")
    ring_loaded = [sem(f"ring_loaded{i}") for i in range(RING)]
    row_cleared = sem("row_cleared")
    v_staged = sem("v_staged")
    max_scores = sem("max_scores")
    max_read = sem("max_read")
    max_done = sem("max_done")
    max_row = sem("max_row")
    shift_ready = sem("shift_ready")
    scored = sem("scored")
    exp_done = sem("exp_done")
    pv_done = sem("pv_done")
    o_copied = sem("o_copied")
    o_turned = sem("o_turned")
    o_scaled = sem("o_scaled")
    rec_done = sem("rec_done")
    proj_made = sem("proj_made")
    proj_read = sem("proj_read")
    mixed = sem("mixed")
    summed = sem("summed")
    hi_done = sem("hi_done")
    rest_done = sem("rest_done")
    mid_done = sem("mid_done")
    lo_done = sem("lo_done")
    parts_out = [sem("parts_out0"), sem("parts_out1")]
    v_made = sem("v_made")
    v_read = sem("v_read")
    turned = sem("turned")
    turned_out = sem("turned_out")
    up_made = sem("up_made")
    act_done = sem("act_done")
    down_made = sem("down_made")
    down_read = sem("down_read")
    weights_in = [sem("weights_in0"), sem("weights_in1")]
    gate_made = sem("gate_made")
    gate_step = sem("gate_step")
    gate_exp = sem("gate_exp")
    stored = sem("stored")
    swept = sem("swept")
    sum_bc = sem("sum_bc")
    zeroed = sem("zeroed")

    with ExitStack() as st:
        mk = sb(st, "mk", [B * H, SC], U8)
        mb = sb(st, "mb", [B * H, SC], BF16)
        ms = sb(st, "ms", [B * H, S], U8)
        mbs = sb(st, "mbs", [B * H, 2, S], BF16)
        with nc.Block() as block:
            @block.sync
            def _(sp):
                sp.dma_start(mk[:, :], T["mask_ctx"]).then_inc(loaded, 16)
                sp.dma_start(ms[:, :], T["mask_x"]).then_inc(loaded, 16)
                sp.dma_start(x_sb[:, :, :], T["x"].rearrange("b (t p) d -> p (b t) d", p=P)).then_inc(loaded2, 16)
                sp.dma_start(ident[:, :], T["ident"]).then_inc(loaded2, 16)
                sp.dma_start(condT[:, :], T["condT"]).then_inc(loaded2, 16)
                sp.dma_start(vecs[:, :], T["vecs"]).then_inc(loaded2, 16)
                sp.wait_ge(chain, 3)
                sp.dma_start(k_ctx_d[:, 0, :], mb[:, :]).then_inc(stored, 16)
                sp.dma_start(k_self_d[:, 0, :], mbs[:, 0, :]).then_inc(stored, 16)
                sp.dma_start(k_first_d[:, 0, :], mbs[:, 1, :]).then_inc(stored, 16)
                sp.wait_ge(stored, 48)
                sp.wait_ge(loaded2, 64)

            @block.vector
            def _(dve):
                dve.memset(nhalf[:, :], -0.5)
                dve.memset(ones_col[:, :], 1.0)
                dve.memset(ones_row[:, :], 1.0)
                dve.wait_ge(loaded, 32)
                dve.tensor_scalar(mb[:, :], mk[:, :], MASKED, None, ALU.mult).then_inc(chain, 1)
                dve.tensor_scalar(mbs[:, 0, :], ms[:, :], MASKED, None, ALU.mult).then_inc(chain, 1)
                dve.memset(mbs[:, 1, :], 0.0).then_inc(chain, 1)
                dve.wait_ge(loaded2, 64)
                dve.tensor_copy(ident_b[:, :], ident[:, :])
        clear()

    def layer_norm(src, dst, passes=1, turn=None, modulate=None, affine=None):
        with nc.Block() as block:
            @block.vector
            def _(dve):
                for n in range(passes):
                    a = src if n == 0 else dst
                    wait(dve, norm_done, TILES * n)
                    for t in range(TILES):
                        dve.bn_stats(stats[:, t, :], a[:, t, :]).then_inc(stat_done, 1)
                    dve.wait_ge(stat_done, TILES * (n + 1))
                    for t in range(TILES):
                        dve.bn_aggr(mv[:, t, :], stats[:, t, :]).then_inc(aggr_done, 1)
                    dve.wait_ge(rstd_done, n + 1)
                    for t in range(TILES):
                        dve.tensor_scalar(dst[:, t, :], a[:, t, :], mv[:, t, 0:1], rstd[:, t:t + 1],
                                          ALU.subtract, ALU.mult).then_inc(norm_done, 1)
                if turn is None:
                    return
                if modulate is not None:
                    wb = modulate[1]
                    dve.wait_ge(mod_made, 1)
                    dve.tensor_scalar(scl[:, :], psum[:, 2, 0:B], wb[:, 0:1], 1.0, ALU.add, ALU.add).then_inc(mod_ready, 1)
                    dve.tensor_scalar(bia[:, :], psum[:, 2, B:2 * B], wb[:, 1:2], None, ALU.add).then_inc(mod_ready, 1)
                    dve.wait_ge(mod_ready, 2)
                for b in range(B):
                    s = scl[:, b:b + 1] if modulate is not None else affine[0](b)
                    o = bia[:, b:b + 1] if modulate is not None else affine[1](b)
                    dve.wait_ge(transposed, QT * (b + 1))
                    dve.tensor_scalar(turn[:, b * S:(b + 1) * S], psum[:, b % 2, 0:S], s, o,
                                      ALU.mult, ALU.add).then_inc(affine_done, 1)

            @block.gpsimd
            def _(pool):
                for n in range(passes):
                    pool.wait_ge(aggr_done, TILES * (n + 1))
                    pool.tensor_scalar(rstd[:, 0:TILES], mv[:, 0:TILES, 1], EPS, None, ALU.add).then_inc(eps_added, 1)
                    pool.wait_ge(eps_added, n + 1)
                    pool.tensor_tensor(rstd[:, 0:TILES], rstd[:, 0:TILES], nhalf[:, 0:TILES], ALU.pow).then_inc(rstd_done, 1)

            @block.tensor
            def _(pe):
                if turn is None:
                    return
                if modulate is not None:
                    w = modulate[0]
                    pe.matmul(psum[:, 2, 0:B], w[:, 0:P], condT[:, :], start=True, stop=True)
                    pe.matmul(psum[:, 2, B:2 * B], w[:, P:2 * P], condT[:, :], start=True, stop=True).then_inc(mod_made, 1)
                for t in range(TILES):
                    b, h = divmod(t, QT)
                    pe.wait_ge(norm_done, TILES * (passes - 1) + t + 1)
                    wait(pe, affine_done, b - 1)
                    pe.transpose(psum[:, b % 2, h * P:(h + 1) * P], dst[:, t, :], ident[:, :]).then_inc(transposed, 1)
        clear()

    def resampler():
        KTS = key_tiles(SC) + [(SC, P), (SC + P, P)]
        NK = SC + S
        KT = len(KTS)
        CT = len(key_tiles(SC))
        st = ExitStack()
        a_sb = sb(st, "a_sb", [P, H, P])
        b_sb = sb(st, "b_sb", [P, H, D])
        qp = sb(st, "qp", [P, UNITS, 2 * S])
        qhi = sb(st, "qhi", [P, UNITS, 2 * S], BF16)
        ones_f = sb(st, "ones_f", [P, P])
        ones_b = sb(st, "ones_b", [1, P], BF16)
        lnw = sb(st, "lnw", [P, 2, D])

        layer_norm(x_sb, xhat, passes=2, turn=None)

        with ExitStack() as s2:
            wq = sb(s2, "wq", [EA, H, D])
            wk = sb(s2, "wk", [EA, H, D])
            wv = sb(s2, "wv", [EA, H, D])
            wo = sb(s2, "wo", [EA, H, D])
            with nc.Block() as block:
                @block.sync
                def _(sp):
                    sp.dma_start(wq[:, :, :], T["Wq"]).then_inc(loaded, 16)
                    sp.dma_start(wk[:, :, :], T["Wk"]).then_inc(loaded, 16)
                    sp.dma_start(wv[:, :, :], T["Wv"]).then_inc(loaded, 16)
                    sp.dma_start(wo[:, :, :], T["Wo"]).then_inc(loaded, 16)
                    sp.dma_start(lnw[:, 0, :], T["ln1_w"].partition_broadcast(P)).then_inc(loaded2, 16)
                    sp.dma_start(lnw[:, 1, :], T["ln1_b"].partition_broadcast(P)).then_inc(loaded2, 16)
                    sp.wait_ge(loaded2, 32)

                @block.vector
                def _(dve):
                    dve.memset(ones_f[:, :], 1.0)
                    dve.memset(ones_b[:, :], 1.0)
                    dve.tensor_scalar(scl[:, :], condT[:, :], 1.0, vecs[:, 0:1], ALU.add, ALU.mult).then_inc(chain, 1)
                    dve.tensor_scalar(bia[:, :], condT[:, :], 1.0, vecs[:, 1:2], ALU.add, ALU.mult).then_inc(chain, 1)
                    dve.wait_ge(chain, 2)
                    dve.tensor_tensor(bia[:, :], bia[:, :], condT[:, :], ALU.add).then_inc(chain, 1)
                    dve.wait_ge(chain, 3)
                    for b in range(B):
                        dve.wait_ge(transposed, QT * (b + 1))
                        dve.tensor_scalar(xnT[:, b * S:(b + 1) * S], psum[:, b % 2, 0:S], scl[:, b:b + 1], bia[:, b:b + 1],
                                          ALU.mult, ALU.add).then_inc(affine_done, 1)
                    for h in range(H):
                        dve.wait_ge(proj_made, h + 1)
                        dve.tensor_copy(a_sb[:, h, :], psum[:, 2 + h % 2, 0:P]).then_inc(proj_read, 1)
                        dve.tensor_copy(b_sb[:, h, :], psum[:, 2 + h % 2, P:2 * P]).then_inc(proj_read, 1)
                    for h in range(H):
                        for c in range(2):
                            n = 2 * h + c
                            dve.wait_ge(up_made, n + 1)
                            dve.tensor_copy(qp[:, :, :].rearrange("p (b u) (h q) -> p b u h q", u=PAIRS, h=2)[:, 2 * c:2 * c + 2, h // 2, h % 2, :],
                                            psum[:, 4 + n % 2, :].rearrange("p (b q) -> p b q", b=2)).then_inc(down_made, 1)

                @block.scalar
                def _(act):
                    for h in range(H):
                        for c in range(2):
                            n = 2 * h + c
                            act.wait_ge(down_made, n + 1)
                            act.activation(qhi[:, :, :].rearrange("p (b u) (h q) -> p b u h q", u=PAIRS, h=2)[:, 2 * c:2 * c + 2, h // 2, h % 2, :],
                                           qp[:, :, :].rearrange("p (b u) (h q) -> p b u h q", u=PAIRS, h=2)[:, 2 * c:2 * c + 2, h // 2, h % 2, :], ACT.Copy)

                @block.tensor
                def _(pe):
                    for t in range(TILES):
                        b, h = divmod(t, QT)
                        wait(pe, affine_done, b - 1)
                        pe.transpose(psum[:, b % 2, h * P:(h + 1) * P], xhat[:, t, :], ident[:, :]).then_inc(transposed, 1)
                    pe.wait_ge(loaded, 64)
                    for h in range(H):
                        wait(pe, proj_read, 2 * (h - 1))
                        pe.matmul(psum[:, 2 + h % 2, 0:P], wq[:, h, :], wk[:, h, :], start=True, stop=True)
                        pe.matmul(psum[:, 2 + h % 2, P:2 * P], wv[:, h, :], wo[:, h, :], start=True, stop=True).then_inc(proj_made, 1)
                    pe.wait_ge(affine_done, B)
                    pe.wait_ge(proj_read, 2 * H)
                    for h in range(H):
                        for c in range(2):
                            n = 2 * h + c
                            wait(pe, down_made, n - 1)
                            pe.matmul(psum[:, 4 + n % 2, :], a_sb[:, h, :], xnT[:, c * 512:(c + 1) * 512], start=True, stop=True).then_inc(up_made, 1)
            clear()

        craw = sb(st, "craw", [P, CT, D])
        ck = sb(st, "ck", [P, KT, D])
        cT = sb(st, "cT", [P, NK])
        cTh = sb(st, "cTh", [P, NK], BF16)
        NP = 3
        probs = sb(st, "probs", [P, NP, 512])
        psumm = sb(st, "psumm", [P, 2, 512])
        mp = sb(st, "mp", [P, 2, 4, 2])
        nm = sb(st, "nm", [P, 2, 4], BF16)
        nrow = sb(st, "nrow", [1, 2, 512], BF16)
        yraw = sb(st, "yraw", [P, 512])
        rec = sb(st, "rec", [P, 512])
        yn = sb(st, "yn", [P, 512])
        acc = sb(st, "acc", [P, QT, D])
        tail = KTS[CT - 1][1]

        with nc.Fori(0, B) as b:
            with nc.Block() as block:
                @block.sync
                def _(sp):
                    sp.dma_start(craw[:, 0:CT - 1, :], T["ctx"][b, 0:(CT - 1) * P, :].rearrange("(t p) d -> p t d", p=P)).then_inc(loaded, 16)
                    sp.dma_start(craw[0:tail, CT - 1, :], T["ctx"][b, (CT - 1) * P:SC, :]).then_inc(loaded, 16)

                @block.vector
                def _(dve):
                    dve.tensor_copy(cT[:, SC:NK], xnT[:, bass.ds(b * S, S)]).then_inc(mixed, 1)
                    dve.memset(acc[:, :, :], 0.0)
                    dve.wait_ge(loaded, 32)
                    for t in range(CT):
                        n = KTS[t][1]
                        dve.bn_stats(stats[0:n, t, :], craw[0:n, t, :]).then_inc(stat_done, 1)
                    dve.wait_ge(stat_done, CT)
                    for t in range(CT):
                        n = KTS[t][1]
                        dve.bn_aggr(mv[0:n, t, :], stats[0:n, t, :]).then_inc(aggr_done, 1)
                    dve.wait_ge(rstd_done, 2)
                    for t in range(CT):
                        n = KTS[t][1]
                        dve.tensor_scalar(craw[0:n, t, :], craw[0:n, t, :], mv[0:n, t, 0:1], rstd[0:n, t:t + 1],
                                          ALU.subtract, ALU.mult).then_inc(norm_done, 1)
                    for t in range(CT):
                        n = KTS[t][1]
                        dve.wait_ge(norm_done, t + 1)
                        dve.tensor_tensor(ck[0:n, t, :], craw[0:n, t, :], lnw[0:n, 0, :], ALU.mult).then_inc(chain, 1)
                    for t in range(CT):
                        n = KTS[t][1]
                        dve.wait_ge(chain, t + 1)
                        dve.tensor_tensor(ck[0:n, t, :], ck[0:n, t, :], lnw[0:n, 1, :], ALU.add).then_inc(affine_done, 1)
                    for t in range(CT, KT):
                        dve.wait_ge(transposed, t - CT + 1)
                        dve.tensor_copy(ck[:, t, :], psum[:, t - CT, 0:P]).then_inc(mixed, 1)
                    for t in range(CT):
                        k, n = KTS[t]
                        dve.wait_ge(turned, t + 1)
                        dve.tensor_copy(cT[:, k:k + n], psum[:, 2 + t % 2, 0:n]).then_inc(turned_out, 1)

                @block.gpsimd
                def _(pool):
                    pool.wait_ge(aggr_done, CT)
                    for lo, hi, n in ((0, CT - 1, P), (CT - 1, CT, tail)):
                        pool.tensor_scalar(rstd[0:n, lo:hi], mv[0:n, lo:hi, 1], EPS, None, ALU.add).then_inc(eps_added, 1)
                    pool.wait_ge(eps_added, 2)
                    for lo, hi, n in ((0, CT - 1, P), (CT - 1, CT, tail)):
                        pool.tensor_tensor(rstd[0:n, lo:hi], rstd[0:n, lo:hi], nhalf[0:n, lo:hi], ALU.pow).then_inc(rstd_done, 1)

                @block.scalar
                def _(act):
                    act.wait_ge(mixed, 1)
                    act.activation(cTh[:, SC:NK], cT[:, SC:NK], ACT.Copy)
                    for t in range(CT):
                        k, n = KTS[t]
                        act.wait_ge(turned_out, t + 1)
                        act.activation(cTh[:, k:k + n], cT[:, k:k + n], ACT.Copy)

                @block.tensor
                def _(pe):
                    pe.wait_ge(mixed, 1)
                    for t in range(CT, KT):
                        k, n = KTS[t]
                        pe.transpose(psum[:, t - CT, 0:P], cT[:, k:k + n], ident[:, :]).then_inc(transposed, 1)
                    for t in range(CT):
                        n = KTS[t][1]
                        pe.wait_ge(affine_done, t + 1)
                        wait(pe, turned_out, t - 1)
                        pe.transpose(psum[:, 2 + t % 2, 0:n], ck[0:n, t, :], ident[0:n, 0:n]).then_inc(turned, 1)
            clear()

            NG = 8
            WIDE = 1024
            STEP = 2
            SUM_AT, PROJ_AT, MAX_AT = 2, 6, KT - 2
            group_at = [1 + g for g in range(NG)]

            def loop(eng, body, prologue, epilogue):
                prologue()
                for r in range(STEP):
                    body(Unit(STEP, 0, r), r == 0, False)
                with eng.Fori(1, PAIRS // STEP - 1) as i:
                    for r in range(STEP):
                        body(Unit(STEP, i, r), False, False)
                for r in range(STEP):
                    body(Unit(STEP, PAIRS // STEP - 1, r), False, r == STEP - 1)
                epilogue(Unit(STEP, PAIRS // STEP - 1, STEP - 1))

            with nc.Block() as block:
                @block.tensor
                def _(pe):
                    def group(u, k, g):
                        hq, c = divmod(g, 2)
                        lo, hi = c * WIDE, min(NK, (c + 1) * WIDE)
                        wait(pe, max_read, NG * u.at(k) + g - 1)
                        for o in range(lo, hi, 512):
                            m = min(512, hi - o)
                            mm = pe.matmul(psum[:, 2 * (g % 2) + (o - lo) // 512, 0:m],
                                           qhi[:, PAIRS * b + u.at(k), hq * P:(hq + 1) * P],
                                           cTh[:, o:o + m], start=True, stop=True)
                        mm.then_inc(max_scores, 1)

                    def turn_max(u, k):
                        pe.wait_ge(max_done, u.at(k) + 1)
                        wait(pe, proj_read, u.at(k) - 1)
                        for hq in range(4):
                            mm = pe.matmul(psum[0:1, 7, hq * P:(hq + 1) * P], nm[:, u.buf(2, k), hq:hq + 1], ident_b[:, :],
                                           start=True, stop=True)
                        mm.then_inc(max_row, 1)

                    def broadcast_sum(u, k):
                        pe.wait_ge(summed, KT * (u.at(k) + 1))
                        wait(pe, proj_read, u.at(k))
                        pe.matmul(psum[:, 7, :], ones_f[:, :], psumm[:, u.buf(2, k), :], start=True, stop=True).then_inc(sum_bc, 1)

                    def project(u, k):
                        pe.wait_ge(o_scaled, u.at(k) + 1)
                        for q in range(QT):
                            for h in range(2):
                                mm = pe.matmul(psum[:, 7, q * D:(q + 1) * D], yn[:, h * S + q * P:h * S + (q + 1) * P],
                                               b_sb[:, 2 * u.at(k) + h, :], start=(h == 0), stop=(h == 1))
                        mm.then_inc(proj_made, 1)

                    def prologue():
                        u = Unit(STEP, 0, 0)
                        for g in range(NG):
                            group(u, 0, g)
                        turn_max(u, 0)

                    def body(u, first, last):
                        pe.wait_ge(shift_ready, u.at() + 1)
                        for s in range(KT + 1):
                            m = KT * u.r + s
                            if s < KT:
                                k, n = KTS[s]
                                wait(pe, exp_done, KT * u.at() + s - 1)
                                pe.matmul(psum[0:n, 4 + m % 2, :], cT[:, k:k + n], qp[:, PAIRS * b + u.at(), :], start=True, stop=False)
                                pe.matmul(psum[0:n, 4 + m % 2, :], ones_b[0:1, 0:n], nrow[0:1, u.buf(2), :],
                                          start=False, stop=True).then_inc(scored, 1)
                            if not last:
                                for g in range(NG):
                                    if group_at[g] == s:
                                        group(u, 1, g)
                            if s >= 1:
                                k, n = KTS[s - 1]
                                pe.wait_ge(exp_done, KT * u.at() + s)
                                if s == 1:
                                    wait(pe, o_copied, u.at())
                                pe.matmul(psum[:, 6, :], ck[0:n, s - 1, :], probs[0:n, (m - 1) % NP, :],
                                          start=(s == 1), stop=(s == KT)).then_inc(pv_done, 1)
                            if s == SUM_AT and not first:
                                broadcast_sum(u, -1)
                            if s == PROJ_AT and not first:
                                project(u, -1)
                            if s == MAX_AT and not last:
                                turn_max(u, 1)

                    def epilogue(u):
                        broadcast_sum(u, 0)
                        project(u, 0)

                    loop(pe, body, prologue, epilogue)

                @block.scalar
                def _(act):
                    def row(u, k):
                        act.wait_ge(max_row, u.at(k) + 1)
                        wait(act, scored, KT * u.at(k - 1))
                        act.activation(nrow[0:1, u.buf(2, k), :], psum[0:1, 7, :], ACT.Copy).then_inc(shift_ready, 1)

                    def copy_o(u, k):
                        act.wait_ge(pv_done, KT * (u.at(k) + 1))
                        wait(act, o_scaled, u.at(k))
                        act.activation(yraw[:, :], psum[:, 6, :], ACT.Copy).then_inc(o_copied, 1)

                    def body(u, first, last):
                        if not first:
                            copy_o(u, -1)
                        for s in range(KT):
                            m = KT * u.r + s
                            if s == MAX_AT + 1 and not last:
                                row(u, 1)
                            n = KTS[s][1]
                            act.wait_ge(scored, KT * u.at() + s + 1)
                            wait(act, pv_done, KT * u.at() + s - NP + 1)
                            wait(act, summed, KT * u.at() + s - NP + 1)
                            act.activation(probs[0:n, m % NP, :], psum[0:n, 4 + m % 2, :], ACT.Exp, scale=EA ** -0.5).then_inc(exp_done, 1)

                    loop(act, body, lambda: row(Unit(STEP, 0, 0), 0), lambda u: copy_o(u, 0))

                @block.vector
                def _(dve):
                    def group(u, k, g):
                        hq, c = divmod(g, 2)
                        m = min(NK, (c + 1) * WIDE) - c * WIDE
                        dve.wait_ge(max_scores, NG * u.at(k) + g + 1)
                        src = psum[:, 2 * (g % 2):2 * (g % 2) + 2, :].rearrange("p a n -> p (a n)")[:, 0:m]
                        dve.tensor_reduce(mp[:, u.buf(2, k), hq, c:c + 1], src, op=ALU.max, axis=AX.X).then_inc(max_read, 1)

                    def merge(u, k):
                        dve.wait_ge(max_read, NG * (u.at(k) + 1))
                        wait(dve, max_row, u.at(k) - 1)
                        dve.tensor_reduce(nm[:, u.buf(2, k), :], mp[:, u.buf(2, k), :, :], op=ALU.max, axis=AX.X,
                                          negate=True).then_inc(max_done, 1)

                    def scale(u, k):
                        dve.wait_ge(sum_bc, u.at(k) + 1)
                        dve.reciprocal(rec[:, :], psum[:, 7, :]).then_inc(rec_done, 1)
                        dve.wait_ge(rec_done, u.at(k) + 1)
                        dve.wait_ge(o_copied, u.at(k) + 1)
                        wait(dve, proj_made, u.at(k))
                        dve.tensor_tensor(yn[:, :], yraw[:, :], rec[:, :], ALU.mult).then_inc(o_scaled, 1)

                    def add(u, k):
                        dve.wait_ge(proj_made, u.at(k) + 1)
                        dve.tensor_tensor(acc[:, :, :], acc[:, :, :], psum[:, 7, 0:QT * D].rearrange("p (t d) -> p t d", t=QT),
                                          ALU.add).then_inc(proj_read, 1)

                    def prologue():
                        u = Unit(STEP, 0, 0)
                        for g in range(NG):
                            group(u, 0, g)
                        merge(u, 0)

                    def body(u, first, last):
                        for g in range(NG):
                            if not last:
                                group(u, 1, g)
                            if g == 1 and not first:
                                scale(u, -1)
                            if g == 5 and not first:
                                add(u, -1)
                        if not last:
                            merge(u, 1)

                    def epilogue(u):
                        scale(u, 0)
                        add(u, 0)
                        dve.wait_ge(proj_read, PAIRS)
                        dve.tensor_tensor(x_sb[:, bass.ds(QT * b, QT), :], x_sb[:, bass.ds(QT * b, QT), :], acc[:, :, :], ALU.add)

                    loop(dve, body, prologue, epilogue)

                @block.gpsimd
                def _(pool):
                    def body(u, first, last):
                        for s in range(KT):
                            m = KT * u.r + s
                            if s == 0:
                                continue
                            n = KTS[s][1]
                            pool.wait_ge(exp_done, KT * u.at() + s + 1)
                            if s == 1:
                                wait(pool, sum_bc, u.at() - 1)
                                pool.tensor_tensor(psumm[:, u.buf(2), :], probs[:, (m - 1) % NP, :], probs[:, m % NP, :],
                                                   ALU.add).then_inc(summed, 2)
                            else:
                                pool.wait_ge(summed, KT * u.at() + s)
                                pool.tensor_tensor(psumm[0:n, u.buf(2), :], psumm[0:n, u.buf(2), :], probs[0:n, m % NP, :],
                                                   ALU.add).then_inc(summed, 1)

                    loop(pool, body, lambda: None, lambda u: None)
            clear()
        st.close()

    def make_operands(st, jobs, vjobs, par):
        NJ, NV = len(jobs), len(vjobs)
        mixA, mixB, tot, rest, hi, mid, lo = par
        parts = (hi, mid, lo)
        with nc.Block() as block:
            @block.tensor
            def _(pe):
                vi = 0
                for j, job in enumerate(jobs):
                    n = job["n"]
                    wait(pe, mixed, 2 * (j - 1))
                    mm = pe.matmul(psum[:, 2 * (j % 2), 0:n], job["w"], job["rhs"], start=True, stop=True)
                    if job["ws"] is not None:
                        mm = pe.matmul(psum[:, 2 * (j % 2) + 1, 0:n], job["ws"], job["rhs"], start=True, stop=True)
                    mm.then_inc(up_made, 1)
                    while vi < NV and vi * NJ < (j + 1) * NV:
                        lhsT, rhs, n, dst, bias = vjobs[vi]
                        wait(pe, v_read, vi - 1)
                        mm = pe.matmul(psum[0:n, 4 + vi % 2, 0:D], lhsT, rhs, start=True, stop=bias is None)
                        if bias is not None:
                            mm = pe.matmul(psum[0:n, 4 + vi % 2, 0:D], ones_row[0:1, 0:n], bias, start=False, stop=True)
                        mm.then_inc(v_made, 1)
                        vi += 1

            @block.vector
            def _(dve):
                def remainder(j):
                    n = jobs[j]["n"]
                    dve.wait_ge(hi_done, j + 1)
                    wait(dve, lo_done, j - 1)
                    dve.tensor_tensor(rest[:, j % 2, 0:n], tot[:, j % 2, 0:n], hi[:, j % 2, 0:n], ALU.subtract).then_inc(rest_done, 1)

                for j, job in enumerate(jobs):
                    n = job["n"]
                    dve.wait_ge(up_made, j + 1)
                    wait(dve, summed, j - 1)
                    if job["ws"] is None:
                        dve.tensor_scalar(mixA[:, j % 2, 0:n], psum[:, 2 * (j % 2), 0:n], job["bias"], None, ALU.add).then_inc(mixed, 2)
                    else:
                        dve.tensor_tensor(mixA[:, j % 2, 0:n], psum[:, 2 * (j % 2), 0:n], job["cos"], ALU.mult).then_inc(mixed, 1)
                        dve.tensor_tensor(mixB[:, j % 2, 0:n], psum[:, 2 * (j % 2) + 1, 0:n], job["sin"], ALU.mult).then_inc(mixed, 1)
                    if j >= 1:
                        remainder(j - 1)
                remainder(NJ - 1)

            @block.gpsimd
            def _(pool):
                def last_part(j):
                    n = jobs[j]["n"]
                    pool.wait_ge(mid_done, j + 1)
                    wait(pool, parts_out[j % 2], 16 * SLOTS * (j // 2))
                    pool.tensor_tensor(lo[:, j % 2, 0:n], rest[:, j % 2, 0:n], mid[:, j % 2, 0:n], ALU.subtract).then_inc(lo_done, 1)

                for j, job in enumerate(jobs):
                    n = job["n"]
                    pool.wait_ge(mixed, 2 * (j + 1))
                    wait(pool, rest_done, j - 1)
                    if job["ws"] is None:
                        pool.tensor_copy(tot[:, j % 2, 0:n], mixA[:, j % 2, 0:n]).then_inc(summed, 1)
                    else:
                        pool.tensor_tensor(tot[:, j % 2, 0:n], mixA[:, j % 2, 0:n], mixB[:, j % 2, 0:n], ALU.add).then_inc(summed, 1)
                    if j >= 1:
                        last_part(j - 1)
                last_part(NJ - 1)

            @block.scalar
            def _(act):
                def middle(j):
                    n = jobs[j]["n"]
                    act.wait_ge(rest_done, j + 1)
                    wait(act, lo_done, j - 1)
                    act.activation(mid[:, j % 2, 0:n], rest[:, j % 2, 0:n], ACT.Copy).then_inc(mid_done, 1)

                vi = 0
                for j, job in enumerate(jobs):
                    n = job["n"]
                    act.wait_ge(summed, j + 1)
                    wait(act, rest_done, j - 1)
                    wait(act, parts_out[j % 2], 16 * SLOTS * (j // 2))
                    act.activation(hi[:, j % 2, 0:n], tot[:, j % 2, 0:n], ACT.Copy).then_inc(hi_done, 1)
                    if j >= 1:
                        middle(j - 1)
                    while vi < NV and vi * NJ < (j + 1) * NV:
                        _, _, n, dst, _ = vjobs[vi]
                        act.wait_ge(v_made, vi + 1)
                        act.activation(dst, psum[0:n, 4 + vi % 2, 0:D].rearrange("k (u h d) -> k u h d", u=PAIRS, h=2), ACT.Copy).then_inc(v_read, 1)
                        vi += 1
                middle(NJ - 1)

            @block.sync
            def _(sp):
                for j, job in enumerate(jobs):
                    n = job["n"]
                    for part, done in enumerate((hi_done, mid_done, lo_done)):
                        sp.wait_ge(done, j + 1)
                        for slot in range(SLOTS):
                            if job["parts"][slot] == part:
                                sp.dma_start(job["dst"](slot), parts[part][:, j % 2, 0:n]).then_inc(parts_out[j % 2], 16)
                sp.wait_ge(parts_out[0], 16 * SLOTS * ((NJ + 1) // 2))
                sp.wait_ge(parts_out[1], 16 * SLOTS * (NJ // 2))
        clear()

    def key_rows(dram, b, slot, lo, hi):
        return dram[b * H:(b + 1) * H, 1 + slot:1 + ROWS:SLOTS, lo:hi]

    def unit_loop(eng, body, prologue, epilogue):
        last = UNITS // RING - 1
        prologue()
        for r in range(RING):
            body(Unit(RING, 0, r), lambda k, n=r: 0 <= n + k)
        with eng.Fori(1, last) as i:
            for r in range(RING):
                body(Unit(RING, i, r), lambda k: True)
        for r in range(RING):
            body(Unit(RING, last, r), lambda k, n=RING * last + r: n + k < UNITS)
        epilogue(Unit(RING, last, RING - 1))

    def attention(bufs, NK, k_dram, values, o_tok):
        kst, qst, vst, probs, mp, nm, oT, rec, sel = bufs
        KTS = key_tiles(NK)
        KT = len(KTS)
        long = KT > 2
        if long:
            CHUNKS = 4
            cut = [NK * c // CHUNKS for c in range(CHUNKS + 1)]
            groups = [(hq, c) for hq in range(4) for c in range(CHUNKS)]
        else:
            groups = [0, 1]
        NG = len(groups)
        MB = 4 if long else 2
        SB = 6 - MB
        max_slots = [[] for _ in range(KT)]
        pv_slots = [[] for _ in range(KT)]
        if long:
            EARLY = 3
            for g in range(NG):
                at = g * KT // NG - EARLY
                max_slots[at % KT].append((1 if at >= 0 else 2, g))
            for t in range(KT):
                at = max(t + 2, 3)
                pv_slots[at % KT].append((-(at // KT), t))
            TURN_AT, MAX_AT, COPY_AFTER, STAGE_AT = 4, KT - 2, 1, 3
        else:
            max_slots[1] = [(2, 0), (2, 1)]
            pv_slots[1] = [(-1, 0), (-1, 1)]
        k_units = k_dram
        q_units = q_d.rearrange("b (h d) s n -> (b h) (d s) n", h=H)

        with nc.Block() as block:
            @block.sync
            def _(sp):
                def load(u, k):
                    wait(sp, scored, KT * u.at(k - RING + 1))
                    r = u.buf(RING, k)
                    for h in range(2):
                        lo = 64 * h + R0
                        sp.dma_start(kst[lo - 1:lo + ROWS, r, 0:NK], k_units[2 * u.at(k) + h]).then_inc(ring_loaded[r], 16)
                        sp.dma_start(qst[lo:lo + ROWS, r, h * S:(h + 1) * S], q_units[2 * u.at(k) + h]).then_inc(ring_loaded[r], 16)

                def prologue():
                    for k in range(RING - 1):
                        load(Unit(RING, 0, 0), k)

                def body(u, there):
                    if there(RING - 1):
                        load(u, RING - 1)

                unit_loop(sp, body, prologue, lambda u: None)

            @block.tensor
            def _(pe):
                def group(u, k, g):
                    r = u.buf(RING, k)
                    if g == 0:
                        pe.wait_ge(ring_loaded[r], 16 * 4 * u.turn(k))
                        pe.wait_ge(row_cleared, 2 * u.at(k) + 2)
                    wait(pe, max_read, NG * u.at(k) + g - MB + 1)
                    if long:
                        hq, c = groups[g]
                        mm = pe.matmul(psum[:, g % MB, 0:cut[c + 1] - cut[c]], qst[:, r, hq * P:(hq + 1) * P],
                                       kst[:, r, cut[c]:cut[c + 1]], start=True, stop=True)
                    else:
                        for q in range(QT):
                            hq = QT * g + q
                            mm = pe.matmul(psum[:, g, q * S:(q + 1) * S], qst[:, r, hq * P:(hq + 1) * P],
                                           kst[:, r, 0:NK], start=True, stop=True)
                    mm.then_inc(max_scores, 1)

                def turn_max(u, k):
                    pe.wait_ge(max_done, u.at(k) + 1)
                    wait(pe, o_scaled, u.at(k - 1) if long else u.at(k - 3))
                    for q in range(QT):
                        mm = pe.matmul(psum[0:65, 7, q * P:(q + 1) * P], nm[:, u.buf(2, k), q, :], ident_b[:, :],
                                       start=True, stop=True)
                    mm.then_inc(max_row, 1)

                def score(u, s):
                    k, n = KTS[s]
                    m = KT * u.r + s
                    wait(pe, exp_done, KT * u.at() + s - SB + 1)
                    pe.matmul(psum[0:n, MB + m % SB, :], kst[:, u.buf(RING), k:k + n], qst[:, u.buf(RING), :],
                              start=True, stop=True).then_inc(scored, 1)

                def product(u, k, t):
                    n = KTS[t][1]
                    if t == 0:
                        pe.wait_ge(v_staged, u.at(k) + 1)
                        wait(pe, o_copied, u.at(k))
                    pe.wait_ge(exp_done, KT * u.at(k) + t + 1)
                    for h in range(2):
                        c = 2 * (t % 2) + h
                        mm = pe.matmul(psum[VW * c:VW * (c + 1), 6, 0:S], vst[0:n, u.buf(2, k), t, h, :],
                                       probs[0:n, (KT * (u.r + k) + t) % 4, h * S:(h + 1) * S], start=(t < 2), stop=(t >= KT - 2))
                    mm.then_inc(pv_done, 1)

                def turn_o(u, k):
                    pe.wait_ge(o_copied, u.at(k) + 1)
                    wait(pe, o_scaled, u.at(k))
                    ahead = u.at(k + (1 if long else 3))
                    if not isinstance(ahead, int) or ahead < UNITS:
                        pe.wait_ge(shift_ready, 2 * ahead + 2)
                    for q in range(QT):
                        mm = pe.matmul(psum[:, 7, S + 18 * q:S + 18 * (q + 1)], oT[:, u.buf(2, k), q * P:(q + 1) * P], sel[:, :],
                                       start=True, stop=True)
                    mm.then_inc(o_turned, 1)

                def prologue():
                    u = Unit(RING, 0, 0)
                    for g in range(NG):
                        group(u, 0, g)
                    turn_max(u, 0)
                    if long:
                        for s in range(KT):
                            for k, g in max_slots[s]:
                                if k == 2:
                                    group(u, 1, g)
                    else:
                        for g in range(NG):
                            group(u, 1, g)

                def body(u, there):
                    pe.wait_ge(shift_ready, 2 * u.at() + 2)
                    for s in range(KT):
                        score(u, s)
                        if not long and s == 1 and there(1):
                            turn_max(u, 1)
                        for k, g in max_slots[s][0:1] if long else max_slots[s]:
                            if there(k):
                                group(u, k, g)
                        for k, t in pv_slots[s]:
                            if there(k):
                                product(u, k, t)
                        for k, g in max_slots[s][1:] if long else ():
                            if there(k):
                                group(u, k, g)
                        if long and s == TURN_AT and there(-1):
                            turn_o(u, -1)
                        if long and s == MAX_AT and there(1):
                            turn_max(u, 1)
                    if not long and there(-2):
                        turn_o(u, -2)

                def epilogue(u):
                    for s in range(KT):
                        for k, t in pv_slots[s]:
                            if k == -1:
                                product(u, 0, t)
                    if not long:
                        turn_o(u, -1)
                    turn_o(u, 0)

                unit_loop(pe, body, prologue, epilogue)

            @block.scalar
            def _(act):
                def rows(u, k):
                    act.wait_ge(max_row, u.at(k) + 1)
                    r = u.buf(RING, k)
                    act.activation(qst[0:1, r, 0:S], psum[0:1, 7, 0:S], ACT.Copy).then_inc(shift_ready, 1)
                    act.activation(qst[64:65, r, S:2 * S], psum[64:65, 7, 0:S], ACT.Copy).then_inc(shift_ready, 1)

                def copy_o(u, k):
                    act.wait_ge(pv_done, KT * (u.at(k) + 1))
                    wait(act, o_turned, u.at(k) - 1)
                    act.activation(oT[:, u.buf(2, k), :], psum[:, 6, 0:S], ACT.Copy).then_inc(o_copied, 1)

                def body(u, there):
                    for s in range(KT):
                        m = KT * u.r + s
                        if long and s == MAX_AT + 1 and there(1):
                            rows(u, 1)
                        n = KTS[s][1]
                        act.wait_ge(scored, KT * u.at() + s + 1)
                        wait(act, pv_done, KT * u.at() + s - 3)
                        act.activation(probs[0:n, m % 4, :], psum[0:n, MB + m % SB, :], ACT.Exp, scale=HD ** -0.5).then_inc(exp_done, 1)
                        if long and s == COPY_AFTER and there(-1):
                            copy_o(u, -1)
                    if not long:
                        if there(1):
                            rows(u, 1)
                        if there(-1):
                            copy_o(u, -1)

                unit_loop(act, body, lambda: rows(Unit(RING, 0, 0), 0), lambda u: copy_o(u, 0))

            @block.vector
            def _(dve):
                def group(u, k, g):
                    dve.wait_ge(max_scores, NG * u.at(k) + g + 1)
                    if long:
                        hq, c = groups[g]
                        dve.tensor_reduce(mp[:, u.buf(2, k), hq, c:c + 1], psum[:, g % MB, 0:cut[c + 1] - cut[c]],
                                          op=ALU.max, axis=AX.X).then_inc(max_read, 1)
                        if g == NG - 1:
                            dve.wait_ge(max_read, NG * (u.at(k) + 1))
                            wait(dve, max_row, u.at(k) - 1)
                            dve.tensor_reduce(nm[:, u.buf(2, k), :, 0:65:64].rearrange("p q h -> p h q"),
                                              mp[:, u.buf(2, k), :, :].rearrange("p (h q) c -> p h q c", h=2), op=ALU.max, axis=AX.X,
                                              negate=True).then_inc(max_done, 1)
                    else:
                        wait(dve, max_row, u.at(k) - 1)
                        ins = dve.tensor_reduce(nm[:, u.buf(2, k), :, 64 * g:64 * g + 1].rearrange("p q h -> p (q h)"),
                                                psum[:, g, :].rearrange("p (q n) -> p q n", q=QT),
                                                op=ALU.max, axis=AX.X, negate=True)
                        ins.then_inc(max_read, 1)
                        if g == NG - 1:
                            dve.wait_ge(max_read, NG * (u.at(k) + 1))
                            dve.sem_inc(max_done, 1)

                def normalise(u, k):
                    dve.wait_ge(o_turned, u.at(k) + 1)
                    o = psum[:, 7, S:S + 36].rearrange("p (g e) -> p g e", g=4)
                    dve.reciprocal(rec[:, u.buf(2, k), :], o[:, :, HD]).then_inc(rec_done, 1)
                    dve.wait_ge(rec_done, u.at(k) + 1)
                    dve.tensor_tensor(o_tok[:, u.at(k), :, :], o[:, :, 0:HD],
                                      rec[:, u.buf(2, k), :].unsqueeze(2).to_broadcast([P, 4, HD]), ALU.mult).then_inc(o_scaled, 1)

                def clear_row(u, k):
                    wait(dve, scored, KT * u.at(k - RING + 1))
                    r = u.buf(RING, k)
                    dve.memset(qst[0:1, r, 0:S].bitcast(U32), 0).then_inc(row_cleared, 1)
                    dve.memset(qst[64:65, r, S:2 * S].bitcast(U32), 0).then_inc(row_cleared, 1)

                def prologue():
                    u = Unit(RING, 0, 0)
                    for k in range(RING - 1):
                        clear_row(u, k)
                    for g in range(NG):
                        group(u, 0, g)
                    if long:
                        for s in range(KT):
                            for k, g in max_slots[s]:
                                if k == 2:
                                    group(u, 1, g)
                    else:
                        for g in range(NG):
                            group(u, 1, g)

                def body(u, there):
                    for s in range(KT):
                        for k, g in max_slots[s]:
                            if there(k):
                                group(u, k, g)
                        if long and s == TURN_AT + 2 and there(-1):
                            normalise(u, -1)
                        if long and s == TURN_AT + 4 and there(3):
                            clear_row(u, 3)
                    if not long:
                        if there(-2):
                            normalise(u, -2)
                        if there(3):
                            clear_row(u, 3)

                def epilogue(u):
                    if not long:
                        normalise(u, -1)
                    normalise(u, 0)

                unit_loop(dve, body, prologue, epilogue)

            @block.gpsimd
            def _(pool):
                def stage(u, k):
                    wait(pool, pv_done, KT * u.at(k - 1))
                    v = values[:, u.at(k), :, :, :]
                    pool.tensor_tensor(vst[:, u.buf(2, k), 0:KT, :, 0:HD + 1], v,
                                       ones_col[:, :].to_broadcast([P, KT * 2 * (HD + 1)]).rearrange("p (t h e) -> p t h e", t=KT, h=2),
                                       ALU.mult).then_inc(v_staged, 1)

                def body(u, there):
                    if there(1):
                        stage(u, 1)

                unit_loop(pool, body, lambda: stage(Unit(RING, 0, 0), 0), lambda u: None)
        clear()

    def project_out(o_tok, oTT, w, bias, z):
        with nc.Block() as block:
            @block.tensor
            def _(pe):
                for t in range(TILES):
                    pe.wait_ge(swept, t + 1)
                    pe.transpose(psum[:, t // 4, (t % 4) * P:(t % 4 + 1) * P], xhat[:, t, :], ident[:, :]).then_inc(turned, 1)
                for t in range(TILES):
                    k = t // 4
                    pe.wait_ge(turned_out, k + 1)
                    o = psum[:, 2 + k, (t % 4) * D:(t % 4 + 1) * D]
                    mm = pe.matmul(o, oTT[:, t * P:(t + 1) * P], w, start=True, stop=bias is None)
                    if bias is not None:
                        mm = pe.matmul(o, ones_row[0:1, :], bias, start=False, stop=True)
                    mm.then_inc(proj_made, 1)

            @block.gpsimd
            def _(pool):
                for t in range(TILES):
                    b, q = divmod(t, QT)
                    pool.tensor_copy(xhat[:, t, :].rearrange("p (u h d) -> p u h d", u=PAIRS, h=2),
                                     o_tok[:, b * PAIRS:(b + 1) * PAIRS, 2 * q:2 * q + 2, :]).then_inc(swept, 1)

            @block.scalar
            def _(act):
                for k in range(2):
                    act.wait_ge(turned, 4 * (k + 1))
                    act.activation(oTT[:, k * 512:(k + 1) * 512], psum[:, k, :], ACT.Copy).then_inc(turned_out, 1)

            @block.vector
            def _(dve):
                for k in range(2):
                    dve.wait_ge(proj_made, 4 * (k + 1))
                    dve.tensor_tensor(z[:, 4 * k:4 * k + 4, :], z[:, 4 * k:4 * k + 4, :],
                                      psum[:, 2 + k, :].rearrange("p (t d) -> p t d", t=4), ALU.add)
        clear()

    def feed_forward(w1, b1, w2, b2, hT, z):
        with nc.Block() as block:
            @block.tensor
            def _(pe):
                for k in range(2):
                    for c in range(FC):
                        n = FC * k + c
                        wait(pe, act_done, n - 1)
                        pe.matmul(psum[:, n % 2, :], w1[:, c * P:(c + 1) * P], xnT[:, k * 512:(k + 1) * 512],
                                  start=True, stop=True).then_inc(up_made, 1)
                for t in range(TILES):
                    k = t // 4
                    pe.wait_ge(act_done, FC * (k + 1))
                    o = psum[:, 2 + k, (t % 4) * D:(t % 4 + 1) * D]
                    for c in range(FC):
                        pe.matmul(o, hT[:, c, t * P:(t + 1) * P], w2[:, c * D:(c + 1) * D], start=(c == 0), stop=False)
                    pe.matmul(o, ones_row[0:1, :], b2, start=False, stop=True).then_inc(down_made, 1)

            @block.scalar
            def _(act):
                for k in range(2):
                    for c in range(FC):
                        act.wait_ge(up_made, FC * k + c + 1)
                        act.activation(hT[:, c, k * 512:(k + 1) * 512], psum[:, (FC * k + c) % 2, :], ACT.Gelu,
                                       bias=b1[:, c:c + 1]).then_inc(act_done, 1)

            @block.vector
            def _(dve):
                for k in range(2):
                    dve.wait_ge(down_made, 4 * (k + 1))
                    dve.tensor_tensor(z[:, 4 * k:4 * k + 4, :], z[:, 4 * k:4 * k + 4, :],
                                      psum[:, 2 + k, :].rearrange("p (t d) -> p t d", t=4), ALU.add)
        clear()

    def experts(gate_w, gate_b, w1_d, b1_d, w2_d, b2_d, func, top, z, tag):
        with ExitStack() as st:
            hT = sb(st, tag + "_moe_h", [P, FC, NTOK])
            w1 = sb(st, tag + "_moe_w1", [P, 2, DFF])
            w2 = sb(st, tag + "_moe_w2", [P, 2, DFF])
            b1 = sb(st, tag + "_moe_b1", [P, 2, FC])
            b2 = sb(st, tag + "_moe_b2", [1, 2, D])
            gw = sb(st, tag + "_gate_w", [P, E])
            gb = sb(st, tag + "_gate_b", [1, E])
            iota = sb(st, tag + "_iota", [P, E])
            logit = sb(st, tag + "_logit", [P, TILES, E])
            best = sb(st, tag + "_best", [P, TILES, 8])
            besti = sb(st, tag + "_besti", [P, TILES, 8], U32)
            bestf = sb(st, tag + "_bestf", [P, TILES, 8])
            g1 = sb(st, tag + "_g1", [P, TILES, 2])
            we = sb(st, tag + "_we", [P, TILES, E])
            tmp = sb(st, tag + "_moe_tmp", [P, TILES, E])
            wcol = sb(st, tag + "_wcol", [P, 2, TILES])
            with nc.Block() as block:
                @block.sync
                def _(sp):
                    sp.dma_start(gw[:, :], gate_w).then_inc(loaded, 16)
                    sp.dma_start(iota[:, :], T["iota"]).then_inc(loaded, 16)
                    if gate_b is not None:
                        sp.dma_start(gb[:, :], gate_b).then_inc(loaded, 16)

                @block.tensor
                def _(pe):
                    pe.wait_ge(loaded, 48 if gate_b is not None else 32)
                    for t in range(TILES):
                        mm = pe.matmul(psum[:, 0, t * E:(t + 1) * E], xnT[:, t * P:(t + 1) * P], gw[:, :], start=True, stop=gate_b is None)
                        if gate_b is not None:
                            mm = pe.matmul(psum[:, 0, t * E:(t + 1) * E], ones_row[0:1, :], gb[:, :], start=False, stop=True)
                    mm.then_inc(gate_made, 1)

                @block.scalar
                def _(act):
                    if top == 2:
                        act.wait_ge(gate_step, 4)
                        act.activation(g1[:, :, 1:2], g1[:, :, 0:1], ACT.Exp).then_inc(gate_exp, 1)

                @block.vector
                def _(dve):
                    n = [0]

                    def link(ins):
                        n[0] += 1
                        ins.then_inc(gate_step, 1)
                        dve.wait_ge(gate_step, n[0])

                    dve.wait_ge(gate_made, 1)
                    dve.wait_ge(loaded, 48 if gate_b is not None else 32)
                    link(dve.tensor_copy(logit[:, :, :], psum[:, 0, 0:TILES * E].rearrange("p (t e) -> p t e", e=E)))
                    for t in range(TILES):
                        ins = dve.max(best[:, t, :], logit[:, t, :])
                        ins.then_inc(chain, 1)
                    dve.wait_ge(chain, TILES)
                    for t in range(TILES):
                        ins = dve.max_index(besti[:, t, :], best[:, t, :], logit[:, t, :])
                        ins.then_inc(swept, 1)
                    dve.wait_ge(swept, TILES)
                    link(dve.tensor_copy(bestf[:, :, :], besti[:, :, :]))
                    ids = iota[:, :].unsqueeze(1).to_broadcast([P, TILES, E])
                    link(dve.tensor_tensor(we[:, :, :], ids, bestf[:, :, 0:1].to_broadcast([P, TILES, E]), ALU.is_equal))
                    if top == 2:
                        link(dve.tensor_tensor(g1[:, :, 0:1], best[:, :, 1:2], best[:, :, 0:1], ALU.subtract))
                        link(dve.tensor_tensor(tmp[:, :, :], ids, bestf[:, :, 1:2].to_broadcast([P, TILES, E]), ALU.is_equal))
                        dve.wait_ge(gate_exp, 1)
                        link(dve.tensor_tensor(tmp[:, :, :], tmp[:, :, :], g1[:, :, 1:2].to_broadcast([P, TILES, E]), ALU.mult))
                        link(dve.tensor_tensor(we[:, :, :], we[:, :, :], tmp[:, :, :], ALU.add))
                        link(dve.tensor_scalar(g1[:, :, 0:1], g1[:, :, 1:2], 1.0, None, ALU.add))
                        link(dve.reciprocal(g1[:, :, 1:2], g1[:, :, 0:1]))
                        link(dve.tensor_tensor(we[:, :, :], we[:, :, :], g1[:, :, 1:2].to_broadcast([P, TILES, E]), ALU.mult))
            clear()

            NU = 2 * FC
            with nc.Block() as block:
                @block.sync
                def _(sp):
                    with sp.Fori(0, E // 2) as i:
                        for r in range(2):
                            sp.wait_ge(swept, 2 * i + r + 1)
                            e = 2 * i + r
                            sp.dma_start(w1[:, r, :], w1_d[e]).then_inc(weights_in[r], 16)
                            sp.dma_start(w2[:, r, :], w2_d[e]).then_inc(weights_in[r], 16)
                            sp.dma_start(b1[:, r, :], b1_d[e]).then_inc(weights_in[r], 16)
                            sp.dma_start(b2[:, r, :], b2_d[e]).then_inc(weights_in[r], 16)

                @block.tensor
                def _(pe):
                    pe.sem_inc(swept, 2)
                    with pe.Fori(0, E // 2) as i:
                        for r in range(2):
                            pe.wait_ge(weights_in[r], 64 * i + 64)
                            for k in range(2):
                                for c in range(FC):
                                    n = FC * k + c
                                    pe.wait_ge(act_done, NU * (2 * i + r) + n + 1)
                                    pe.matmul(psum[:, n % 2, :], w1[:, r, c * P:(c + 1) * P], xnT[:, k * 512:(k + 1) * 512],
                                              start=True, stop=True).then_inc(up_made, 1)
                            for t in range(TILES):
                                k = t // 4
                                if t % 4 == 0:
                                    pe.wait_ge(act_done, NU * (2 * i + r) + FC * (k + 1) + 2)
                                    pe.wait_ge(down_read, TILES * (2 * i + r) + 4 * k + 4)
                                o = psum[:, 2 + k, (t % 4) * D:(t % 4 + 1) * D]
                                for c in range(FC):
                                    pe.matmul(o, hT[:, c, t * P:(t + 1) * P], w2[:, r, c * D:(c + 1) * D], start=(c == 0), stop=False)
                                mm = pe.matmul(o, ones_row[0:1, :], b2[0:1, r, :], start=False, stop=True)
                                if t % 4 == 3:
                                    mm.then_inc(down_made, 1)
                            pe.wait_ge(down_made, 2 * (2 * i + r) + 2)
                            pe.sem_inc(swept, 1)

                @block.scalar
                def _(act):
                    act.sem_inc(act_done, 2)
                    with act.Fori(0, E // 2) as i:
                        for r in range(2):
                            for k in range(2):
                                for c in range(FC):
                                    n = FC * k + c
                                    act.wait_ge(up_made, NU * (2 * i + r) + n + 1)
                                    if c == 0:
                                        act.wait_ge(swept, 2 * i + r + 2 - 0)
                                    act.activation(hT[:, c, k * 512:(k + 1) * 512], psum[:, n % 2, :], func,
                                                   bias=b1[:, r, c:c + 1]).then_inc(act_done, 1)

                @block.vector
                def _(dve):
                    dve.sem_inc(down_read, TILES)
                    with dve.Fori(0, E // 2) as i:
                        for r in range(2):
                            dve.tensor_copy(wcol[:, r, :], we[:, :, 2 * i + r]).then_inc(chain, 1)
                            dve.wait_ge(chain, 2 * i + r + 1)
                            for t in range(TILES):
                                k = t // 4
                                if t % 4 == 0:
                                    dve.wait_ge(down_made, 2 * (2 * i + r) + k + 1)
                                dve.scalar_tensor_tensor(z[:, t, :], psum[:, 2 + k, (t % 4) * D:(t % 4 + 1) * D], wcol[:, r, t:t + 1],
                                                         z[:, t, :], ALU.mult, ALU.add).then_inc(down_read, 1)
            clear()

    def add_into(a, b):
        with nc.Block() as block:
            @block.vector
            def _(dve):
                dve.tensor_tensor(a[:, :, :], a[:, :, :], b[:, :, :], ALU.add)
        clear()

    def finish(src, inner=None):
        with nc.Block() as block:
            @block.sync
            def _(sp):
                sp.dma_start(out.rearrange("b (t p) d -> p (b t) d", p=P), src[:, :, :]).then_inc(stored, 16)
                sp.wait_ge(stored, 16)
        if inner is not None:
            inner.close()
        top.close()

    resampler()
    if stop == "A":
        return finish(x_sb)

    KTC = len(key_tiles(SC))
    st = ExitStack()
    KTS_SELF = S // P
    v_self = sb(st, "v_self", [P, UNITS, KTS_SELF, 2, HD + 1])
    kst = sb(st, "kst", [P, RING, SC], BF16)
    qst = sb(st, "qst", [P, RING, 2 * S], BF16)
    vst = sb(st, "vst", [P, 2, KTC, 2, VW])
    probs = sb(st, "probs8", [P, 4, 2 * S])
    mp = sb(st, "mp8", [P, 2, 4, 4])
    nm = sb(st, "nm8", [P, 2, QT, 65], BF16)
    oT = sb(st, "oT", [P, 2, S])
    rec = sb(st, "rec8", [P, 2, 4])
    sel = sb(st, "sel", [P, 18])
    o_tok = sb(st, "o_tok", [P, UNITS, 4, HD])
    oTT = sb(st, "oTT", [P, NTOK])
    bufs = (kst, qst, vst, probs, mp, nm, oT, rec, sel)
    par = (sb(st, "mixA", [P, 2, 512]), sb(st, "mixB", [P, 2, 512]), sb(st, "tot", [P, 2, 512]), sb(st, "rest", [P, 2, 512]),
           sb(st, "hi", [P, 2, 512], BF16), sb(st, "mid", [P, 2, 512], BF16), sb(st, "lo", [P, 2, 512], BF16))

    with nc.Block() as block:
        @block.vector
        def _(dve):
            dve.memset(qst[:, :, :], 0.0)
            dve.memset(nm[:, :, :, :], 0.0)
            dve.memset(v_self[:, :, :, :, :], 1.0)
            dve.memset(kst[:, :, :], 0.0).then_inc(zeroed, 1)
            dve.wait_ge(zeroed, 1)
            dve.memset(kst[0:1, :, :], 1.0)
            dve.memset(kst[64:65, :, :], 1.0)

        @block.gpsimd
        def _(pool):
            pool.memset(vst[:, :, :, :, :], 0.0)

        @block.sync
        def _(sp):
            sp.dma_start(sel[:, :], T["sel"]).then_inc(loaded, 16)
            sp.wait_ge(loaded, 16)
    clear()
    with nc.Block() as block:
        @block.sync
        def _(sp):
            for r in range(RING):
                sp.dma_start(qst[1:2, r, 0:S], T["ones"]).then_inc(loaded2, 16)
                sp.dma_start(qst[65:66, r, S:2 * S], T["ones"]).then_inc(loaded2, 16)
            sp.wait_ge(loaded2, 32 * RING)
    clear()

    with ExitStack() as s2:
        wqkv = sb(s2, "wqkv", [P, 3 * D])
        wo2 = sb(s2, "wo2", [P, D])
        bq = sb(s2, "bq", [P, 2])
        bvr = sb(s2, "bvr", [1, D])
        bor = sb(s2, "bor", [1, D])
        with nc.Block() as block:
            @block.sync
            def _(sp):
                sp.dma_start(wqkv[:, :], T["w_qkv"]).then_inc(loaded, 16)
                sp.dma_start(wo2[:, :], T["w_o"]).then_inc(loaded, 16)
                sp.dma_start(bq[:, :], T["b_qk"]).then_inc(loaded, 16)
                sp.dma_start(bvr[:, :], T["b_v"]).then_inc(loaded, 16)
                sp.dma_start(bor[:, :], T["b_o"]).then_inc(loaded, 16)
                sp.wait_ge(loaded, 80)
        clear()
        layer_norm(x_sb, z_sb)
        layer_norm(z_sb, xhat, turn=xnT, affine=(lambda b: vecs[:, 2:3], lambda b: vecs[:, 3:4]))
        jobs, vjobs = [], []
        for b in range(B):
            for w, parts, dram in ((0, PARTS_Q, None), (1, PARTS_K, k_first_d)):
                jobs.append(dict(n=S, w=wqkv[:, w * D:(w + 1) * D], ws=None, bias=bq[:, w:w + 1], rhs=xnT[:, b * S:(b + 1) * S],
                                 parts=parts, dst=lambda slot, b=b, dram=dram: q_d[b, :, slot, :] if dram is None else key_rows(dram, b, slot, 0, S)))
            for t in range(KTS_SELF):
                at = b * S + t * P
                vjobs.append((xnT[:, at:at + P], wqkv[:, 2 * D:3 * D], P,
                              v_self[:, b * PAIRS:(b + 1) * PAIRS, t, :, 0:HD], bvr[0:1, :]))
        make_operands(st, jobs, vjobs, par)
        attention(bufs, S, k_first_d, v_self, o_tok)
        project_out(o_tok, oTT, wo2[:, :], bor[0:1, :], z_sb)
    if stop == "B1":
        return finish(z_sb, st)
    layer_norm(z_sb, xhat, turn=xnT, affine=(lambda b: vecs[:, 4:5], lambda b: vecs[:, 5:6]))
    experts(T["w_gate"], None, T["L0_w1"], T["L0_b1"], T["L0_w2"], T["L0_b2"], ACT.Gelu_apprx_tanh, 2, z_sb, "l0")
    add_into(x_sb, z_sb)
    if stop == "B":
        return finish(x_sb, st)

    with ExitStack() as s2:
        v_ctx = sb(s2, "v_ctx", [P, UNITS, KTC, 2, HD + 1])
        ctxT = sb(s2, "ctxT", [P, B * SC])
        cos = sb(s2, "cos", [P, SC])
        sin = sb(s2, "sin", [P, SC])
        W = sb(s2, "W", [P, WCOLS])
        hT = oTT

        layer_norm(x_sb, z_sb)
        with nc.Block() as block:
            @block.sync
            def _(sp):
                sp.dma_start(ctxT[:, :], T["ctxT"]).then_inc(loaded, 16)
                sp.dma_start(cos[:, :], T["cos"]).then_inc(loaded, 16)
                sp.dma_start(sin[:, :], T["sin"]).then_inc(loaded, 16)
                sp.wait_ge(loaded, 48)

            @block.vector
            def _(dve):
                dve.memset(v_ctx[:, :, :, :, :], 1.0)
        clear()

        def w(name):
            at, n = COL[name]
            return W[:, at:at + n]

        def rope_jobs(wn, ws, rhs, n, pos, parts, dst):
            return dict(n=n, w=w(wn), ws=w(ws), rhs=rhs, cos=cos[:, pos:pos + n], sin=sin[:, pos:pos + n], parts=parts, dst=dst)

        with nc.Fori(0, NL if stop != "C1" else 1) as l:
            with nc.Block() as block:
                @block.sync
                def _(sp):
                    sp.dma_start(W[:, :], T["layers"][l]).then_inc(loaded, 16)
                    sp.dma_start(brow[0:1, 0:D], T["f2_b"][l]).then_inc(loaded, 16)
                    sp.wait_ge(loaded, 32)
            clear()
            layer_norm(z_sb, xhat, turn=xnT, modulate=(w("n1"), w("n1b")))
            jobs, vjobs = [], []
            for b in range(B):
                for wn, parts, dram in (("q", PARTS_Q, None), ("k", PARTS_K, k_self_d)):
                    jobs.append(rope_jobs(wn, wn + "s", xnT[:, b * S:(b + 1) * S], S, 0, parts,
                                          lambda slot, b=b, dram=dram: q_d[b, :, slot, :] if dram is None else key_rows(dram, b, slot, 0, S)))
                for t in range(KTS_SELF):
                    at = b * S + t * P
                    vjobs.append((xnT[:, at:at + P], w("v"), P, v_self[:, b * PAIRS:(b + 1) * PAIRS, t, :, 0:HD], None))
            make_operands(st, jobs, vjobs, par)
            attention(bufs, S, k_self_d, v_self, o_tok)
            project_out(o_tok, oTT, w("so"), None, z_sb)
            layer_norm(z_sb, xhat, turn=xnT, modulate=(w("n2"), w("n2b")))
            jobs, vjobs = [], []
            cuts = [0, 401, 801, 1201, SC]
            for b in range(B):
                jobs.append(rope_jobs("cq", "cqs", xnT[:, b * S:(b + 1) * S], S, 0, PARTS_Q, lambda slot, b=b: q_d[b, :, slot, :]))
                for lo_, hi_ in zip(cuts, cuts[1:]):
                    jobs.append(rope_jobs("ck", "cks", ctxT[:, b * SC + lo_:b * SC + hi_], hi_ - lo_, lo_, PARTS_K,
                                          lambda slot, b=b, lo_=lo_, hi_=hi_: key_rows(k_ctx_d, b, slot, lo_, hi_)))
                for t, (k, n) in enumerate(key_tiles(SC)):
                    vjobs.append((ctxT[:, b * SC + k:b * SC + k + n], w("cv"), n,
                                  v_ctx[0:n, b * PAIRS:(b + 1) * PAIRS, t, :, 0:HD], None))
            make_operands(st, jobs, vjobs, par)
            attention(bufs, SC, k_ctx_d, v_ctx, o_tok)
            project_out(o_tok, oTT, w("co"), None, z_sb)
            layer_norm(z_sb, xhat, turn=xnT, modulate=(w("n3"), w("n3b")))
            with ExitStack() as s3:
                hid = sb(s3, "hid", [P, FC, NTOK])
                feed_forward(w("f1"), w("f1b"), w("f2"), brow[0:1, 0:D], hid, z_sb)
    if stop in ("C", "C1"):
        return finish(z_sb, st)
    add_into(x_sb, z_sb)

    layer_norm(x_sb, xhat, turn=xnT, affine=(lambda b: 1.0, lambda b: 0.0))
    experts(T["gate_w"], T["gate_b"], T["L1_w1"], T["L1_b1"], T["L1_w2"], T["L1_b2"], ACT.Relu, 1, x_sb, "l1")
    st.close()
    finish(x_sb)


def _layout(I):
    f = np.ascontiguousarray
    A = {k: np.asarray(v) for k, v in I.items()}
    T = {}
    T["x"] = A["x"]
    T["ctx"] = A["ctx_1024"]
    T["ctxT"] = f(A["ctx_1024"].transpose(2, 0, 1).reshape(D, B * SC))
    T["condT"] = f(A["cond_1024"].T)
    T["mask_ctx"] = f(np.repeat(A["mask_BxS2_bf0"], H, axis=0))
    T["mask_x"] = f(np.repeat(A["mask_BxS_bf0"], H, axis=0))
    T["ident"] = np.eye(P, dtype=np.float32)
    names = ["L0_xcond_ln2_w", "L0_xcond_ln2_b", "L0_ffn_ln1_w", "L0_ffn_ln1_b", "L0_ffn_ln2_w", "L0_ffn_ln2_b"]
    T["vecs"] = f(np.stack([A[n] for n in names] * 2, axis=1))
    T["ln1_w"], T["ln1_b"] = A["L0_xcond_ln1_w"].reshape(1, D), A["L0_xcond_ln1_b"].reshape(1, D)
    heads = lambda a: f(a.reshape(H, EA, D).transpose(1, 0, 2))
    T["Wq"] = heads(A["L0_xcond_Wq"])
    T["Wk"] = heads(A["L0_xcond_Wkv"][:H * EA])
    T["Wv"] = heads(A["L0_xcond_Wkv"][H * EA:])
    T["Wo"] = heads(A["L0_xcond_Wo"].T)
    sel = np.zeros((P, 18), np.float32)
    for c in range(4):
        for e in range(HD + 1):
            sel[VW * c + e, (HD + 1) * (c % 2) + e] = 1
    T["sel"] = sel
    T["ones"] = np.ones((1, S), T_BF16())
    T["iota"] = f(np.tile(np.arange(E, dtype=np.float32), (P, 1)))
    half = HD // 2
    inv = (np.float32(1.0) / np.float32(10000.0) ** (np.arange(half, dtype=np.float32) / np.float32(half))).astype(np.float32)
    ang = (np.arange(SC, dtype=np.float32)[:, None] * inv).astype(np.float32)
    c, s = np.cos(ang).T, np.sin(ang).T
    T["cos"] = f(np.tile(np.concatenate([c, c]), (H, 1)).astype(np.float32))
    T["sin"] = f(np.tile(np.concatenate([-s, s]), (H, 1)).astype(np.float32))
    T["w_qkv"], T["w_o"] = A["L0_ffn_w_qkv"], A["L0_ffn_w_o"]
    bqkv = A["L0_ffn_b_qkv"].reshape(3, D)
    T["b_qk"] = f(bqkv[0:2].T)
    T["b_v"] = f(bqkv[2:3])
    T["b_o"] = A["L0_ffn_b_o"].reshape(1, D)
    T["w_gate"] = A["L0_ffn_w_gate"]
    T["L0_w1"] = A["L0_ffn_w1"]
    T["L0_b1"] = f(A["L0_ffn_b1"].reshape(E, FC, P).transpose(0, 2, 1))
    T["L0_w2"] = f(A["L0_ffn_w2"].reshape(E, FC, P, D).transpose(0, 2, 1, 3).reshape(E, P, FC * D))
    T["L0_b2"] = A["L0_ffn_b2"].reshape(E, 1, D)
    T["gate_w"] = f(A["L1_ffn_gate_w"].T)
    T["gate_b"] = A["L1_ffn_gate_b"].reshape(1, E)
    T["L1_w1"] = f(A["L1_ffn_w1"].transpose(0, 2, 1))
    T["L1_b1"] = f(A["L1_ffn_b1"].reshape(E, FC, P).transpose(0, 2, 1))
    T["L1_w2"] = f(A["L1_ffn_w2"].reshape(E, D, FC, P).transpose(0, 3, 2, 1).reshape(E, P, FC * D))
    T["L1_b2"] = A["L1_ffn_b2"].reshape(E, 1, D)
    g = lambda n: A["L1_xcond_" + n]
    swap = np.arange(D).reshape(H, 2, half)[:, ::-1].reshape(D)
    t = lambda a: a.transpose(0, 2, 1)
    qkv = g("qkv_w")
    q, k, v = qkv[:, 0:D], qkv[:, D:2 * D], qkv[:, 2 * D:]
    col = lambda a, n: a.reshape(NL, n, P).transpose(0, 2, 1)
    parts = [t(g("n1_w")), t(g("n2_w")), t(g("n3_w")), t(q), t(q[:, swap]), t(k), t(k[:, swap]), t(v), t(g("so_w")),
             t(g("cq_w")), t(g("cq_w")[:, swap]), t(g("ck_w")), t(g("ck_w")[:, swap]), t(g("cv_w")), t(g("co_w")), t(g("f1_w")),
             g("f2_w").reshape(NL, D, FC, P).transpose(0, 3, 2, 1).reshape(NL, P, FC * D),
             col(g("n1_b"), 2), col(g("n2_b"), 2), col(g("n3_b"), 2), col(g("f1_b"), FC)]
    T["layers"] = f(np.concatenate(parts, axis=2))
    T["f2_b"] = g("f2_b").reshape(NL, 1, D)
    return {n: f(a) for n, a in T.items()}


def T_BF16():
    return mybir.dt.np(BF16)


def kernel(**inputs):
    import concourse.bacc as _bacc
    from concourse.bass_utils import run_bass_kernel_spmd as _run

    T = _layout(inputs)
    nc = _bacc.Bacc("TRN2", target_bir_lowering=False, num_devices=1)
    arrays, aps = {}, {}
    for name, a in T.items():
        arrays[f"in_{name}"] = a
        aps[name] = nc.dram_tensor(f"in_{name}", a.shape, mybir.dt.from_np(a.dtype), kind="ExternalInput").ap()
    out = nc.dram_tensor("out", (B, S, D), F32, kind="ExternalOutput").ap()
    build_program(nc, aps, out)
    r = _run(nc, [arrays], core_ids=[0])
    return r.results[0]["out"]
```

```python
from contextlib import ExitStack

import numpy as np

import concourse.bass as bass
from concourse import mybir

F32 = mybir.dt.float32
BF16 = mybir.dt.bfloat16
U8 = mybir.dt.uint8
U32 = mybir.dt.uint32
ALU = mybir.AluOpType
ACT = mybir.ActivationFunctionType
AX = mybir.AxisListType

P = 128
B, S, D = 4, 256, 128
NTOK = B * S
TILES = NTOK // P
QT = S // P
SC = 1601
H, HD = 16, 8
PAIRS = H // 2
UNITS = B * PAIRS
NL, DFF, E = 6, 512, 8
FC = DFF // P
EA = 64
EPS = 1e-5
ONES_BF16 = float(np.array([0x3F803F80], np.uint32).view(np.float32)[0])
MASKED = -1.0e30 / 8

PARTS_Q = (0, 0, 0, 1, 2, 1)
PARTS_K = (1, 2, 0, 0, 0, 1)
SLOTS = len(PARTS_Q) + 1
BIAS = SLOTS - 1
ROWS = HD * SLOTS
R0 = 1
VW = 32
JB = 3

_NAMES = [("n1", 256), ("n2", 256), ("n3", 256), ("q", 128), ("qs", 128), ("k", 128), ("ks", 128), ("v", 128),
          ("so", 128), ("cq", 128), ("cqs", 128), ("ck", 128), ("cks", 128), ("cv", 128), ("co", 128),
          ("n1b", 2), ("n2b", 2), ("n3b", 2), ("f1", DFF), ("f2", DFF), ("f1b", FC)]
COL, _at = {}, 0
for _n, _w in _NAMES:
    COL[_n] = (_at, _w)
    _at += _w
WCOLS = _at
WLATE = COL["f1"][0]


def key_tiles(n):
    return [(k, min(P, n - k)) for k in range(0, n, P)]


class Unit:

    def __init__(self, step, i, r):
        self.step, self.i, self.r = step, i, r

    def at(self, k=0):
        return self.step * self.i + (self.r + k)

    def turn(self, k=0):
        return self.i + (self.r + k) // self.step + 1

    def pair(self, k=0):
        return self.step // B * self.i + (self.r + k) // B

    def batch(self, k=0):
        return (self.r + k) % B

    def buf(self, n, k=0):
        return (self.r + k) % n


def wait(eng, sem, value):
    if isinstance(value, int) and value <= 0:
        return
    eng.wait_ge(sem, value)


def build_program(nc, T, out):
    top = ExitStack()
    sems = []

    def sem(name):
        s = top.enter_context(nc.semaphore(name))
        sems.append(s)
        return s

    def clear():
        nc.all_engine_barrier(sems_to_clear=range(sems[0].num, sems[-1].num + 1))

    def sb(st, name, shape, dt=F32):
        return st.enter_context(nc.sbuf_tensor(name, shape, dt))

    psum = top.enter_context(nc.psum_tensor("psum", [P, 8, 512], F32))

    k_ctx_d = nc.dram_tensor("k_ctx_parts", [P, SLOTS, B, SC], BF16, kind="Internal").ap()
    k_self_d = nc.dram_tensor("k_self_parts", [P, SLOTS, NTOK], BF16, kind="Internal").ap()
    k_first_d = nc.dram_tensor("k_first_parts", [P, SLOTS, NTOK], BF16, kind="Internal").ap()
    q_d = nc.dram_tensor("q_parts", [P, SLOTS, NTOK], BF16, kind="Internal").ap()

    x_sb = sb(top, "x_sb", [P, TILES, D])
    z_sb = sb(top, "z_sb", [P, TILES, D])
    xhat = sb(top, "xhat", [P, TILES, D])
    xnT = sb(top, "xnT", [P, NTOK])
    ident = sb(top, "ident", [P, P])
    ident_b = sb(top, "ident_b", [P, P], BF16)
    condT = sb(top, "condT", [P, B])
    vecs = sb(top, "vecs", [P, 12])
    stats = sb(top, "stats", [P, TILES + 6, 6])
    mv = sb(top, "mv", [P, TILES + 6, 2])
    rstd = sb(top, "rstd", [P, TILES + 6])
    nhalf = sb(top, "nhalf", [P, TILES + 6])
    scl = sb(top, "scl", [P, B])
    bia = sb(top, "bia", [P, B])
    ones_col = sb(top, "ones_col", [P, 1])
    ones_row = sb(top, "ones_row", [1, P])
    brow = sb(top, "brow", [1, 2 * D])

    loaded = sem("loaded")
    loaded2 = sem("loaded2")
    stat_done = sem("stat_done")
    aggr_done = sem("aggr_done")
    eps_added = sem("eps_added")
    rstd_done = sem("rstd_done")
    norm_done = sem("norm_done")
    transposed = sem("transposed")
    affine_done = sem("affine_done")
    mod_made = sem("mod_made")
    mod_ready = sem("mod_ready")
    ring_loaded = [sem(f"ring_loaded{i}") for i in range(4)]
    row_cleared = sem("row_cleared")
    v_staged = sem("v_staged")
    max_scores = sem("max_scores")
    max_read = sem("max_read")
    max_done = sem("max_done")
    max_row = sem("max_row")
    shift_ready = sem("shift_ready")
    scored = sem("scored")
    exp_done = sem("exp_done")
    pv_done = sem("pv_done")
    o_copied = sem("o_copied")
    o_turned = sem("o_turned")
    o_scaled = sem("o_scaled")
    rec_done = sem("rec_done")
    proj_made = sem("proj_made")
    proj_read = sem("proj_read")
    summed = sem("summed")
    hi_done = sem("hi_done")
    rest_done = sem("rest_done")
    mid_done = sem("mid_done")
    lo_done = sem("lo_done")
    parts_out = [sem(f"parts_out{i}") for i in range(JB)]
    v_made = sem("v_made")
    v_read = sem("v_read")
    v_read2 = sem("v_read2")
    turned = sem("turned")
    turned_out = sem("turned_out")
    up_made = sem("up_made")
    act_done = sem("act_done")
    down_made = sem("down_made")
    down_read = sem("down_read")
    up_weights = [sem("up_weights0"), sem("up_weights1")]
    down_weights = [sem("down_weights0"), sem("down_weights1")]
    gate_made = sem("gate_made")
    gate_step = sem("gate_step")
    gate_exp = sem("gate_exp")
    stored = sem("stored")
    sum_bc = sem("sum_bc")
    bias_rows_made = sem("bias_rows_made")
    mod_step = sem("mod_step")
    q_made = sem("q_made")
    q_read = sem("q_read")
    latents_in = sem("latents_in")
    weighted = sem("weighted")
    straight_made = sem("straight_made")
    swapped_made = sem("swapped_made")
    rotated = sem("rotated")
    total_made = sem("total_made")
    best_found = sem("best_found")
    index_found = sem("index_found")
    weights_picked = sem("weights_picked")

    with nc.Block() as block:
        @block.sync
        def _(sp):
            sp.dma_start(x_sb[:, :, :], T["x"].rearrange("b (t p) d -> p (b t) d", p=P)).then_inc(loaded, 16)
            sp.dma_start(ident[:, :], T["ident"]).then_inc(loaded, 16)
            sp.dma_start(condT[:, :], T["condT"]).then_inc(loaded, 16)
            sp.dma_start(vecs[:, :], T["vecs"]).then_inc(loaded, 16)

        @block.vector
        def _(dve):
            dve.memset(nhalf[:, :], -0.5)
            dve.memset(ones_col[:, :], 1.0)
            dve.memset(ones_row[:, :], 1.0)
            dve.wait_ge(loaded, 64)
            dve.tensor_copy(ident_b[:, :], ident[:, :])
    clear()

    def layer_norm(src, dst, passes=1):
        with nc.Block() as block:
            @block.vector
            def _(dve):
                for n in range(passes):
                    a = src if n == 0 else dst
                    wait(dve, norm_done, TILES * n)
                    for t in range(TILES):
                        dve.bn_stats(stats[:, t, :], a[:, t, :]).then_inc(stat_done, 1)
                    dve.wait_ge(stat_done, TILES * (n + 1))
                    for t in range(TILES):
                        dve.bn_aggr(mv[:, t, :], stats[:, t, :]).then_inc(aggr_done, 1)
                    dve.wait_ge(rstd_done, n + 1)
                    for t in range(TILES):
                        dve.tensor_scalar(dst[:, t, :], a[:, t, :], mv[:, t, 0:1], rstd[:, t:t + 1],
                                          ALU.subtract, ALU.mult).then_inc(norm_done, 1)

            @block.gpsimd
            def _(pool):
                for n in range(passes):
                    pool.wait_ge(aggr_done, TILES * (n + 1))
                    pool.tensor_scalar(rstd[:, 0:TILES], mv[:, 0:TILES, 1], EPS, None, ALU.add).then_inc(eps_added, 1)
                    pool.wait_ge(eps_added, n + 1)
                    pool.tensor_tensor(rstd[:, 0:TILES], rstd[:, 0:TILES], nhalf[:, 0:TILES], ALU.pow).then_inc(rstd_done, 1)
        clear()

    def norm_turned(src, affine=None, modulate=None, project=None, loads=()):
        STAGES = 5
        with nc.Block() as block:
            @block.sync
            def _(sp):
                for to, frm in loads:
                    sp.dma_start(to, frm).then_inc(loaded, 16)
                wait(sp, loaded, 16 * len(loads))

            @block.tensor
            def _(pe):
                if modulate is not None:
                    w = modulate[0]
                    pe.matmul(psum[:, 6, 0:B], w[:, 0:P], condT[:, :], start=True, stop=True)
                    pe.matmul(psum[:, 6, B:2 * B], w[:, P:2 * P], condT[:, :], start=True, stop=True).then_inc(mod_made, 1)
                for i in range(B + STAGES):
                    b = i
                    if project is not None and b < B:
                        wait(pe, turned_out, b - 1)
                        for q in range(QT):
                            mm = pe.transpose(psum[:, b % 2, q * P:(q + 1) * P], project[0][:, b, q, :], ident[:, :])
                        mm.then_inc(turned, 1)
                    b = i - 1
                    if project is not None and 0 <= b < B:
                        pe.wait_ge(turned_out, b + 1)
                        wait(pe, proj_read, b - 1)
                        for q in range(QT):
                            o = psum[:, 2 + b % 2, q * D:(q + 1) * D]
                            at = b * S + q * P
                            mm = pe.matmul(o, project[1][:, at:at + P], project[2], start=True, stop=project[3] is None)
                            if project[3] is not None:
                                mm = pe.matmul(o, ones_row[0:1, :], project[3], start=False, stop=True)
                        mm.then_inc(proj_made, 1)
                    b = i - 3
                    if 0 <= b < B:
                        pe.wait_ge(norm_done, QT * (b + 1))
                        wait(pe, affine_done, b - 1)
                        for q in range(QT):
                            mm = pe.transpose(psum[:, 4 + b % 2, q * P:(q + 1) * P], xhat[:, QT * b + q, :], ident[:, :])
                        mm.then_inc(transposed, 1)

            @block.scalar
            def _(act):
                if project is not None:
                    for b in range(B):
                        act.wait_ge(turned, b + 1)
                        act.activation(project[1][:, b * S:(b + 1) * S], psum[:, b % 2, 0:S], ACT.Copy).then_inc(turned_out, 1)

            @block.gpsimd
            def _(pool):
                for b in range(B):
                    own = slice(QT * b, QT * (b + 1))
                    pool.wait_ge(aggr_done, QT * (b + 1))
                    pool.tensor_scalar(rstd[:, own], mv[:, own, 1], EPS, None, ALU.add).then_inc(eps_added, 1)
                    pool.wait_ge(eps_added, b + 1)
                    pool.tensor_tensor(rstd[:, own], rstd[:, own], nhalf[:, own], ALU.pow).then_inc(rstd_done, 1)

            @block.vector
            def _(dve):
                if modulate is not None:
                    wb = modulate[1]
                    dve.wait_ge(mod_made, 1)
                    dve.tensor_scalar(scl[:, :], psum[:, 6, 0:B], wb[:, 0:1], 1.0, ALU.add, ALU.add).then_inc(mod_ready, 1)
                    dve.tensor_scalar(bia[:, :], psum[:, 6, B:2 * B], wb[:, 1:2], None, ALU.add).then_inc(mod_ready, 1)
                    dve.wait_ge(mod_ready, 2)
                for i in range(B + STAGES):
                    b = i
                    if b < B:
                        tiles = range(QT * b, QT * (b + 1))
                        if project is not None:
                            dve.wait_ge(proj_made, b + 1)
                            own = slice(QT * b, QT * (b + 1))
                            dve.tensor_tensor(src[:, own, :], src[:, own, :], psum[:, 2 + b % 2, 0:QT * D].rearrange("p (t d) -> p t d", t=QT),
                                              ALU.add).then_inc(proj_read, 1)
                            dve.wait_ge(proj_read, b + 1)
                        for t in tiles:
                            dve.bn_stats(stats[:, t, :], src[:, t, :]).then_inc(stat_done, 1)
                        dve.wait_ge(stat_done, QT * (b + 1))
                        for t in tiles:
                            dve.bn_aggr(mv[:, t, :], stats[:, t, :]).then_inc(aggr_done, 1)
                    b = i - 1
                    if 0 <= b < B:
                        dve.wait_ge(rstd_done, b + 1)
                        for t in range(QT * b, QT * (b + 1)):
                            dve.tensor_scalar(xhat[:, t, :], src[:, t, :], mv[:, t, 0:1], rstd[:, t:t + 1],
                                              ALU.subtract, ALU.mult).then_inc(norm_done, 1)
                    b = i - 2
                    if 0 <= b < B:
                        s = scl[:, b:b + 1] if modulate is not None else affine[0]
                        o = bia[:, b:b + 1] if modulate is not None else affine[1]
                        dve.wait_ge(transposed, b + 1)
                        dve.tensor_scalar(xnT[:, b * S:(b + 1) * S], psum[:, 4 + b % 2, 0:S], s, o,
                                          ALU.mult, ALU.add).then_inc(affine_done, 1)
        clear()

    def resampler():
        KTS = key_tiles(SC) + [(SC, P), (SC + P, P)]
        NK = SC + S
        KT = len(KTS)
        CT = len(key_tiles(SC))
        st = ExitStack()
        a_sb = sb(st, "a_sb", [P, H, P])
        wv = sb(st, "wv", [P, H * EA])
        wo = sb(st, "wo", [P, PAIRS, D])
        qp = sb(st, "qp", [P, PAIRS, 2 * S])
        qhi = sb(st, "qhi", [P, PAIRS, 2 * S], BF16)
        ones_f = sb(st, "ones_f", [P, P])
        ones_b = sb(st, "ones_b", [1, P], BF16)
        lnw = sb(st, "lnw", [P, 2, D])

        layer_norm(x_sb, xhat, passes=2)

        with ExitStack() as s2:
            wq = sb(s2, "wq", [EA, H, D])
            wk = sb(s2, "wk", [EA, H, D])
            ms = sb(s2, "ms", [P, NTOK], U8)
            mbs = sb(s2, "mbs", [P, 3, NTOK], BF16)
            with nc.Block() as block:
                @block.sync
                def _(sp):
                    sp.dma_start(ms[:, :], T["mask_x"].partition_broadcast(P)).then_inc(loaded2, 16)
                    sp.dma_start(wq[:, :, :], T["Wq"]).then_inc(loaded, 16)
                    sp.dma_start(wk[:, :, :], T["Wk"]).then_inc(loaded, 16)
                    sp.dma_start(wv[:, :], T["Wv"]).then_inc(loaded2, 16)
                    sp.dma_start(wo[:, :, :], T["Wo"]).then_inc(loaded2, 16)
                    sp.dma_start(lnw[:, 0, :], T["ln1_w"].partition_broadcast(P)).then_inc(loaded2, 16)
                    sp.dma_start(lnw[:, 1, :], T["ln1_b"].partition_broadcast(P)).then_inc(loaded2, 16)
                    sp.wait_ge(bias_rows_made, 3)
                    sp.dma_start(k_self_d[:, BIAS, :], mbs[:, 0, :]).then_inc(stored, 16)
                    sp.dma_start(k_first_d[:, BIAS, :], mbs[:, 1, :]).then_inc(stored, 16)
                    sp.dma_start(q_d[:, BIAS, :], mbs[:, 2, :]).then_inc(stored, 16)
                    sp.wait_ge(stored, 48)

                @block.gpsimd
                def _(pool):
                    pool.memset(mbs[:, 1, :], 0.0).then_inc(bias_rows_made, 1)
                    pool.memset(mbs[:, 2, :], 1.0).then_inc(bias_rows_made, 1)
                    pool.wait_ge(loaded2, 80)
                    pool.tensor_scalar(mbs[:, 0, :], ms[:, :], MASKED, None, ALU.mult).then_inc(bias_rows_made, 1)

                @block.vector
                def _(dve):
                    dve.memset(ones_f[:, :], 1.0)
                    dve.memset(ones_b[:, :], 1.0)
                    dve.tensor_scalar(scl[:, :], condT[:, :], 1.0, vecs[:, 0:1], ALU.add, ALU.mult).then_inc(mod_step, 1)
                    dve.tensor_scalar(bia[:, :], condT[:, :], 1.0, vecs[:, 1:2], ALU.add, ALU.mult).then_inc(mod_step, 1)
                    dve.wait_ge(mod_step, 2)
                    dve.tensor_tensor(bia[:, :], bia[:, :], condT[:, :], ALU.add).then_inc(mod_step, 1)
                    dve.wait_ge(mod_step, 3)
                    for b in range(B):
                        dve.wait_ge(transposed, QT * (b + 1))
                        dve.tensor_scalar(xnT[:, b * S:(b + 1) * S], psum[:, b % 2, 0:S], scl[:, b:b + 1], bia[:, b:b + 1],
                                          ALU.mult, ALU.add).then_inc(affine_done, 1)
                    for h in range(H):
                        dve.wait_ge(proj_made, h + 1)
                        dve.tensor_copy(a_sb[:, h, :], psum[:, 2 + h % 2, 0:P]).then_inc(proj_read, 1)

                @block.tensor
                def _(pe):
                    for t in range(TILES):
                        b, h = divmod(t, QT)
                        wait(pe, affine_done, b - 1)
                        pe.transpose(psum[:, b % 2, h * P:(h + 1) * P], xhat[:, t, :], ident[:, :]).then_inc(transposed, 1)
                    pe.wait_ge(loaded, 32)
                    for h in range(H):
                        wait(pe, proj_read, h - 1)
                        pe.matmul(psum[:, 2 + h % 2, 0:P], wq[:, h, :], wk[:, h, :], start=True, stop=True).then_inc(proj_made, 1)
            clear()

        craw = sb(st, "craw", [P, CT, D])
        ck = sb(st, "ck", [P, CT, D])
        cT = sb(st, "cT", [P, NK])
        cTh = sb(st, "cTh", [P, NK], BF16)
        NP = 3
        probs = sb(st, "probs", [P, NP, 512])
        psumm = sb(st, "psumm", [P, 2, 512])
        mp = sb(st, "mp", [P, 2, 4, 2])
        nm = sb(st, "nm", [P, 2, 4], BF16)
        nrow = sb(st, "nrow", [1, 2, 512], BF16)
        mk = sb(st, "mk", [P, SC], U8)
        mb = sb(st, "mb", [P, SC], BF16)
        values = sb(st, "values", [P, KT, H * EA])
        vpair = sb(st, "vpair", [P, 2, KT, 2 * EA])
        yraw = sb(st, "yraw", [P, S])
        rec = sb(st, "rec", [P, S])
        yn = sb(st, "yn", [P, S])
        acc = sb(st, "acc", [P, QT, D])
        tail = KTS[CT - 1][1]

        with nc.Block() as block:
            @block.vector
            def _(dve):
                dve.memset(values[:, CT - 1, :], 0.0)
        clear()

        with nc.Fori(0, B) as b:
            ORDER = [CT, CT + 1] + list(range(CT))
            with nc.Block() as block:
                @block.sync
                def _(sp):
                    sp.dma_start(craw[:, 0:CT - 1, :], T["ctx"][b, 0:(CT - 1) * P, :].rearrange("(t p) d -> p t d", p=P)).then_inc(loaded, 16)
                    sp.dma_start(craw[0:tail, CT - 1, :], T["ctx"][b, (CT - 1) * P:SC, :]).then_inc(loaded, 16)
                    sp.dma_start(mk[:, :], T["mask_ctx"][b].partition_broadcast(P)).then_inc(loaded2, 16)
                    sp.wait_ge(bias_rows_made, 1)
                    sp.dma_start(k_ctx_d[:, BIAS, b, :], mb[:, :]).then_inc(stored, 16)
                    sp.wait_ge(stored, 16)

                @block.vector
                def _(dve):
                    dve.tensor_copy(cT[:, SC:NK], xnT[:, bass.ds(b * S, S)]).then_inc(latents_in, 1)
                    dve.memset(acc[:, :, :], 0.0)
                    dve.wait_ge(loaded, 32)
                    for t in range(CT):
                        n = KTS[t][1]
                        dve.bn_stats(stats[0:n, t, :], craw[0:n, t, :]).then_inc(stat_done, 1)
                    dve.wait_ge(stat_done, CT)
                    for t in range(CT):
                        n = KTS[t][1]
                        dve.bn_aggr(mv[0:n, t, :], stats[0:n, t, :]).then_inc(aggr_done, 1)
                    dve.wait_ge(rstd_done, 2)
                    def shift(t):
                        n = KTS[t][1]
                        dve.wait_ge(weighted, t + 1)
                        dve.tensor_tensor(ck[0:n, t, :], ck[0:n, t, :], lnw[0:n, 1, :], ALU.add).then_inc(affine_done, 1)

                    def values_out(m):
                        n = KTS[ORDER[m]][1]
                        dve.wait_ge(v_made, 2 * m + 2)
                        dve.tensor_copy(values[0:n, ORDER[m], 512:1024], psum[0:n, 3 + 2 * (m % 2), :]).then_inc(v_read2, 1)

                    for m in range(2):
                        values_out(m)
                    LAG = 4
                    for t in range(CT):
                        n = KTS[t][1]
                        dve.tensor_scalar(craw[0:n, t, :], craw[0:n, t, :], mv[0:n, t, 0:1], rstd[0:n, t:t + 1],
                                          ALU.subtract, ALU.mult).then_inc(norm_done, 1)
                        if t >= LAG:
                            shift(t - LAG)
                        if t >= LAG + 3:
                            values_out(t - LAG - 1)
                    for t in range(CT - LAG, CT):
                        shift(t)
                        values_out(t - 1)
                    for m in range(CT - 1, CT + 2):
                        values_out(m)

                @block.gpsimd
                def _(pool):
                    pool.wait_ge(aggr_done, CT)
                    for lo, hi, n in ((0, CT - 1, P), (CT - 1, CT, tail)):
                        pool.tensor_scalar(rstd[0:n, lo:hi], mv[0:n, lo:hi, 1], EPS, None, ALU.add).then_inc(eps_added, 1)
                    pool.wait_ge(eps_added, 2)
                    for lo, hi, n in ((0, CT - 1, P), (CT - 1, CT, tail)):
                        pool.tensor_tensor(rstd[0:n, lo:hi], rstd[0:n, lo:hi], nhalf[0:n, lo:hi], ALU.pow).then_inc(rstd_done, 1)
                    for t in range(CT):
                        n = KTS[t][1]
                        pool.wait_ge(norm_done, t + 1)
                        pool.tensor_tensor(ck[0:n, t, :], craw[0:n, t, :], lnw[0:n, 0, :], ALU.mult).then_inc(weighted, 1)
                    pool.wait_ge(loaded2, 16)
                    pool.tensor_scalar(mb[:, :], mk[:, :], MASKED, None, ALU.mult).then_inc(bias_rows_made, 1)

                @block.scalar
                def _(act):
                    def high(t):
                        k, n = KTS[t]
                        act.wait_ge(turned_out, t + 1)
                        act.activation(cTh[:, k:k + n], cT[:, k:k + n], ACT.Copy)

                    def values_out(m):
                        n = KTS[ORDER[m]][1]
                        act.wait_ge(v_made, 2 * m + 1)
                        act.activation(values[0:n, ORDER[m], 0:512], psum[0:n, 2 + 2 * (m % 2), :], ACT.Copy).then_inc(v_read, 1)

                    act.wait_ge(latents_in, 1)
                    act.activation(cTh[:, SC:NK], cT[:, SC:NK], ACT.Copy)
                    for m in range(2):
                        values_out(m)
                    for p in range(PAIRS):
                        act.wait_ge(q_made, p + 1)
                        act.activation(qp[:, p, :], psum[:, 6 + p % 2, :], ACT.Copy).then_inc(q_read, 1)
                        if p >= 1:
                            act.wait_ge(q_read, p)
                            act.activation(qhi[:, p - 1, :], qp[:, p - 1, :], ACT.Copy)
                    act.wait_ge(q_read, PAIRS)
                    act.activation(qhi[:, PAIRS - 1, :], qp[:, PAIRS - 1, :], ACT.Copy)
                    for t in range(CT):
                        k, n = KTS[t]
                        act.wait_ge(turned, t + 1)
                        act.activation(cT[:, k:k + n], psum[:, t % 2, 0:n], ACT.Copy).then_inc(turned_out, 1)
                        if t >= 1:
                            high(t - 1)
                        if t >= 3:
                            values_out(t - 1)
                    high(CT - 1)
                    for m in range(CT - 1, CT + 2):
                        values_out(m)

                @block.tensor
                def _(pe):
                    def values_of(m):
                        k, n = KTS[ORDER[m]]
                        for c, read in enumerate((v_read, v_read2)):
                            wait(pe, read, m - 1)
                            pe.matmul(psum[0:n, 2 + 2 * (m % 2) + c, :], cT[:, k:k + n], wv[:, c * 512:(c + 1) * 512],
                                      start=True, stop=True).then_inc(v_made, 1)

                    pe.wait_ge(latents_in, 1)
                    for m in range(2):
                        values_of(m)
                    for p in range(PAIRS):
                        wait(pe, q_read, p - 1)
                        for h in range(2):
                            mm = pe.matmul(psum[:, 6 + p % 2, h * S:(h + 1) * S], a_sb[:, 2 * p + h, :], xnT[:, bass.ds(b * S, S)],
                                           start=True, stop=True)
                        mm.then_inc(q_made, 1)
                    for t in range(CT):
                        n = KTS[t][1]
                        pe.wait_ge(affine_done, t + 1)
                        wait(pe, turned_out, t - 1)
                        pe.transpose(psum[:, t % 2, 0:n], ck[0:n, t, :], ident[0:n, 0:n]).then_inc(turned, 1)
                        if t >= 2:
                            pe.wait_ge(turned_out, t - 1)
                            values_of(t)
                    for m in (CT, CT + 1):
                        pe.wait_ge(turned_out, m - 1)
                        values_of(m)
            clear()

            NG = 8
            WIDE = 1024
            STEP = 2
            SUM_AT, PROJ_AT, MAX_AT = 2, 6, KT - 2
            group_at = [1 + g for g in range(NG)]

            def loop(eng, body, prologue, epilogue):
                prologue()
                for r in range(STEP):
                    body(Unit(STEP, 0, r), r == 0, False)
                with eng.Fori(1, PAIRS // STEP - 1) as i:
                    for r in range(STEP):
                        body(Unit(STEP, i, r), False, False)
                for r in range(STEP):
                    body(Unit(STEP, PAIRS // STEP - 1, r), False, r == STEP - 1)
                epilogue(Unit(STEP, PAIRS // STEP - 1, STEP - 1))

            with nc.Block() as block:
                @block.tensor
                def _(pe):
                    def group(u, k, g):
                        hq, c = divmod(g, 2)
                        lo, hi = c * WIDE, min(NK, (c + 1) * WIDE)
                        wait(pe, max_read, NG * u.at(k) + g - 1)
                        for o in range(lo, hi, 512):
                            m = min(512, hi - o)
                            mm = pe.matmul(psum[:, 2 * (g % 2) + (o - lo) // 512, 0:m],
                                           qhi[:, u.at(k), hq * P:(hq + 1) * P],
                                           cTh[:, o:o + m], start=True, stop=True)
                        mm.then_inc(max_scores, 1)

                    def turn_max(u, k):
                        pe.wait_ge(max_done, u.at(k) + 1)
                        wait(pe, proj_read, u.at(k) - 1)
                        for hq in range(4):
                            mm = pe.matmul(psum[0:1, 7, hq * P:(hq + 1) * P], nm[:, u.buf(2, k), hq:hq + 1], ident_b[:, :],
                                           start=True, stop=True)
                        mm.then_inc(max_row, 1)

                    def broadcast_sum(u, k):
                        pe.wait_ge(summed, KT * (u.at(k) + 1))
                        wait(pe, proj_read, u.at(k))
                        for h in range(2):
                            mm = pe.matmul(psum[EA * h:EA * (h + 1), 7, 0:S], ones_f[:, 0:EA], psumm[:, u.buf(2, k), h * S:(h + 1) * S],
                                           start=True, stop=True)
                        mm.then_inc(sum_bc, 1)

                    def project(u, k):
                        pe.wait_ge(o_scaled, u.at(k) + 1)
                        for q in range(QT):
                            mm = pe.matmul(psum[:, 7, q * D:(q + 1) * D], yn[:, q * P:(q + 1) * P], wo[:, u.at(k), :], start=True, stop=True)
                        mm.then_inc(proj_made, 1)

                    def prologue():
                        u = Unit(STEP, 0, 0)
                        for g in range(NG):
                            group(u, 0, g)
                        turn_max(u, 0)

                    def body(u, first, last):
                        pe.wait_ge(shift_ready, u.at() + 1)
                        for s in range(KT + 1):
                            m = KT * u.r + s
                            if s < KT:
                                k, n = KTS[s]
                                wait(pe, exp_done, KT * u.at() + s - 1)
                                pe.matmul(psum[0:n, 4 + m % 2, :], cT[:, k:k + n], qp[:, u.at(), :], start=True, stop=False)
                                pe.matmul(psum[0:n, 4 + m % 2, :], ones_b[0:1, 0:n], nrow[0:1, u.buf(2), :],
                                          start=False, stop=True).then_inc(scored, 1)
                            if not last:
                                for g in range(NG):
                                    if group_at[g] == s:
                                        group(u, 1, g)
                            if s >= 1:
                                k, n = KTS[s - 1]
                                pe.wait_ge(exp_done, KT * u.at() + s)
                                if s == 1:
                                    wait(pe, o_copied, u.at())
                                    pe.wait_ge(v_staged, u.at() + 1)
                                for h in range(2):
                                    mm = pe.matmul(psum[EA * h:EA * (h + 1), 6, 0:S], vpair[0:n, u.buf(2), s - 1, EA * h:EA * (h + 1)],
                                                   probs[0:n, (m - 1) % NP, h * S:(h + 1) * S], start=(s == 1), stop=(s == KT))
                                mm.then_inc(pv_done, 1)
                            if s == SUM_AT and not first:
                                broadcast_sum(u, -1)
                            if s == PROJ_AT and not first:
                                project(u, -1)
                            if s == MAX_AT and not last:
                                turn_max(u, 1)

                    def epilogue(u):
                        broadcast_sum(u, 0)
                        project(u, 0)

                    loop(pe, body, prologue, epilogue)

                @block.scalar
                def _(act):
                    def row(u, k):
                        act.wait_ge(max_row, u.at(k) + 1)
                        wait(act, scored, KT * u.at(k - 1))
                        act.activation(nrow[0:1, u.buf(2, k), :], psum[0:1, 7, :], ACT.Copy).then_inc(shift_ready, 1)

                    def copy_o(u, k):
                        act.wait_ge(pv_done, KT * (u.at(k) + 1))
                        wait(act, o_scaled, u.at(k))
                        act.activation(yraw[:, :], psum[:, 6, 0:S], ACT.Copy).then_inc(o_copied, 1)

                    def body(u, first, last):
                        if not first:
                            copy_o(u, -1)
                        for s in range(KT):
                            m = KT * u.r + s
                            if s == MAX_AT + 1 and not last:
                                row(u, 1)
                            n = KTS[s][1]
                            act.wait_ge(scored, KT * u.at() + s + 1)
                            wait(act, pv_done, KT * u.at() + s - NP + 1)
                            wait(act, summed, KT * u.at() + s - NP + 1)
                            act.activation(probs[0:n, m % NP, :], psum[0:n, 4 + m % 2, :], ACT.Exp, scale=EA ** -0.5).then_inc(exp_done, 1)

                    loop(act, body, lambda: row(Unit(STEP, 0, 0), 0), lambda u: copy_o(u, 0))

                @block.vector
                def _(dve):
                    def group(u, k, g):
                        hq, c = divmod(g, 2)
                        m = min(NK, (c + 1) * WIDE) - c * WIDE
                        dve.wait_ge(max_scores, NG * u.at(k) + g + 1)
                        src = psum[:, 2 * (g % 2):2 * (g % 2) + 2, :].rearrange("p a n -> p (a n)")[:, 0:m]
                        dve.tensor_reduce(mp[:, u.buf(2, k), hq, c:c + 1], src, op=ALU.max, axis=AX.X).then_inc(max_read, 1)

                    def merge(u, k):
                        dve.wait_ge(max_read, NG * (u.at(k) + 1))
                        wait(dve, max_row, u.at(k) - 1)
                        dve.tensor_reduce(nm[:, u.buf(2, k), :], mp[:, u.buf(2, k), :, :], op=ALU.max, axis=AX.X,
                                          negate=True).then_inc(max_done, 1)

                    def scale(u, k):
                        dve.wait_ge(sum_bc, u.at(k) + 1)
                        dve.reciprocal(rec[:, :], psum[:, 7, 0:S]).then_inc(rec_done, 1)
                        dve.wait_ge(rec_done, u.at(k) + 1)
                        dve.wait_ge(o_copied, u.at(k) + 1)
                        wait(dve, proj_made, u.at(k))
                        dve.tensor_tensor(yn[:, :], yraw[:, :], rec[:, :], ALU.mult).then_inc(o_scaled, 1)

                    def stage(u, k):
                        wait(dve, pv_done, KT * u.at(k - 1))
                        dve.tensor_copy(vpair[:, u.buf(2, k), :, :], values[:, :, bass.ds(2 * EA * u.at(k), 2 * EA)]).then_inc(v_staged, 1)

                    def add(u, k):
                        dve.wait_ge(proj_made, u.at(k) + 1)
                        dve.tensor_tensor(acc[:, :, :], acc[:, :, :], psum[:, 7, 0:QT * D].rearrange("p (t d) -> p t d", t=QT),
                                          ALU.add).then_inc(proj_read, 1)

                    def prologue():
                        u = Unit(STEP, 0, 0)
                        stage(u, 0)
                        for g in range(NG):
                            group(u, 0, g)
                        merge(u, 0)

                    def body(u, first, last):
                        for g in range(NG):
                            if not last:
                                group(u, 1, g)
                            if g == 1 and not first:
                                scale(u, -1)
                            if g == 3 and not last:
                                stage(u, 1)
                            if g == 5 and not first:
                                add(u, -1)
                        if not last:
                            merge(u, 1)

                    def epilogue(u):
                        scale(u, 0)
                        add(u, 0)
                        dve.wait_ge(proj_read, PAIRS)
                        dve.tensor_tensor(x_sb[:, bass.ds(QT * b, QT), :], x_sb[:, bass.ds(QT * b, QT), :], acc[:, :, :], ALU.add)

                    loop(dve, body, prologue, epilogue)

                @block.gpsimd
                def _(pool):
                    def body(u, first, last):
                        for s in range(KT):
                            m = KT * u.r + s
                            if s == 0:
                                continue
                            n = KTS[s][1]
                            pool.wait_ge(exp_done, KT * u.at() + s + 1)
                            if s == 1:
                                wait(pool, sum_bc, u.at() - 1)
                                pool.tensor_tensor(psumm[:, u.buf(2), :], probs[:, (m - 1) % NP, :], probs[:, m % NP, :],
                                                   ALU.add).then_inc(summed, 2)
                            else:
                                pool.wait_ge(summed, KT * u.at() + s)
                                pool.tensor_tensor(psumm[0:n, u.buf(2), :], psumm[0:n, u.buf(2), :], probs[0:n, m % NP, :],
                                                   ALU.add).then_inc(summed, 1)

                    loop(pool, body, lambda: None, lambda u: None)
            clear()
        st.close()

    def make_operands(jobs, vjobs, par):
        NJ, NV = len(jobs), len(vjobs)
        mixA, mixB, tot, rest, hi, mid, lo = par
        parts = (hi, mid, lo)
        steps = 2 * (NJ + 2)
        late = min(NV, 5)
        at = [v * 2 * NJ // (NV - late) for v in range(NV - late)] + [2 * NJ + 4 * v // late for v in range(late)]
        v_after = [[v for v in range(NV) if at[v] == i] for i in range(steps)]
        with nc.Block() as block:
            @block.tensor
            def _(pe):
                def value(v):
                    xT, weights, tiles, dst, bias = vjobs[v]
                    wait(pe, v_read, v - 1)
                    for t, (k, n) in enumerate(tiles):
                        to = psum[0:n, 6 + v % 2, t * D:(t + 1) * D]
                        mm = pe.matmul(to, xT[:, k:k + n], weights, start=True, stop=bias is None)
                        if bias is not None:
                            mm = pe.matmul(to, ones_row[0:1, 0:n], bias, start=False, stop=True)
                    mm.then_inc(v_made, 1)

                for j in range(NJ + 2):
                    job = jobs[j] if j < NJ else None
                    if job is not None:
                        n, bank = job["n"], 2 * (j % JB)
                        wait(pe, rotated, 2 * (j - JB + 1))
                        pe.matmul(psum[:, bank, 0:n], job["w"], job["rhs"], start=True, stop=True).then_inc(straight_made, 1)
                    for v in v_after[2 * j]:
                        value(v)
                    if job is not None and job["ws"] is not None:
                        pe.matmul(psum[:, bank + 1, 0:n], job["ws"], job["rhs"], start=True, stop=True).then_inc(swapped_made, 1)
                    for v in v_after[2 * j + 1]:
                        value(v)

            @block.vector
            def _(dve):
                def remainder(j):
                    n = jobs[j]["n"]
                    dve.wait_ge(hi_done, j + 1)
                    wait(dve, lo_done, j - JB + 1)
                    dve.tensor_tensor(rest[:, j % JB, 0:n], tot[:, j % JB, 0:n], hi[:, j % JB, 0:n], ALU.subtract).then_inc(rest_done, 1)

                for j, job in enumerate(jobs):
                    n, bank = job["n"], 2 * (j % JB)
                    dve.wait_ge(straight_made, j + 1)
                    wait(dve, total_made, j - JB + 1)
                    if job["ws"] is None:
                        dve.tensor_scalar(mixA[:, j % JB, 0:n], psum[:, bank, 0:n], job["bias"], None, ALU.add).then_inc(rotated, 2)
                    else:
                        of = lambda a: a.rearrange("p (b s) -> p b s", s=job["cos"].shape[2])
                        dve.tensor_tensor(of(mixA[:, j % JB, 0:n]), of(psum[:, bank, 0:n]), job["cos"], ALU.mult).then_inc(rotated, 1)
                        dve.wait_ge(swapped_made, j + 1)
                        dve.tensor_tensor(of(mixB[:, j % JB, 0:n]), of(psum[:, bank + 1, 0:n]), job["sin"], ALU.mult).then_inc(rotated, 1)
                    if j >= 1:
                        remainder(j - 1)
                remainder(NJ - 1)

            @block.gpsimd
            def _(pool):
                def last_part(j):
                    n = jobs[j]["n"]
                    pool.wait_ge(mid_done, j + 1)
                    wait(pool, parts_out[j % JB], 16 * 3 * (j // JB))
                    pool.tensor_tensor(lo[:, j % JB, 0:n], rest[:, j % JB, 0:n], mid[:, j % JB, 0:n], ALU.subtract).then_inc(lo_done, 1)

                for j, job in enumerate(jobs):
                    n = job["n"]
                    pool.wait_ge(rotated, 2 * (j + 1))
                    wait(pool, rest_done, j - JB + 1)
                    if job["ws"] is None:
                        pool.tensor_copy(tot[:, j % JB, 0:n], mixA[:, j % JB, 0:n]).then_inc(total_made, 1)
                    else:
                        pool.tensor_tensor(tot[:, j % JB, 0:n], mixA[:, j % JB, 0:n], mixB[:, j % JB, 0:n], ALU.add).then_inc(total_made, 1)
                    if j >= 2:
                        last_part(j - 2)
                for j in range(max(0, NJ - 2), NJ):
                    last_part(j)

            @block.scalar
            def _(act):
                def middle(j):
                    n = jobs[j]["n"]
                    act.wait_ge(rest_done, j + 1)
                    act.activation(mid[:, j % JB, 0:n], rest[:, j % JB, 0:n], ACT.Copy).then_inc(mid_done, 1)

                def value(v):
                    _, _, tiles, dst, _ = vjobs[v]
                    act.wait_ge(v_made, v + 1)
                    act.activation(dst.rearrange("k u t e -> k t u e"),
                                   psum[0:tiles[0][1], 6 + v % 2, 0:len(tiles) * D].rearrange("k (t u e) -> k t u e", t=len(tiles), u=PAIRS),
                                   ACT.Copy).then_inc(v_read, 1)

                def high(j):
                    n = jobs[j]["n"]
                    act.wait_ge(total_made, j + 1)
                    wait(act, parts_out[j % JB], 16 * 3 * (j // JB))
                    act.activation(hi[:, j % JB, 0:n], tot[:, j % JB, 0:n], ACT.Copy).then_inc(hi_done, 1)

                for j in range(NJ + 2):
                    for v in v_after[2 * j]:
                        value(v)
                    if 1 <= j <= NJ:
                        high(j - 1)
                    for v in v_after[2 * j + 1]:
                        value(v)
                    if j >= 2:
                        middle(j - 2)

            @block.sync
            def _(sp):
                for j, job in enumerate(jobs):
                    n = job["n"]
                    for part, done in enumerate((hi_done, mid_done, lo_done)):
                        slots = [s for s in range(BIAS) if job["parts"][s] == part]
                        step = slots[1] - slots[0] if len(slots) > 1 else 1
                        src = parts[part][:, j % JB, 0:n].unsqueeze(1).to_broadcast([P, len(slots), n])
                        sp.wait_ge(done, j + 1)
                        sp.dma_start(job["dst"](slice(slots[0], slots[-1] + 1, step)), src).then_inc(parts_out[j % JB], 16)
                for r in range(JB):
                    wait(sp, parts_out[r], 16 * 3 * len(range(r, NJ, JB)))
        clear()

    def unit_loop(eng, step, body, prologue, epilogue):
        last = UNITS // step - 1
        prologue()
        for r in range(step):
            body(Unit(step, 0, r), lambda k, n=r: 0 <= n + k)
        with eng.Fori(1, last) as i:
            for r in range(step):
                body(Unit(step, i, r), lambda k: True)
        for r in range(step):
            body(Unit(step, last, r), lambda k, n=step * last + r: n + k < UNITS)
        epilogue(Unit(step, last, step - 1))

    def attention(bufs, NK, k_dram, values, o_tok):
        kst, qst, vst, probs, mp, nm, oT, rec, sel, zeros = bufs
        KTS = key_tiles(NK)
        KT = len(KTS)
        long = KT > 2
        RING, LOAD = (4, 1) if long else (8, 2)
        CLEAR = RING - LOAD - (0 if long else 1)
        kst = kst[:, 0:RING * NK].rearrange("p (r n) -> p r n", r=RING)
        if long:
            CHUNKS = 4
            cut = [NK * c // CHUNKS for c in range(CHUNKS + 1)]
            groups = [(hq, c) for hq in range(4) for c in range(CHUNKS)]
        else:
            groups = [0, 1]
        NG = len(groups)
        MB = 4 if long else 2
        SB = 2
        OB = 7 if long else 5
        max_slots = [[] for _ in range(KT)]
        pv_slots = [[] for _ in range(KT)]
        if long:
            EARLY = 4
            for g in range(NG):
                at = g * KT // NG - EARLY
                max_slots[at % KT].append((1 if at >= 0 else 2, g))
            for t in range(KT):
                at = max(t + 2, 3)
                pv_slots[at % KT].append((-(at // KT), t))
            TURN_AT, MAX_AT, COPY_AFTER = 5, KT - 3, 1
        else:
            max_slots[1] = [(2, 0), (2, 1)]
            pv_slots[1] = [(-1, 0), (-1, 1)]
        k_units = k_dram.rearrange("(h d) s b n -> h (d s) b n" if long else "(h d) s (b n) -> h (d s) b n", h=H, b=B)
        q_units = q_d.rearrange("(h d) s (b n) -> h (d s) b n", h=H, b=B)

        with nc.Block() as block:
            @block.sync
            def _(sp):
                def load(u, k):
                    wait(sp, scored, KT * u.at(k - RING + LOAD))
                    r, b = u.buf(RING, k), u.batch(k)
                    for h in range(2):
                        rows = slice(64 * h + R0, 64 * h + R0 + ROWS)
                        loads = ring_loaded[r // LOAD]
                        sp.dma_start(kst[rows, r:r + LOAD, 0:NK], k_units[2 * u.pair(k) + h, :, b:b + LOAD, :]).then_inc(loads, 16)
                        sp.dma_start(qst[rows, r:r + LOAD, h * S:(h + 1) * S], q_units[2 * u.pair(k) + h, :, b:b + LOAD, :]).then_inc(loads, 16)

                def prologue():
                    for k in range(0, RING - LOAD, LOAD):
                        load(Unit(RING, 0, 0), k)

                def body(u, there):
                    if u.r % LOAD == 0 and there(RING - LOAD):
                        load(u, RING - LOAD)

                unit_loop(sp, RING, body, prologue, lambda u: None)

            @block.tensor
            def _(pe):
                def group(u, k, g):
                    r = u.buf(RING, k)
                    if g == 0:
                        pe.wait_ge(ring_loaded[r // LOAD], 16 * 4 * u.turn(k))
                        pe.wait_ge(row_cleared, 2 * u.at(k) + 2)
                    wait(pe, max_read, NG * u.at(k) + g - MB + 1)
                    if long:
                        hq, c = groups[g]
                        mm = pe.matmul(psum[:, g % MB, 0:cut[c + 1] - cut[c]], qst[:, r, hq * P:(hq + 1) * P],
                                       kst[:, r, cut[c]:cut[c + 1]], start=True, stop=True)
                    else:
                        for q in range(QT):
                            hq = QT * g + q
                            mm = pe.matmul(psum[:, g, q * S:(q + 1) * S], qst[:, r, hq * P:(hq + 1) * P],
                                           kst[:, r, 0:NK], start=True, stop=True)
                    mm.then_inc(max_scores, 1)

                def turn_max(u, k):
                    pe.wait_ge(max_done, u.at(k) + 1)
                    if long:
                        wait(pe, o_scaled, u.at(k - 1))
                    else:
                        wait(pe, shift_ready, 2 * u.at(k))
                    for q in range(QT):
                        mm = pe.matmul(psum[0:65, 7, q * P:(q + 1) * P], nm[:, u.buf(2, k), q, :], ident_b[:, :],
                                       start=True, stop=True)
                    mm.then_inc(max_row, 1)

                def score(u, s):
                    k, n = KTS[s]
                    m = KT * u.r + s
                    wait(pe, exp_done, KT * u.at() + s - SB + 1)
                    pe.matmul(psum[0:n, MB + m % SB, :], kst[:, u.buf(RING), k:k + n], qst[:, u.buf(RING), :],
                              start=True, stop=True).then_inc(scored, 1)

                def product(u, k, t):
                    n = KTS[t][1]
                    if t == 0:
                        pe.wait_ge(v_staged, u.at(k) + 1)
                        wait(pe, o_copied, u.at(k))
                    pe.wait_ge(exp_done, KT * u.at(k) + t + 1)
                    for h in range(2):
                        c = 2 * (t % 2) + h
                        mm = pe.matmul(psum[VW * c:VW * (c + 1), 6, 0:S], vst[0:n, u.buf(2, k), t, h, :],
                                       probs[0:n, (KT * (u.r + k) + t) % 4, h * S:(h + 1) * S], start=(t < 2), stop=(t >= KT - 2))
                    mm.then_inc(pv_done, 1)

                def turn_o(u, k):
                    pe.wait_ge(o_copied, u.at(k) + 1)
                    wait(pe, o_scaled, u.at(k))
                    ahead = u.at(k + 1)
                    if long and (not isinstance(ahead, int) or ahead < UNITS):
                        pe.wait_ge(shift_ready, 2 * ahead + 2)
                    for q in range(QT):
                        mm = pe.matmul(psum[:, OB, S + 18 * q:S + 18 * (q + 1)], oT[:, u.buf(2, k), q * P:(q + 1) * P], sel[:, :],
                                       start=True, stop=True)
                    mm.then_inc(o_turned, 1)

                def prologue():
                    u = Unit(RING, 0, 0)
                    for g in range(NG):
                        group(u, 0, g)
                    turn_max(u, 0)
                    if long:
                        for s in range(KT):
                            for k, g in max_slots[s]:
                                if k == 2:
                                    group(u, 1, g)
                    else:
                        for g in range(NG):
                            group(u, 1, g)

                def body(u, there):
                    pe.wait_ge(shift_ready, 2 * u.at() + 2)
                    for s in range(KT):
                        score(u, s)
                        if not long and s == 1 and there(1):
                            turn_max(u, 1)
                        for k, g in max_slots[s][0:1] if long else max_slots[s]:
                            if there(k):
                                group(u, k, g)
                        for k, t in pv_slots[s]:
                            if there(k):
                                product(u, k, t)
                        for k, g in max_slots[s][1:] if long else ():
                            if there(k):
                                group(u, k, g)
                        if long and s == TURN_AT and there(-1):
                            turn_o(u, -1)
                        if long and s == MAX_AT and there(1):
                            turn_max(u, 1)
                    if not long and there(-2):
                        turn_o(u, -2)

                def epilogue(u):
                    for s in range(KT):
                        for k, t in pv_slots[s]:
                            if k == -1:
                                product(u, 0, t)
                    if not long:
                        turn_o(u, -1)
                    turn_o(u, 0)

                unit_loop(pe, RING, body, prologue, epilogue)

            @block.scalar
            def _(act):
                def rows(u, k):
                    act.wait_ge(max_row, u.at(k) + 1)
                    r = u.buf(RING, k)
                    act.activation(qst[0:1, r, 0:S], psum[0:1, 7, 0:S], ACT.Copy).then_inc(shift_ready, 1)
                    act.activation(qst[64:65, r, S:2 * S], psum[64:65, 7, 0:S], ACT.Copy).then_inc(shift_ready, 1)

                def copy_o(u, k):
                    act.wait_ge(pv_done, KT * (u.at(k) + 1))
                    wait(act, o_turned, u.at(k) - 1)
                    act.activation(oT[:, u.buf(2, k), :], psum[:, 6, 0:S], ACT.Copy).then_inc(o_copied, 1)

                def body(u, there):
                    for s in range(KT):
                        m = KT * u.r + s
                        if long and s == MAX_AT + 1 and there(1):
                            rows(u, 1)
                        n = KTS[s][1]
                        act.wait_ge(scored, KT * u.at() + s + 1)
                        wait(act, pv_done, KT * u.at() + s - 3)
                        act.activation(probs[0:n, m % 4, :], psum[0:n, MB + m % SB, :], ACT.Exp, scale=HD ** -0.5).then_inc(exp_done, 1)
                        if long and s == COPY_AFTER and there(-1):
                            copy_o(u, -1)
                        if not long and s == 0 and there(1):
                            rows(u, 1)
                    if not long and there(-1):
                        copy_o(u, -1)

                unit_loop(act, RING, body, lambda: rows(Unit(RING, 0, 0), 0), lambda u: copy_o(u, 0))

            @block.vector
            def _(dve):
                def group(u, k, g):
                    dve.wait_ge(max_scores, NG * u.at(k) + g + 1)
                    if long:
                        hq, c = groups[g]
                        dve.tensor_reduce(mp[:, u.buf(2, k), hq, c:c + 1], psum[:, g % MB, 0:cut[c + 1] - cut[c]],
                                          op=ALU.max, axis=AX.X).then_inc(max_read, 1)
                        if g == NG - 1:
                            dve.wait_ge(max_read, NG * (u.at(k) + 1))
                            wait(dve, max_row, u.at(k) - 1)
                            dve.tensor_reduce(nm[:, u.buf(2, k), :, 0:65:64].rearrange("p q h -> p h q"),
                                              mp[:, u.buf(2, k), :, :].rearrange("p (h q) c -> p h q c", h=2), op=ALU.max, axis=AX.X,
                                              negate=True).then_inc(max_done, 1)
                    else:
                        wait(dve, max_row, u.at(k) - 1)
                        ins = dve.tensor_reduce(nm[:, u.buf(2, k), :, 64 * g:64 * g + 1].rearrange("p q h -> p (q h)"),
                                                psum[:, g, :].rearrange("p (q n) -> p q n", q=QT),
                                                op=ALU.max, axis=AX.X, negate=True)
                        ins.then_inc(max_read, 1)
                        if g == NG - 1:
                            dve.wait_ge(max_read, NG * (u.at(k) + 1))
                            dve.sem_inc(max_done, 1)

                def normalise(u, k):
                    dve.wait_ge(o_turned, u.at(k) + 1)
                    o = psum[:, OB, S:S + 36].rearrange("p (q h e) -> p q h e", q=QT, h=2)
                    dve.reciprocal(rec[:, u.buf(2, k), :, :], o[:, :, :, HD]).then_inc(rec_done, 1)
                    dve.wait_ge(rec_done, u.at(k) + 1)
                    dve.tensor_tensor(o_tok[:, u.batch(k), :, bass.ds(2 * HD * u.pair(k), 2 * HD)].rearrange("p q (h d) -> p q h d", h=2),
                                      o[:, :, :, 0:HD], rec[:, u.buf(2, k), :, :].unsqueeze(3).to_broadcast([P, QT, 2, HD]), ALU.mult).then_inc(o_scaled, 1)

                def prologue():
                    u = Unit(RING, 0, 0)
                    for g in range(NG):
                        group(u, 0, g)
                    if long:
                        for s in range(KT):
                            for k, g in max_slots[s]:
                                if k == 2:
                                    group(u, 1, g)
                    else:
                        for g in range(NG):
                            group(u, 1, g)

                def body(u, there):
                    for s in range(KT):
                        for k, g in max_slots[s]:
                            if there(k):
                                group(u, k, g)
                        if long and s == TURN_AT + 2 and there(-1):
                            normalise(u, -1)
                    if not long:
                        if there(-2):
                            normalise(u, -2)

                def epilogue(u):
                    if not long:
                        normalise(u, -1)
                    normalise(u, 0)

                unit_loop(dve, RING, body, prologue, epilogue)

            @block.gpsimd
            def _(pool):
                def stage(u, k):
                    wait(pool, pv_done, KT * u.at(k - 1))
                    cleared = u.at(k - 1 + CLEAR)
                    pool.wait_ge(row_cleared, 2 * (min(cleared, UNITS - 1) if isinstance(cleared, int) else cleared) + 2)
                    v = values[:, u.at(k), :, :].rearrange("p t (h d) -> p t h d", h=2)
                    one = ones_col[:, :].to_broadcast([P, KT * 2 * HD]).rearrange("p (t h d) -> p t h d", t=KT, h=2)
                    pool.tensor_tensor(vst[:, u.buf(2, k), 0:KT, :, 0:HD], v, one, ALU.mult).then_inc(v_staged, 1)

                def clear_row(u, k):
                    wait(pool, scored, KT * u.at(k - RING + 1))
                    r = u.buf(RING, k)
                    for h in range(2):
                        wait(pool, row_cleared, 2 * u.at(k) + h)
                        if h == 0:
                            wait(pool, v_staged, u.at(k - CLEAR) + 1 if not isinstance(u.at(k - CLEAR), int) or u.at(k - CLEAR) >= 0 else 0)
                        row, zero = qst[64 * h:64 * h + 1, r, h * S:(h + 1) * S], zeros[64 * h:64 * h + 1, :]
                        pool.tensor_tensor(row, zero, zero, ALU.add).then_inc(row_cleared, 1)

                def prologue():
                    u = Unit(RING, 0, 0)
                    for k in range(CLEAR):
                        clear_row(u, k)
                    stage(u, 0)

                def body(u, there):
                    if there(CLEAR):
                        clear_row(u, CLEAR)
                    if there(1):
                        stage(u, 1)

                unit_loop(pool, RING, body, prologue, lambda u: None)
        clear()

    def feed_forward(w1, b1, w2, b2, hT, z, load):
        with nc.Block() as block:
            @block.sync
            def _(sp):
                sp.dma_start(load[0], load[1]).then_inc(loaded, 16)
                sp.wait_ge(loaded, 16)

            @block.tensor
            def _(pe):
                for k in range(2):
                    for c in range(FC):
                        n = FC * k + c
                        wait(pe, act_done, n - 1)
                        pe.matmul(psum[:, n % 2, :], w1[:, c * P:(c + 1) * P], xnT[:, k * 512:(k + 1) * 512],
                                  start=True, stop=True).then_inc(up_made, 1)
                for t in range(TILES):
                    k = t // 4
                    pe.wait_ge(act_done, FC * (k + 1))
                    o = psum[:, 2 + k, (t % 4) * D:(t % 4 + 1) * D]
                    for c in range(FC):
                        pe.matmul(o, hT[:, c, t * P:(t + 1) * P], w2[:, c * D:(c + 1) * D], start=(c == 0), stop=False)
                    pe.matmul(o, ones_row[0:1, :], b2, start=False, stop=True).then_inc(down_made, 1)

            @block.scalar
            def _(act):
                for k in range(2):
                    for c in range(FC):
                        act.wait_ge(up_made, FC * k + c + 1)
                        act.activation(hT[:, c, k * 512:(k + 1) * 512], psum[:, (FC * k + c) % 2, :], ACT.Gelu,
                                       bias=b1[:, c:c + 1]).then_inc(act_done, 1)

            @block.vector
            def _(dve):
                for k in range(2):
                    dve.wait_ge(down_made, 4 * (k + 1))
                    dve.tensor_tensor(z[:, 4 * k:4 * k + 4, :], z[:, 4 * k:4 * k + 4, :],
                                      psum[:, 2 + k, :].rearrange("p (t d) -> p t d", t=4), ALU.add)
        clear()

    def experts(gate_w, gate_b, w1_d, b1_d, w2_d, b2_d, func, top, z, tag, loads=()):
        with ExitStack() as st:
            hT = sb(st, tag + "_moe_h", [P, 2, FC, NTOK])
            w1 = sb(st, tag + "_moe_w1", [P, 2, DFF])
            w2 = sb(st, tag + "_moe_w2", [P, 2, DFF])
            b1 = sb(st, tag + "_moe_b1", [P, 2, FC])
            b2 = sb(st, tag + "_moe_b2", [1, 2, D])
            gw = sb(st, tag + "_gate_w", [P, E])
            gb = sb(st, tag + "_gate_b", [1, E])
            iota = sb(st, tag + "_iota", [P, E])
            logit = sb(st, tag + "_logit", [P, TILES, E])
            best = sb(st, tag + "_best", [P, TILES, 8])
            besti = sb(st, tag + "_besti", [P, TILES, 8], U32)
            bestf = sb(st, tag + "_bestf", [P, TILES, 8])
            g1 = sb(st, tag + "_g1", [P, TILES, 2])
            we = sb(st, tag + "_we", [P, TILES, E])
            tmp = sb(st, tag + "_moe_tmp", [P, TILES, E])
            wcol = sb(st, tag + "_wcol", [P, 2, TILES])
            with nc.Block() as block:
                @block.sync
                def _(sp):
                    sp.dma_start(gw[:, :], gate_w).then_inc(loaded, 16)
                    sp.dma_start(iota[:, :], T["iota"]).then_inc(loaded, 16)
                    if gate_b is not None:
                        sp.dma_start(gb[:, :], gate_b).then_inc(loaded, 16)

                @block.tensor
                def _(pe):
                    pe.wait_ge(loaded, 48 if gate_b is not None else 32)
                    for t in range(TILES):
                        mm = pe.matmul(psum[:, 0, t * E:(t + 1) * E], xnT[:, t * P:(t + 1) * P], gw[:, :], start=True, stop=gate_b is None)
                        if gate_b is not None:
                            mm = pe.matmul(psum[:, 0, t * E:(t + 1) * E], ones_row[0:1, :], gb[:, :], start=False, stop=True)
                    mm.then_inc(gate_made, 1)

                @block.scalar
                def _(act):
                    if top == 2:
                        act.wait_ge(gate_step, 4)
                        act.activation(g1[:, :, 1:2], g1[:, :, 0:1], ACT.Exp).then_inc(gate_exp, 1)

                @block.vector
                def _(dve):
                    n = [0]

                    def link(ins):
                        n[0] += 1
                        ins.then_inc(gate_step, 1)
                        dve.wait_ge(gate_step, n[0])

                    dve.wait_ge(gate_made, 1)
                    dve.wait_ge(loaded, 48 if gate_b is not None else 32)
                    link(dve.tensor_copy(logit[:, :, :], psum[:, 0, 0:TILES * E].rearrange("p (t e) -> p t e", e=E)))
                    for t in range(TILES):
                        ins = dve.max(best[:, t, :], logit[:, t, :])
                        ins.then_inc(best_found, 1)
                    dve.wait_ge(best_found, TILES)
                    for t in range(TILES):
                        ins = dve.max_index(besti[:, t, :], best[:, t, :], logit[:, t, :])
                        ins.then_inc(index_found, 1)
                    dve.wait_ge(index_found, TILES)
                    link(dve.tensor_copy(bestf[:, :, :], besti[:, :, :]))
                    ids = iota[:, :].unsqueeze(1).to_broadcast([P, TILES, E])
                    link(dve.tensor_tensor(we[:, :, :], ids, bestf[:, :, 0:1].to_broadcast([P, TILES, E]), ALU.is_equal))
                    if top == 2:
                        link(dve.tensor_tensor(g1[:, :, 0:1], best[:, :, 1:2], best[:, :, 0:1], ALU.subtract))
                        link(dve.tensor_tensor(tmp[:, :, :], ids, bestf[:, :, 1:2].to_broadcast([P, TILES, E]), ALU.is_equal))
                        dve.wait_ge(gate_exp, 1)
                        link(dve.tensor_tensor(tmp[:, :, :], tmp[:, :, :], g1[:, :, 1:2].to_broadcast([P, TILES, E]), ALU.mult))
                        link(dve.tensor_tensor(we[:, :, :], we[:, :, :], tmp[:, :, :], ALU.add))
                        link(dve.tensor_scalar(g1[:, :, 0:1], g1[:, :, 1:2], 1.0, None, ALU.add))
                        link(dve.reciprocal(g1[:, :, 1:2], g1[:, :, 0:1]))
                        link(dve.tensor_tensor(we[:, :, :], we[:, :, :], g1[:, :, 1:2].to_broadcast([P, TILES, E]), ALU.mult))
            clear()

            NU = 2 * FC

            def each(eng, step, between=lambda: None):
                for r in range(2):
                    step(r, r, 0)
                between()
                with eng.Fori(1, E // 2) as i:
                    for r in range(2):
                        step(2 * i + r, r, i)

            with nc.Block() as block:
                @block.sync
                def _(sp):
                    def load(e, r, i):
                        wait(sp, act_done, NU * (e - 1))
                        sp.dma_start(w1[:, r, :], w1_d[e]).then_inc(up_weights[r], 16)
                        sp.dma_start(b1[:, r, :], b1_d[e]).then_inc(up_weights[r], 16)
                        wait(sp, down_made, 2 * (e - 1))
                        sp.dma_start(w2[:, r, :], w2_d[e]).then_inc(down_weights[r], 16)
                        sp.dma_start(b2[:, r, :], b2_d[e]).then_inc(down_weights[r], 16)

                    each(sp, load, between=lambda: [sp.dma_start(to, frm).then_inc(loaded, 16) for to, frm in loads])
                    wait(sp, loaded, 16 * len(loads))

                @block.tensor
                def _(pe):
                    def up(e, r, i):
                        pe.wait_ge(up_weights[r], 32 * i + 32)
                        for k in range(2):
                            for c in range(FC):
                                n = FC * k + c
                                wait(pe, act_done, NU * e + n - 1)
                                pe.matmul(psum[:, n % 2, :], w1[:, r, c * P:(c + 1) * P], xnT[:, k * 512:(k + 1) * 512],
                                          start=True, stop=True).then_inc(up_made, 1)

                    def down(e, r, i):
                        pe.wait_ge(down_weights[r], 32 * i + 32)
                        for t in range(TILES):
                            k = t // 4
                            if t % 4 == 0:
                                pe.wait_ge(act_done, NU * e + FC * (k + 1))
                                wait(pe, down_read, 2 * (e - 2) + k + 1)
                            o = psum[:, 2 + 2 * r + k, (t % 4) * D:(t % 4 + 1) * D]
                            for c in range(FC):
                                pe.matmul(o, hT[:, r, c, t * P:(t + 1) * P], w2[:, r, c * D:(c + 1) * D], start=(c == 0), stop=False)
                            mm = pe.matmul(o, ones_row[0:1, :], b2[0:1, r, :], start=False, stop=True)
                            if t % 4 == 3:
                                mm.then_inc(down_made, 1)

                    up(0, 0, 0)
                    up(1, 1, 0)
                    down(0, 0, 0)
                    up(2, 0, 1)
                    down(1, 1, 0)
                    with pe.Fori(1, E // 2 - 1) as i:
                        up(2 * i + 1, 1, i)
                        down(2 * i, 0, i)
                        up(2 * i + 2, 0, i + 1)
                        down(2 * i + 1, 1, i)
                    last = E // 2 - 1
                    up(E - 1, 1, last)
                    down(E - 2, 0, last)
                    down(E - 1, 1, last)

                @block.scalar
                def _(act):
                    def hidden(e, r, i):
                        wait(act, down_made, 2 * (e - 1))
                        for k in range(2):
                            for c in range(FC):
                                n = FC * k + c
                                act.wait_ge(up_made, NU * e + n + 1)
                                act.activation(hT[:, r, c, k * 512:(k + 1) * 512], psum[:, n % 2, :], func,
                                               bias=b1[:, r, c:c + 1]).then_inc(act_done, 1)

                    each(act, hidden)

                @block.vector
                def _(dve):
                    def add(e, r, i):
                        dve.tensor_copy(wcol[:, r, :], we[:, :, e]).then_inc(weights_picked, 1)
                        dve.wait_ge(weights_picked, e + 1)
                        for t in range(TILES):
                            k = t // 4
                            if t % 4 == 0:
                                dve.wait_ge(down_made, 2 * e + k + 1)
                            ins = dve.scalar_tensor_tensor(z[:, t, :], psum[:, 2 + 2 * r + k, (t % 4) * D:(t % 4 + 1) * D],
                                                           wcol[:, r, t:t + 1], z[:, t, :], ALU.mult, ALU.add)
                            if t % 4 == 3:
                                ins.then_inc(down_read, 1)

                    each(dve, add)
            clear()

    def add_into(a, b):
        with nc.Block() as block:
            @block.vector
            def _(dve):
                dve.tensor_tensor(a[:, :, :], a[:, :, :], b[:, :, :], ALU.add)
        clear()

    resampler()
    KTC = len(key_tiles(SC))
    st = ExitStack()
    KTS_SELF = S // P
    v_self = sb(st, "v_self", [P, UNITS, KTS_SELF, 2 * HD])
    kst = sb(st, "kst", [P, 4 * SC], BF16)
    qst = sb(st, "qst", [P, 8, 2 * S], BF16)
    vst = sb(st, "vst", [P, 2, KTC, 2, VW])
    probs = sb(st, "probs8", [P, 4, 2 * S])
    mp = sb(st, "mp8", [P, 2, 4, 4])
    nm = sb(st, "nm8", [P, 2, QT, 65], BF16)
    oT = sb(st, "oT", [P, 2, S])
    rec = sb(st, "rec8", [P, 2, QT, 2])
    sel = sb(st, "sel", [P, 18])
    o_tok = sb(st, "o_tok", [P, B, QT, D])
    oTT = sb(st, "oTT", [P, NTOK])
    zeros = sb(st, "zeros", [P, S], BF16)
    bufs = (kst, qst, vst, probs, mp, nm, oT, rec, sel, zeros)
    par = (sb(st, "mixA", [P, JB, 512]), sb(st, "mixB", [P, JB, 512]), sb(st, "tot", [P, JB, 512]), sb(st, "rest", [P, JB, 512]),
           sb(st, "hi", [P, JB, 512], BF16), sb(st, "mid", [P, JB, 512], BF16), sb(st, "lo", [P, JB, 512], BF16))

    with nc.Block() as block:
        @block.vector
        def _(dve):
            dve.memset(qst[:, :, :].bitcast(F32), 0.0)
            keys = kst[:, :].bitcast(F32)
            dve.memset(keys, ONES_BF16)

        @block.gpsimd
        def _(pool):
            pool.memset(nm[:, :, :, :], 0.0)
            pool.memset(zeros[:, :], 0.0)
            pool.memset(vst[:, :, :, :, :], 0.0).then_inc(v_staged, 1)
            pool.wait_ge(v_staged, 1)
            pool.memset(vst[:, :, :, :, HD:HD + 1], 1.0)

        @block.sync
        def _(sp):
            sp.dma_start(sel[:, :], T["sel"]).then_inc(loaded, 16)
            sp.wait_ge(loaded, 16)
    clear()

    with ExitStack() as s2:
        wqkv = sb(s2, "wqkv", [P, 3 * D])
        wo2 = sb(s2, "wo2", [P, D])
        bq = sb(s2, "bq", [P, 2])
        bvr = sb(s2, "bvr", [1, D])
        bor = sb(s2, "bor", [1, D])
        with nc.Block() as block:
            @block.sync
            def _(sp):
                sp.dma_start(wqkv[:, :], T["w_qkv"]).then_inc(loaded, 16)
                sp.dma_start(wo2[:, :], T["w_o"]).then_inc(loaded, 16)
                sp.dma_start(bq[:, :], T["b_qk"]).then_inc(loaded, 16)
                sp.dma_start(bvr[:, :], T["b_v"]).then_inc(loaded, 16)
                sp.dma_start(bor[:, :], T["b_o"]).then_inc(loaded, 16)
                sp.wait_ge(loaded, 80)
        clear()
        layer_norm(x_sb, z_sb)
        norm_turned(z_sb, affine=(vecs[:, 2:3], vecs[:, 3:4]))
        jobs, vjobs = [], []
        for c in range(NTOK // 512):
            for w, parts in ((0, PARTS_Q), (1, PARTS_K)):
                cols = slice(c * 512, (c + 1) * 512)
                jobs.append(dict(n=512, w=wqkv[:, w * D:(w + 1) * D], ws=None, bias=bq[:, w:w + 1], rhs=xnT[:, cols], parts=parts,
                                 dst=lambda slots, w=w, cols=cols: (k_first_d if w else q_d)[:, slots, cols]))
        for b in range(B):
            vjobs.append((xnT, wqkv[:, 2 * D:3 * D], [(b * S + t * P, P) for t in range(KTS_SELF)], v_self[:, b:UNITS:B, :, :], bvr[0:1, :]))
        make_operands(jobs, vjobs, par)
        attention(bufs, S, k_first_d, v_self, o_tok)
        norm_turned(z_sb, affine=(vecs[:, 4:5], vecs[:, 5:6]), project=(o_tok, oTT, wo2[:, :], bor[0:1, :]))
    ctxT = sb(st, "ctxT", [P, B * SC])
    W = sb(st, "W", [P, WCOLS])
    cos = sb(st, "cos", [P, SC])
    sin = sb(st, "sin", [P, SC])
    experts(T["w_gate"], None, T["L0_w1"], T["L0_b1"], T["L0_w2"], T["L0_b2"], ACT.Gelu_apprx_tanh, 2, z_sb, "l0",
            loads=[(W[:, 0:WLATE], T["layers"][0, :, 0:WLATE]), (ctxT[:, :], T["ctxT"]), (cos[:, :], T["cos"]), (sin[:, :], T["sin"])])
    add_into(x_sb, z_sb)

    with ExitStack() as s2:
        v_ctx = sb(s2, "v_ctx", [P, UNITS, KTC, 2 * HD])
        layer_norm(x_sb, z_sb)
        with nc.Block() as block:
            @block.vector
            def _(dve):
                dve.memset(v_ctx[:, :, KTC - 1, :], 0.0)
        clear()

        def w(name):
            at, n = COL[name]
            return W[:, at:at + n]

        def rope_job(wn, rhs, n, pos, parts, dst):
            m = min(n, S) if pos is None else n
            turn = lambda a: a[:, (pos or 0):(pos or 0) + m].unsqueeze(1).to_broadcast([P, n // m, m])
            return dict(n=n, w=w(wn), ws=w(wn + "s"), rhs=rhs, cos=turn(cos), sin=turn(sin), parts=parts, dst=dst)

        with nc.Fori(0, NL) as l:
            norm_turned(z_sb, modulate=(w("n1"), w("n1b")),
                        loads=((W[:, WLATE:], T["layers"][l, :, WLATE:]), (brow[0:1, 0:D], T["f2_b"][l])))
            jobs, vjobs = [], []
            for c in range(NTOK // 512):
                cols = slice(c * 512, (c + 1) * 512)
                jobs.append(rope_job("q", xnT[:, cols], 512, None, PARTS_Q, lambda slots, cols=cols: q_d[:, slots, cols]))
                jobs.append(rope_job("k", xnT[:, cols], 512, None, PARTS_K, lambda slots, cols=cols: k_self_d[:, slots, cols]))
            for b in range(B):
                vjobs.append((xnT, w("v"), [(b * S + t * P, P) for t in range(KTS_SELF)], v_self[:, b:UNITS:B, :, :], None))
            make_operands(jobs, vjobs, par)
            attention(bufs, S, k_self_d, v_self, o_tok)
            norm_turned(z_sb, modulate=(w("n2"), w("n2b")), project=(o_tok, oTT, w("so"), None))
            jobs, vjobs = [], []
            cuts = [0, 401, 801, 1201, SC]
            for c in range(NTOK // 512):
                cols = slice(c * 512, (c + 1) * 512)
                jobs.append(rope_job("cq", xnT[:, cols], 512, None, PARTS_Q, lambda slots, cols=cols: q_d[:, slots, cols]))
            for b in range(B):
                for lo_, hi_ in zip(cuts, cuts[1:]):
                    jobs.append(rope_job("ck", ctxT[:, b * SC + lo_:b * SC + hi_], hi_ - lo_, lo_, PARTS_K,
                                         lambda slots, b=b, keys=slice(lo_, hi_): k_ctx_d[:, slots, b, keys]))
                tiles = key_tiles(SC)
                for lo_, hi_ in ((0, 4), (4, 8), (8, 12), (12, 13)):
                    vjobs.append((ctxT, w("cv"), [(b * SC + k, n) for k, n in tiles[lo_:hi_]],
                                  v_ctx[0:tiles[lo_][1], b:UNITS:B, lo_:hi_, :], None))
            make_operands(jobs, vjobs, par)
            attention(bufs, SC, k_ctx_d, v_ctx, o_tok)
            norm_turned(z_sb, modulate=(w("n3"), w("n3b")), project=(o_tok, oTT, w("co"), None))
            with ExitStack() as s3:
                hid = sb(s3, "hid", [P, FC, NTOK])
                feed_forward(w("f1"), w("f1b"), w("f2"), brow[0:1, 0:D], hid, z_sb,
                             (W[:, 0:WLATE], T["layers"][l + 1, :, 0:WLATE]))
    add_into(x_sb, z_sb)

    norm_turned(x_sb, affine=(1.0, 0.0))
    experts(T["gate_w"], T["gate_b"], T["L1_w1"], T["L1_b1"], T["L1_w2"], T["L1_b2"], ACT.Relu, 1, x_sb, "l1")
    with nc.Block() as block:
        @block.sync
        def _(sp):
            sp.dma_start(out.rearrange("b (t p) d -> p (b t) d", p=P), x_sb[:, :, :]).then_inc(stored, 16)
            sp.wait_ge(stored, 16)
    st.close()
    top.close()


def _layout(I):
    f = np.ascontiguousarray
    A = {k: np.asarray(v) for k, v in I.items()}
    T = {}
    T["x"] = A["x"]
    T["ctx"] = A["ctx_1024"]
    T["ctxT"] = f(A["ctx_1024"].transpose(2, 0, 1).reshape(D, B * SC))
    T["condT"] = f(A["cond_1024"].T)
    T["mask_ctx"] = A["mask_BxS2_bf0"].reshape(B, 1, SC)
    T["mask_x"] = A["mask_BxS_bf0"].reshape(1, NTOK)
    T["ident"] = np.eye(P, dtype=np.float32)
    names = ["L0_xcond_ln2_w", "L0_xcond_ln2_b", "L0_ffn_ln1_w", "L0_ffn_ln1_b", "L0_ffn_ln2_w", "L0_ffn_ln2_b"]
    T["vecs"] = f(np.stack([A[n] for n in names] * 2, axis=1))
    T["ln1_w"], T["ln1_b"] = A["L0_xcond_ln1_w"].reshape(1, D), A["L0_xcond_ln1_b"].reshape(1, D)
    heads = lambda a: f(a.reshape(H, EA, D).transpose(1, 0, 2))
    T["Wq"] = heads(A["L0_xcond_Wq"])
    T["Wk"] = heads(A["L0_xcond_Wkv"][:H * EA])
    T["Wv"] = f(A["L0_xcond_Wkv"][H * EA:].T)
    T["Wo"] = f(A["L0_xcond_Wo"].T.reshape(PAIRS, 2 * EA, D).transpose(1, 0, 2))
    sel = np.zeros((P, 18), np.float32)
    for c in range(4):
        for e in range(HD + 1):
            sel[VW * c + e, (HD + 1) * (c % 2) + e] = 1
    T["sel"] = sel
    T["iota"] = f(np.tile(np.arange(E, dtype=np.float32), (P, 1)))
    half = HD // 2
    inv = (np.float32(1.0) / np.float32(10000.0) ** (np.arange(half, dtype=np.float32) / np.float32(half))).astype(np.float32)
    ang = (np.arange(SC, dtype=np.float32)[:, None] * inv).astype(np.float32)
    c, s = np.cos(ang).T, np.sin(ang).T
    T["cos"] = f(np.tile(np.concatenate([c, c]), (H, 1)).astype(np.float32))
    T["sin"] = f(np.tile(np.concatenate([-s, s]), (H, 1)).astype(np.float32))
    T["w_qkv"], T["w_o"] = A["L0_ffn_w_qkv"], A["L0_ffn_w_o"]
    bqkv = A["L0_ffn_b_qkv"].reshape(3, D)
    T["b_qk"] = f(bqkv[0:2].T)
    T["b_v"] = f(bqkv[2:3])
    T["b_o"] = A["L0_ffn_b_o"].reshape(1, D)
    T["w_gate"] = A["L0_ffn_w_gate"]
    T["L0_w1"] = A["L0_ffn_w1"]
    T["L0_b1"] = f(A["L0_ffn_b1"].reshape(E, FC, P).transpose(0, 2, 1))
    T["L0_w2"] = f(A["L0_ffn_w2"].reshape(E, FC, P, D).transpose(0, 2, 1, 3).reshape(E, P, FC * D))
    T["L0_b2"] = A["L0_ffn_b2"].reshape(E, 1, D)
    T["gate_w"] = f(A["L1_ffn_gate_w"].T)
    T["gate_b"] = A["L1_ffn_gate_b"].reshape(1, E)
    T["L1_w1"] = f(A["L1_ffn_w1"].transpose(0, 2, 1))
    T["L1_b1"] = f(A["L1_ffn_b1"].reshape(E, FC, P).transpose(0, 2, 1))
    T["L1_w2"] = f(A["L1_ffn_w2"].reshape(E, D, FC, P).transpose(0, 3, 2, 1).reshape(E, P, FC * D))
    T["L1_b2"] = A["L1_ffn_b2"].reshape(E, 1, D)
    g = lambda n: A["L1_xcond_" + n]
    swap = np.arange(D).reshape(H, 2, half)[:, ::-1].reshape(D)
    t = lambda a: a.transpose(0, 2, 1)
    qkv = g("qkv_w")
    q, k, v = qkv[:, 0:D], qkv[:, D:2 * D], qkv[:, 2 * D:]
    col = lambda a, n: a.reshape(NL, n, P).transpose(0, 2, 1)
    parts = [t(g("n1_w")), t(g("n2_w")), t(g("n3_w")), t(q), t(q[:, swap]), t(k), t(k[:, swap]), t(v), t(g("so_w")),
             t(g("cq_w")), t(g("cq_w")[:, swap]), t(g("ck_w")), t(g("ck_w")[:, swap]), t(g("cv_w")), t(g("co_w")),
             col(g("n1_b"), 2), col(g("n2_b"), 2), col(g("n3_b"), 2), t(g("f1_w")),
             g("f2_w").reshape(NL, D, FC, P).transpose(0, 3, 2, 1).reshape(NL, P, FC * D),
             col(g("f1_b"), FC)]
    layers = np.concatenate(parts, axis=2)
    T["layers"] = f(np.concatenate([layers, layers[-1:]]))
    T["f2_b"] = g("f2_b").reshape(NL, 1, D)
    return {n: f(a) for n, a in T.items()}


def kernel(**inputs):
    import concourse.bacc as _bacc
    from concourse.bass_utils import run_bass_kernel_spmd as _run

    T = _layout(inputs)
    nc = _bacc.Bacc("TRN2", target_bir_lowering=False, num_devices=1)
    arrays, aps = {}, {}
    for name, a in T.items():
        arrays[f"in_{name}"] = a
        aps[name] = nc.dram_tensor(f"in_{name}", a.shape, mybir.dt.from_np(a.dtype), kind="ExternalInput").ap()
    out = nc.dram_tensor("out", (B, S, D), F32, kind="ExternalOutput").ap()
    build_program(nc, aps, out)
    r = _run(nc, [arrays], core_ids=[0])
    return r.results[0]["out"]
```
